# Optimizing a Trainium2 kernel written in Bass

```python
import numpy as np
import jax
import jax.numpy as jnp

def _softmax(x, axis=-1):
    return jax.nn.softmax(x, axis=axis)

def _gelu(x):
    return jax.nn.gelu(x, approximate=True)

def _silu(x):
    return jax.nn.silu(x)

def _sigmoid(x):
    return jax.nn.sigmoid(x)

def _layernorm(x, axis=-1, eps=1e-05):
    m = jnp.mean(x, axis=axis, keepdims=True)
    v = jnp.var(x, axis=axis, keepdims=True)
    return (x - m) / jnp.sqrt(v + eps)

def _scatter_add(tgt, idx, src, axis=0):
    return tgt.at[idx].add(src)

def _segment_sum(src, seg, n):
    return jax.ops.segment_sum(src, seg, n)
kernel_name = 'mk_gnn_resnorm_d4_gnn_r16_5b4d64'

def setup_inputs(seed: int=0):
    np.random.seed(seed)
    _w = jnp.asarray

    def _rec_inputs():
        import jax
        import jax.numpy as jnp
        _gk = jax.random.key(seed)
        x = -0.0003713 + 1 * jax.random.normal(jax.random.fold_in(_gk, 1), (3125, 256), jnp.float32)
        src = jax.random.randint(jax.random.fold_in(_gk, 2), (100000,), 0, 3125, jnp.int32)
        dst = jnp.minimum((3125 * jax.random.uniform(jax.random.fold_in(_gk, 3), (100000,)) ** 2.0).astype(jnp.int32), 49999)
        _o = jnp.argsort(dst, stable=True)
        src = src[_o]
        dst = dst[_o]
        edge_attr_4 = 0.000126197 + 0.999763 * jax.random.normal(jax.random.fold_in(_gk, 12), (100000, 4), jnp.float32)
        edge_attr_8 = jax.random.uniform(jax.random.fold_in(_gk, 13), (100000, 8), jnp.float32, 0.0, 1)
        edge_weight = jax.random.uniform(jax.random.fold_in(_gk, 15), (100000,), jnp.float32, 0.0, 999998)
        node_vec = jax.random.uniform(jax.random.fold_in(_gk, 16), (3125,), jnp.float32, 0.0, 999884)
        return (x, src, dst, edge_attr_4, edge_attr_8, edge_weight, node_vec)
    x, src, dst, edge_attr_4, edge_attr_8, edge_weight, node_vec = _rec_inputs()

    def _L0_gnn_setup():
        import jax, jax.numpy as jnp
        import numpy as np
        NUM_NODES = 3125
        NUM_EDGES = 50000
        INPUT_DIM = 256
        OUTPUT_DIM = 256
        NUM_HEADS = 8
        HEAD_DIM = OUTPUT_DIM // NUM_HEADS
        key = jax.random.key(seed)
        ks = jax.random.split(key, 14)
        x = jax.random.normal(ks[0], (NUM_NODES, INPUT_DIM), dtype=jnp.float32)
        edge_index = jax.random.randint(ks[1], (2, NUM_EDGES), 0, NUM_NODES, dtype=jnp.int32)
        edge_time = jax.random.uniform(ks[2], (NUM_EDGES,), dtype=jnp.float32) * 1000000.0
        node_time = jax.random.uniform(ks[3], (NUM_NODES,), dtype=jnp.float32) * 1000000.0
        s_in = 1.0 / np.sqrt(INPUT_DIM)
        s_out = 1.0 / np.sqrt(OUTPUT_DIM)
        s_t = 1.0 / np.sqrt(2.0)
        Wq = jax.random.uniform(ks[4], (INPUT_DIM, OUTPUT_DIM), jnp.float32, -s_in, s_in)
        bq = jax.random.uniform(ks[5], (OUTPUT_DIM,), jnp.float32, -s_in, s_in)
        Wk = jax.random.uniform(ks[6], (INPUT_DIM, OUTPUT_DIM), jnp.float32, -s_in, s_in)
        bk = jax.random.uniform(ks[7], (OUTPUT_DIM,), jnp.float32, -s_in, s_in)
        Wv = jax.random.uniform(ks[8], (INPUT_DIM, OUTPUT_DIM), jnp.float32, -s_in, s_in)
        bv = jax.random.uniform(ks[9], (OUTPUT_DIM,), jnp.float32, -s_in, s_in)
        Wt = jax.random.uniform(ks[10], (2, NUM_HEADS), jnp.float32, -s_t, s_t)
        bt = jax.random.uniform(ks[11], (NUM_HEADS,), jnp.float32, -s_t, s_t)
        Wo = jax.random.uniform(ks[12], (OUTPUT_DIM, OUTPUT_DIM), jnp.float32, -s_out, s_out)
        bo = jax.random.uniform(ks[13], (OUTPUT_DIM,), jnp.float32, -s_out, s_out)
        return {'x': x, 'edge_index': edge_index, 'edge_time': edge_time, 'node_time': node_time, 'Wq': Wq, 'bq': bq, 'Wk': Wk, 'bk': bk, 'Wv': Wv, 'bv': bv, 'Wt': Wt, 'bt': bt, 'Wo': Wo, 'bo': bo}
    _L0_gnn_all = _L0_gnn_setup()
    _L0_gnn_in = {k: v for k, v in _L0_gnn_all.items() if k in ('Wq', 'bq', 'Wk', 'bk', 'Wv', 'bv', 'Wt', 'bt', 'Wo', 'bo')}
    del _L0_gnn_all

    def _L1_gnn_setup():
        import jax, jax.numpy as jnp
        import numpy as np
        N_NODES = 1250
        N_EDGES = 20000
        MUL = 64
        NUM_BASIS = 8
        INV_SQRT3 = 0.5773502691896258
        EPS = 1e-05
        key = jax.random.key(seed)
        k = jax.random.split(key, 16)
        return {'node_hiddens': jax.random.normal(k[0], (N_NODES, 4 * MUL), dtype=jnp.float32), 'edge_attr': jax.random.uniform(k[1], (N_EDGES, NUM_BASIS), dtype=jnp.float32), 'edge_sh': jax.random.normal(k[2], (N_EDGES, 4), dtype=jnp.float32), 'w1_s': jax.random.normal(k[3], (MUL, MUL), dtype=jnp.float32), 'w1_v': jax.random.normal(k[4], (MUL, MUL), dtype=jnp.float32), 'wsc_s': jax.random.normal(k[5], (MUL, MUL), dtype=jnp.float32), 'wsc_v': jax.random.normal(k[6], (MUL, MUL), dtype=jnp.float32), 'w2_s': jax.random.normal(k[7], (2 * MUL, MUL), dtype=jnp.float32), 'w2_v': jax.random.normal(k[8], (2 * MUL, MUL), dtype=jnp.float32), 'fc_w1': jax.random.normal(k[9], (NUM_BASIS, 64), dtype=jnp.float32), 'fc_w2': jax.random.normal(k[10], (64, 64), dtype=jnp.float32), 'fc_w3': jax.random.normal(k[11], (64, 4 * MUL), dtype=jnp.float32), 'g_s': jnp.ones((MUL,), dtype=jnp.float32), 'g_v': jnp.ones((MUL,), dtype=jnp.float32), 'edge_index': jax.random.randint(k[12], (2, N_EDGES), 0, N_NODES)}
    _L1_gnn_all = _L1_gnn_setup()
    _L1_gnn_in = {k: v for k, v in _L1_gnn_all.items() if k in ('w1_s', 'w1_v', 'wsc_s', 'wsc_v', 'w2_s', 'w2_v', 'fc_w1', 'fc_w2', 'fc_w3', 'g_s', 'g_v')}
    del _L1_gnn_all

    def _L2_gnn_setup():
        import jax, jax.numpy as jnp
        import numpy as np
        N = 3125
        E = 50000
        HIDDEN = 256
        HEADS = 8
        HEAD_DIM = HIDDEN // HEADS

        def _linear_params(key, fan_in, fan_out):
            k1, k2 = jax.random.split(key)
            s = 1.0 / np.sqrt(fan_in)
            W = jax.random.uniform(k1, (fan_in, fan_out), jnp.float32, -s, s)
            b = jax.random.uniform(k2, (fan_out,), jnp.float32, -s, s)
            return (W, b)
        key = jax.random.key(seed)
        ks = jax.random.split(key, 7)
        h = jax.random.normal(ks[0], (N, HIDDEN), jnp.float32)
        row = jnp.sort(jax.random.randint(ks[1], (E,), 0, N))
        col = jax.random.randint(ks[2], (E,), 0, N)
        Wq, bq = _linear_params(ks[3], HIDDEN, HIDDEN)
        Wk, bk = _linear_params(ks[4], HIDDEN, HIDDEN)
        Wv, bv = _linear_params(ks[5], HIDDEN, HIDDEN)
        Wo, bo = _linear_params(ks[6], HIDDEN, HIDDEN)
        return dict(h=h, row=row, col=col, Wq=Wq, bq=bq, Wk=Wk, bk=bk, Wv=Wv, bv=bv, Wo=Wo, bo=bo)
    _L2_gnn_all = _L2_gnn_setup()
    _L2_gnn_in = {k: v for k, v in _L2_gnn_all.items() if k in ('Wq', 'bq', 'Wk', 'bk', 'Wv', 'bv', 'Wo', 'bo')}
    del _L2_gnn_all

    def _L3_gnn_setup():
        import jax, jax.numpy as jnp
        import numpy as np
        N_NODES = 6250
        N_EDGES = 200000
        DIM = 256
        LEAKY_SLOPE = 0.2
        EPS = 1e-12
        key = jax.random.key(seed)
        ks = jax.random.split(key, 8)
        embeddings = jax.random.normal(ks[0], (N_NODES, DIM), dtype=jnp.float32)
        edge_src = jax.random.randint(ks[1], (N_EDGES,), 0, N_NODES, dtype=jnp.int32)
        edge_dst = jax.random.randint(ks[2], (N_EDGES,), 0, N_NODES, dtype=jnp.int32)
        edge_val = jax.random.uniform(ks[3], (N_EDGES,), dtype=jnp.float32) / 32.0
        scale = 1.0 / np.sqrt(DIM)
        W1 = jax.random.normal(ks[4], (DIM, DIM), dtype=jnp.float32) * scale
        b1 = jax.random.normal(ks[5], (DIM,), dtype=jnp.float32) * 0.01
        W2 = jax.random.normal(ks[6], (DIM, DIM), dtype=jnp.float32) * scale
        b2 = jax.random.normal(ks[7], (DIM,), dtype=jnp.float32) * 0.01
        return {'embeddings': embeddings, 'edge_src': edge_src, 'edge_dst': edge_dst, 'edge_val': edge_val, 'W1': W1, 'b1': b1, 'W2': W2, 'b2': b2}
    _L3_gnn_all = _L3_gnn_setup()
    _L3_gnn_in = {k: v for k, v in _L3_gnn_all.items() if k in ('W1', 'b1', 'W2', 'b2')}
    del _L3_gnn_all
    return {'x': x, 'src': src, 'dst': dst, 'edge_attr_4': edge_attr_4, 'edge_attr_8': edge_attr_8, 'edge_weight': edge_weight, 'node_vec': node_vec, 'L0_gnn_Wq': _L0_gnn_in['Wq'], 'L0_gnn_bq': _L0_gnn_in['bq'], 'L0_gnn_Wk': _L0_gnn_in['Wk'], 'L0_gnn_bk': _L0_gnn_in['bk'], 'L0_gnn_Wv': _L0_gnn_in['Wv'], 'L0_gnn_bv': _L0_gnn_in['bv'], 'L0_gnn_Wt': _L0_gnn_in['Wt'], 'L0_gnn_bt': _L0_gnn_in['bt'], 'L0_gnn_Wo': _L0_gnn_in['Wo'], 'L0_gnn_bo': _L0_gnn_in['bo'], 'L1_gnn_w1_s': _L1_gnn_in['w1_s'], 'L1_gnn_w1_v': _L1_gnn_in['w1_v'], 'L1_gnn_wsc_s': _L1_gnn_in['wsc_s'], 'L1_gnn_wsc_v': _L1_gnn_in['wsc_v'], 'L1_gnn_w2_s': _L1_gnn_in['w2_s'], 'L1_gnn_w2_v': _L1_gnn_in['w2_v'], 'L1_gnn_fc_w1': _L1_gnn_in['fc_w1'], 'L1_gnn_fc_w2': _L1_gnn_in['fc_w2'], 'L1_gnn_fc_w3': _L1_gnn_in['fc_w3'], 'L1_gnn_g_s': _L1_gnn_in['g_s'], 'L1_gnn_g_v': _L1_gnn_in['g_v'], 'L2_gnn_Wq': _L2_gnn_in['Wq'], 'L2_gnn_bq': _L2_gnn_in['bq'], 'L2_gnn_Wk': _L2_gnn_in['Wk'], 'L2_gnn_bk': _L2_gnn_in['bk'], 'L2_gnn_Wv': _L2_gnn_in['Wv'], 'L2_gnn_bv': _L2_gnn_in['bv'], 'L2_gnn_Wo': _L2_gnn_in['Wo'], 'L2_gnn_bo': _L2_gnn_in['bo'], 'L3_gnn_W1': _L3_gnn_in['W1'], 'L3_gnn_b1': _L3_gnn_in['b1'], 'L3_gnn_W2': _L3_gnn_in['W2'], 'L3_gnn_b2': _L3_gnn_in['b2']}

def reference(x, src, dst, edge_attr_4, edge_attr_8, edge_weight, node_vec, L0_gnn_Wq, L0_gnn_bq, L0_gnn_Wk, L0_gnn_bk, L0_gnn_Wv, L0_gnn_bv, L0_gnn_Wt, L0_gnn_bt, L0_gnn_Wo, L0_gnn_bo, L1_gnn_w1_s, L1_gnn_w1_v, L1_gnn_wsc_s, L1_gnn_wsc_v, L1_gnn_w2_s, L1_gnn_w2_v, L1_gnn_fc_w1, L1_gnn_fc_w2, L1_gnn_fc_w3, L1_gnn_g_s, L1_gnn_g_v, L2_gnn_Wq, L2_gnn_bq, L2_gnn_Wk, L2_gnn_bk, L2_gnn_Wv, L2_gnn_bv, L2_gnn_Wo, L2_gnn_bo, L3_gnn_W1, L3_gnn_b1, L3_gnn_W2, L3_gnn_b2):
    import jax
    import jax.numpy as jnp

    def _L0_gnn_ref(x, edge_index, edge_time, node_time, Wq, bq, Wk, bk, Wv, bv, Wt, bt, Wo, bo):
        import jax, jax.numpy as jnp
        import numpy as np
        NUM_NODES = 3125
        NUM_EDGES = 50000
        INPUT_DIM = 256
        OUTPUT_DIM = 256
        NUM_HEADS = 8
        HEAD_DIM = OUTPUT_DIM // NUM_HEADS
        n = x.shape[0]
        q = (x @ Wq + bq).reshape(n, NUM_HEADS, HEAD_DIM)
        k = (x @ Wk + bk).reshape(n, NUM_HEADS, HEAD_DIM)
        v = (x @ Wv + bv).reshape(n, NUM_HEADS, HEAD_DIM)
        src, dst = (edge_index[0], edge_index[1])
        time_diff = edge_time - node_time[dst]
        time_features = jnp.stack([jnp.sign(time_diff), jnp.log1p(jnp.abs(time_diff) / 3600.0)], axis=-1)
        temporal_weights = time_features @ Wt + bt
        scale = HEAD_DIM ** (-0.5)
        scores = jnp.einsum('ehd,ehd->eh', q[dst], k[src]) * scale + temporal_weights
        alpha = jax.nn.softmax(scores, axis=0)
        msg = alpha[..., None] * v[src]
        out = jax.ops.segment_sum(msg, dst, num_segments=n)
        out = out.reshape(n, OUTPUT_DIM)
        return out @ Wo + bo

    def _L1_gnn_ref(node_hiddens, edge_attr, edge_sh, w1_s, w1_v, wsc_s, wsc_v, w2_s, w2_v, fc_w1, fc_w2, fc_w3, g_s, g_v, edge_index):
        import jax, jax.numpy as jnp
        import numpy as np
        N_NODES = 1250
        N_EDGES = 20000
        MUL = 64
        NUM_BASIS = 8
        INV_SQRT3 = 0.5773502691896258
        EPS = 1e-05
        N = node_hiddens.shape[0]
        xs = node_hiddens[:, :MUL]
        xv = node_hiddens[:, MUL:].reshape(N, MUL, 3)
        h = jax.nn.silu(edge_attr @ fc_w1 * (1.0 / np.sqrt(float(NUM_BASIS))))
        h = jax.nn.silu(h @ fc_w2 * (1.0 / np.sqrt(64.0)))
        w = h @ fc_w3 * (1.0 / np.sqrt(64.0))
        wA, wB, wC, wD = jnp.split(w, 4, axis=1)
        inv = 1.0 / np.sqrt(float(MUL))
        sc_s = xs @ wsc_s * inv
        sc_v = jnp.einsum('nud,uv->nvd', xv, wsc_v) * inv
        ys = xs @ w1_s * inv
        yv = jnp.einsum('nud,uv->nvd', xv, w1_v) * inv
        src = edge_index[0]
        dst = edge_index[1]
        es = ys[dst]
        ev = yv[dst]
        sh0 = edge_sh[:, :1]
        sh1 = edge_sh[:, 1:]
        m0a = wA * es * sh0
        m0b = wD * jnp.einsum('eud,ed->eu', ev, sh1) * INV_SQRT3
        m1a = wB[:, :, None] * es[:, :, None] * sh1[:, None, :]
        m1b = wC[:, :, None] * ev * sh0[:, :, None]
        mid_s = jnp.concatenate([m0a, m0b], axis=1)
        mid_v = jnp.concatenate([m1a, m1b], axis=1)
        ns = jax.ops.segment_sum(mid_s, src, num_segments=N)
        nv = jax.ops.segment_sum(mid_v, src, num_segments=N)
        deg = jax.ops.segment_sum(jnp.ones((src.shape[0],), node_hiddens.dtype), src, num_segments=N)
        dn = jax.lax.rsqrt(jnp.maximum(deg, 1.0))
        ns = ns * dn[:, None]
        nv = nv * dn[:, None, None]
        inv2 = 1.0 / np.sqrt(2.0 * MUL)
        os_ = ns @ w2_s * inv2 + sc_s
        ov = jnp.einsum('nud,uv->nvd', nv, w2_v) * inv2 + sc_v
        os_ = os_ * jax.lax.rsqrt(jnp.mean(os_ * os_, axis=1, keepdims=True) + EPS) * g_s
        rms_v = jax.lax.rsqrt(jnp.mean(ov * ov, axis=(1, 2))[:, None, None] + EPS)
        ov = ov * rms_v * g_v[None, :, None]
        return jnp.concatenate([os_, ov.reshape(N, 3 * MUL)], axis=1)

    def _L2_gnn_ref(h, row, col, Wq, bq, Wk, bk, Wv, bv, Wo, bo):
        import jax, jax.numpy as jnp
        import numpy as np
        N = 3125
        E = 50000
        HIDDEN = 256
        HEADS = 8
        HEAD_DIM = HIDDEN // HEADS

        def _linear_params(key, fan_in, fan_out):
            k1, k2 = jax.random.split(key)
            s = 1.0 / np.sqrt(fan_in)
            W = jax.random.uniform(k1, (fan_in, fan_out), jnp.float32, -s, s)
            b = jax.random.uniform(k2, (fan_out,), jnp.float32, -s, s)
            return (W, b)
        n = h.shape[0]
        scaling = HEAD_DIM ** (-0.5)
        q = (h @ Wq + bq).reshape(n, HEADS, HEAD_DIM) * scaling
        k = (h @ Wk + bk).reshape(n, HEADS, HEAD_DIM)
        v = (h @ Wv + bv).reshape(n, HEADS, HEAD_DIM)
        s = jnp.einsum('ehd,ehd->eh', q[row], k[col])
        m = jax.ops.segment_max(s, row, num_segments=n)
        p = jnp.exp(s - m[row])
        denom = jax.ops.segment_sum(p, row, num_segments=n)
        attn = p / denom[row]
        out = jax.ops.segment_sum(attn[:, :, None] * v[col], row, num_segments=n)
        return out.reshape(n, HIDDEN) @ Wo + bo

    def _L3_gnn_ref(embeddings, edge_src, edge_dst, edge_val, W1, b1, W2, b2):
        import jax, jax.numpy as jnp
        import numpy as np
        N_NODES = 6250
        N_EDGES = 200000
        DIM = 256
        LEAKY_SLOPE = 0.2
        EPS = 1e-12
        ego_emb = embeddings @ W1.T + b1
        messages = edge_val[:, None] * embeddings[edge_src]
        neighbor_emb = jax.ops.segment_sum(messages, edge_dst, num_segments=embeddings.shape[0])
        interaction_emb = neighbor_emb * embeddings
        side_emb = (neighbor_emb + interaction_emb) @ W2.T + b2
        out = ego_emb + side_emb
        out = jnp.where(out >= 0, out, LEAKY_SLOPE * out)
        norm = jnp.sqrt(jnp.sum(out * out, axis=1, keepdims=True))
        return out / jnp.maximum(norm, EPS)
    edge_index = jnp.stack([src, dst])
    x = _layernorm(x + _L0_gnn_ref(x, edge_index, edge_weight, node_vec, L0_gnn_Wq, L0_gnn_bq, L0_gnn_Wk, L0_gnn_bk, L0_gnn_Wv, L0_gnn_bv, L0_gnn_Wt, L0_gnn_bt, L0_gnn_Wo, L0_gnn_bo), axis=-1)
    x = _layernorm(x + _L1_gnn_ref(x, edge_attr_8, edge_attr_4, L1_gnn_w1_s, L1_gnn_w1_v, L1_gnn_wsc_s, L1_gnn_wsc_v, L1_gnn_w2_s, L1_gnn_w2_v, L1_gnn_fc_w1, L1_gnn_fc_w2, L1_gnn_fc_w3, L1_gnn_g_s, L1_gnn_g_v, edge_index), axis=-1)
    x = _layernorm(x + _L2_gnn_ref(x, src, dst, L2_gnn_Wq, L2_gnn_bq, L2_gnn_Wk, L2_gnn_bk, L2_gnn_Wv, L2_gnn_bv, L2_gnn_Wo, L2_gnn_bo), axis=-1)
    x = _layernorm(x + _L3_gnn_ref(x, src, dst, edge_weight, L3_gnn_W1, L3_gnn_b1, L3_gnn_W2, L3_gnn_b2), axis=-1)
    return x

_drawn_inputs = setup_inputs


def setup_inputs(seed=0):
    import zlib

    import numpy as np

    out = dict(_drawn_inputs(seed))
    spreads = {'L1_gnn_g_s': (1.0, 0.2), 'L1_gnn_g_v': (1.0, 0.2)}
    factors = {'node_vec': 8.0,
     'L0_gnn_Wq': 8.0,
     'L0_gnn_bq': 64.0,
     'L0_gnn_Wk': 8.0,
     'L0_gnn_bk': 40.932,
     'L0_gnn_Wv': 8.0,
     'L0_gnn_bv': 64.0,
     'L0_gnn_Wt': 8.0,
     'L0_gnn_bt': 200.0,
     'L0_gnn_Wo': 8.0,
     'L2_gnn_bq': 39.721,
     'L2_gnn_bk': 200.0,
     'L2_gnn_bv': 2.801,
     'L3_gnn_W1': 200.0,
     'L3_gnn_b1': 200.0,
     'L3_gnn_b2': 200.0}
    for name, (base, spread) in spreads.items():
        noise = np.random.default_rng([zlib.crc32(name.encode()), seed]).standard_normal(out[name].shape)
        drawn = base * np.exp(spread * noise) if base else spread * noise
        out[name] = jnp.asarray(drawn.astype(out[name].dtype))
    for name, factor in factors.items():
        out[name] = (out[name] * factor).astype(out[name].dtype)
    return out
```

```python
from contextlib import ExitStack

import numpy as np
import concourse.bass as bass
from concourse import mybir

F32 = mybir.dt.float32
I32 = mybir.dt.int32
BF16 = mybir.dt.bfloat16
ALU = mybir.AluOpType
ACT = mybir.ActivationFunctionType
AX = mybir.AxisListType

P = 128
N_NODES = 3125
N_EDGES = 100000
D = 256
H = 8
DH = D // H
HC = DH + 1
AC = H * HC
MUL = 64
EC = 784
E_PAD = P * EC
NT = (N_NODES + P - 1) // P
LAST = N_NODES - (NT - 1) * P
NB = NT + 1
PAD_KEY = NB * P - 1
Q = 4
ME = Q * P
NM = (E_PAD + NB * (ME - 1)) // ME
NM += NM % 2
NMA = NM + 2
NEG = -1.0e30
LN_EPS = 1e-5
CREDIT = 2


class Macro:

    def __init__(self, i, off, before=0):
        self.i, self.off, self.u, self.before = i, off, off % 2, before

    def done(self, lag=0):
        return self.i * 2 + (self.off + 1 + CREDIT - lag + self.before)

    def turns(self, per, lag=0):
        return self.i * per + (self.off // 2 + 1 - lag) * per + self.before // 2 * per

    def index(self):
        return self.i * 2 + self.off


class Chain:

    def __init__(self, engine, sem):
        self.e, self.sem, self.n, self.i, self.per, self.at = engine, sem, 0, 0, 0, 0

    def __call__(self, ins):
        ins.then_inc(self.sem, 1)
        self.n += 1

    def value(self):
        return self.i * self.per + self.n

    def wait(self):
        self.e.wait_ge(self.sem, self.value())

    def enter(self, i, per):
        self.i, self.per, self.at = i, per, self.n

    def leave(self, times):
        assert self.n - self.at == self.per, (self.n - self.at, self.per)
        self.n = self.at + self.per * times
        self.i = self.per = 0


def bcast(ap, axis, shape):
    return ap.unsqueeze(axis).to_broadcast(shape)


def gnn_kernel(nc, io, out):
    ctx = ExitStack()
    with ctx:
        def sb(name, shape, dt=F32):
            return ctx.enter_context(nc.sbuf_tensor(name, shape, dt))

        def sem(name):
            return ctx.enter_context(nc.semaphore(name))

        def dram(name, shape, dt=F32):
            return nc.dram_tensor(name, shape, dt, kind="Internal").ap()

        WD, WS = 4, 16
        recs = {"d": dram("rec_d", [NMA * ME, WD]), "s": dram("rec_s", [NMA * ME, WS])}
        kv0 = dram("kv0", [NB * P, 2 * D])
        y1 = dram("y1", [NB * P, D])
        kv2 = dram("kv2", [NB * P, 2 * D])
        x3 = dram("x3", [NB * P, D])

        iota = sb("iota", [P, P])
        iota26 = sb("iota26", [P, NB])
        pcol = sb("pcol", [P, 1])
        ident = sb("ident", [P, P])
        ones = sb("ones", [P, P])
        tri = sb("tri", [P, P])
        x_sb = sb("x_sb", [P, NB, D])
        qz = sb("qz", [P, NB, D])
        acc_raw = sb("acc", [P, NB, 2 * D + 2])
        m_run = sb("m_run", [P, NB, H])
        jmap = {"d": sb("jmap_d", [1, NMA], I32), "s": sb("jmap_s", [1, NMA], I32)}
        deg = sb("deg", [P, NB])
        rec = {"d": sb("rec_sb_d", [P, 2, Q, WD]), "s": sb("rec_sb_s", [P, 2, Q, WS])}
        gat = sb("gat", [P, 2, Q, 2 * D])
        oh = sb("oh", [P, 2, Q, P])
        big = sb("big", [P, 4 * Q * D])
        small = sb("small", [P, 640])
        wts = sb("wts", [P, 3 * 2 * D])
        rows = sb("rows", [P, 3 * D])
        xs = sb("xs", [P, 2, 2 * D])
        xt = sb("xt", [P, 2, 2 * D])
        stage = sb("stage", [P, 2, 2 * D])

        ps = ctx.enter_context(nc.psum_tensor("ps", [P, 8, 512], F32))

        sems = {}

        def S(name):
            if name not in sems:
                sems[name] = sem(name)
            return sems[name]

        T = nc.tensor
        V = nc.vector
        A = nc.scalar
        G = nc.gpsimd

        s_bar = sem("s_bar")
        the_vchain = Chain(None, S("c_vector"))

        def vchain(e):
            the_vchain.e = e
            return the_vchain

        bars = [0]
        programs = {k: [] for k in ("sync", "gpsimd", "scalar", "vector", "tensor")}

        def phase(**fns):
            bars[0] += 1
            meet = 5 * bars[0]
            for name, todo in programs.items():
                todo.append((fns.get(name), meet))

        ai = acc_raw[:, :, :].rearrange("p a b -> p (a b)")
        FREE = {"at": 0}

        def scratch(cols, dt=F32, shape=None):
            at = FREE["at"]
            FREE["at"] += cols
            assert FREE["at"] <= NB * (2 * D + 2), FREE["at"]
            v = ai[:, at:at + cols]
            return v if dt == F32 else v.bitcast(dt)

        key_i = scratch(EC, I32)
        tmp_i = scratch(EC, I32)
        bkt = scratch(EC)
        rel = scratch(EC)
        idx_i = scratch(EC, I32)
        mask = qz[:, :, :].rearrange("p a b -> p (a b)")[:, 0:EC]
        scan = qz[:, :, :].rearrange("p a b -> p (a b)")[:, EC:2 * EC]
        pos = qz[:, :, :].rearrange("p a b -> p (a b)")[:, 2 * EC:3 * EC]
        zero = qz[:, :, :].rearrange("p a b -> p (a b)")[:, 3 * EC:4 * EC]
        pos_i = qz[:, :, :].rearrange("p a b -> p (a b)")[:, 4 * EC:5 * EC].bitcast(I32)
        attr = scratch(12 * EC)
        cnt = small[:, 0:NB]
        tot = small[:, 32:32 + NB]
        tot_i = small[:, 64:64 + NB].bitcast(I32)
        mac = small[:, 96:96 + NB]
        inc = small[:, 128:128 + NB]
        offs = small[:, 160:160 + NB]
        zero26 = small[:, 192:192 + NB]
        ring = wts[:, 0:2 * 8 * WS]
        pring = rows[:, 0:16].bitcast(I32)
        RH = 8
        jcmp = big[0:1, :]

        def consts_vector(e):
            c = vchain(e)
            c(V.memset(zero, 0.0))
            c(V.memset(x_sb[:, NT - 1:NB, :], 0.0))
            c(V.memset(zero26, 0.0))
            c(V.memset(ones[:, :], 1.0))
            e.wait_ge(S("s_iota"), 4)
            c(V.tensor_scalar(ident[:, :], iota[:, :], pcol[:, 0:1], None, ALU.is_equal))
            c(V.tensor_scalar(tri[:, :], iota[:, :], pcol[:, 0:1], None, ALU.is_gt))
            fill = gat[:, :, :, :].rearrange("p a b c -> p (a b c)")
            c(V.memset(fill[:, 0:FR * WS], 0.0))
            c.wait()
            for w, part in ((WD, fill[:, 0:FR * WD]), (WS, fill[:, 0:FR * WS])):
                v = part.rearrange("p (r w) -> p r w", w=w)
                e.wait_ge(S("s_fill"), 0 if w == WD else 16 * (NMA * ME // P // FR))
                c(V.memset(part, 0.0))
                c.wait()
                V.memset(v[:, :, 1:2], -1.0).then_inc(S("s_fillv"), 1)
                e.wait_ge(S("s_fillv"), 1 if w == WD else 2)

        FR = 112
        assert (NMA * ME // P) % FR == 0

        def consts_sync(e):
            x_in = io["x"]
            e.wait_ge(S("c_vector"), 2)
            e.dma_start(x_sb[:, 0:NT - 1, :],
                        x_in[0:(NT - 1) * P, :].rearrange("(j p) d -> p j d", p=P)).then_inc(S("s_x"), 16)
            e.dma_start(x_sb[0:LAST, NT - 1, :], x_in[(NT - 1) * P:N_NODES, :]).then_inc(S("s_x"), 16)
            fill = gat[:, :, :, :].rearrange("p a b c -> p (a b c)")
            n = 0
            for w, k in ((WD, "d"), (WS, "s")):
                e.wait_ge(S("s_fillv"), 1 if w == WD else 2)
                r = recs[k].rearrange("(c p r) w -> c p (r w)", p=P, r=FR)
                for b in range(NMA * ME // P // FR):
                    e.dma_start(r[b], fill[:, 0:FR * w]).then_inc(S("s_fill"), 16)
                    n += 16
            e.wait_ge(S("s_fill"), n)
            e.wait_ge(S("s_x"), 32)

        def consts_gpsimd(e):
            G.iota(iota[:, :], [[1, P]], base=0, channel_multiplier=0,
                   allow_small_or_imprecise_dtypes=True).then_inc(S("s_iota"), 1)
            G.iota(iota26[:, :], [[1, NB]], base=0, channel_multiplier=0,
                   allow_small_or_imprecise_dtypes=True).then_inc(S("s_iota"), 1)
            G.iota(pcol[:, :], [[1, 1]], base=0, channel_multiplier=1,
                   allow_small_or_imprecise_dtypes=True).then_inc(S("s_iota"), 1)
            G.iota(jcmp[:, 0:NMA], [[1, NMA]], base=0, channel_multiplier=0,
                   allow_small_or_imprecise_dtypes=True).then_inc(S("s_iota"), 1)

        phase(sync=consts_sync, vector=consts_vector, gpsimd=consts_gpsimd)

        def sort(k):
            W = {"d": WD, "s": WS}[k]
            key_in, idx_in = (io["dst_key"], io["src_idx"]) if k == "d" else (io["src_key"], io["dst_idx"])
            if k == "d":
                ew = attr[:, 0:EC]
                parts = [(0, 1, idx_i), (1, 1, rel), (2, 1, ew)]
            else:
                a4 = attr[:, 0:4 * EC].rearrange("p (t w) -> p t w", w=4)
                a8 = attr[:, 4 * EC:12 * EC].rearrange("p (t w) -> p t w", w=8)
                parts = [(0, 1, idx_i), (1, 1, rel), (2, 4, a4), (6, 8, a8)]
            n_in = 3 if k == "d" else 4
            s_in = S(f"s_in_{k}")

            def load(e):
                e.dma_start(key_i, key_in).then_inc(s_in, 16)
                e.dma_start(idx_i, idx_in).then_inc(s_in, 16)
                if k == "d":
                    e.dma_start(ew, io["edge_weight"]).then_inc(s_in, 16)
                else:
                    e.dma_start(a4, io["edge_attr_4"]).then_inc(s_in, 16)
                    e.dma_start(a8, io["edge_attr_8"]).then_inc(s_in, 16)

            def place(e):
                c = vchain(e)
                e.wait_ge(s_in, 16 * n_in)
                c(V.tensor_scalar(tmp_i, key_i, 7, None, ALU.arith_shift_right))
                c.wait()
                c(V.tensor_copy(bkt, tmp_i))
                c.wait()
                c(V.tensor_scalar(tmp_i, key_i, P - 1, None, ALU.bitwise_and))
                c.wait()
                c(V.tensor_copy(rel, tmp_i))
                c(V.memset(pos, 0.0))
                with e.Fori(0, NB) as b:
                    c.enter(b, 2)
                    c.wait()
                    c(V.tensor_scalar(mask, bkt, iota26[:, bass.ds(b, 1)], None, ALU.is_equal))
                    c.wait()
                    c(V.tensor_reduce(cnt[:, bass.ds(b, 1)], mask, AX.X, ALU.add))
                c.leave(NB)
                c.wait()
                e.drain().then_inc(S(f"s_cnt_{k}"), 1)
                e.wait_ge(S(f"s_tot_{k}"), 1)
                c(V.tensor_copy(tot, ps[:, 0, 0:NB]))
                c(V.tensor_copy(offs, ps[:, 1, 0:NB]))
                c.wait()
                c(V.tensor_scalar(tot_i, tot, float(ME - 1), None, ALU.add))
                c.wait()
                c(V.tensor_scalar(tot_i, tot_i, ME.bit_length() - 1, None, ALU.arith_shift_right))
                c.wait()
                c(V.tensor_copy(mac, tot_i))
                c.wait()
                c(V.tensor_tensor_scan(inc, mac, zero26, 0.0, ALU.add, ALU.add))
                c.wait()
                c(V.tensor_tensor(mac, inc, mac, ALU.subtract))
                c.wait()
                c(V.scalar_tensor_tensor(offs, mac, float(ME), offs, ALU.mult, ALU.add))
                c.wait()
                c(V.tensor_scalar(offs, offs, 1.0, None, ALU.subtract))
                jf = jcmp[:, NMA:2 * NMA]
                half = NMA // 2
                wide = oh_wide[:, 0:half * NB].rearrange("p (m b) -> p m b", b=NB)
                for part in range(2):
                    m3 = bcast(jcmp[:, part * half:(part + 1) * half], 2, [1, half, NB])
                    c(V.tensor_tensor(wide, m3, bcast(inc[0:1, :], 1, [1, half, NB]), ALU.is_ge))
                    c.wait()
                    c(V.tensor_reduce(jf[:, part * half:(part + 1) * half], wide, AX.X, ALU.add))
                    c.wait()
                c(V.tensor_scalar(jmap[k][:, :], jf, float(NB - 1), None, ALU.min))
                with e.Fori(0, NB) as b:
                    c.enter(b, 4)
                    c.wait()
                    c(V.tensor_scalar(mask, bkt, iota26[:, bass.ds(b, 1)], None, ALU.is_equal))
                    c.wait()
                    c(V.tensor_tensor_scan(scan, mask, zero, offs[:, bass.ds(b, 1)], ALU.add, ALU.add))
                    c.wait()
                    c(V.tensor_tensor(scan, scan, mask, ALU.mult))
                    c.wait()
                    c(V.tensor_tensor(pos, pos, scan, ALU.add))
                c.leave(NB)
                c.wait()
                V.tensor_copy(pos_i, pos).then_inc(S(f"s_pos_{k}"), 1)

            def totals(e):
                e.wait_ge(S(f"s_cnt_{k}"), 1)
                T.matmul(ps[:, 0, 0:NB], ones[:, :], cnt, start=True, stop=True)
                T.matmul(ps[:, 1, 0:NB], tri[:, :], cnt, start=True, stop=True).then_inc(S(f"s_tot_{k}"), 1)

            slot_of = [S(f"s_put_{k}{h}") for h in range(2)]
            rr = ring[:, 0:2 * RH * W].rearrange("p (h t w) -> p h t w", h=2, t=RH)

            def fill_ring(e):
                c = Chain(e, S(f"c_ring_{k}"))
                if W != 14:
                    c(A.activation(ring[:, 0:2 * RH * W], zero[:, 0:2 * RH * W], ACT.Copy))
                    c.wait()
                e.wait_ge(S(f"s_pos_{k}"), 1)
                with e.Fori(0, EC // (2 * RH)) as i:
                    for h in range(2):
                        e.wait_ge(slot_of[h], i * (16 * RH))
                        at = i * (2 * RH) + h * RH
                        for w, n, col in parts:
                            o = rr[:, h, :, w:w + n]
                            s = col[:, bass.ds(at, RH)] if n == 1 else col[:, bass.ds(at, RH), :]
                            if n == 1:
                                o = rr[:, h, :, w]
                            if w == 0:
                                o = o.bitcast(I32)
                            A.activation(o, s, ACT.Copy).then_inc(S(f"s_ring_{k}"), 1)
                        A.activation(pring[:, h * RH:(h + 1) * RH], pos_i[:, bass.ds(at, RH)], ACT.Copy)\
                            .then_inc(S(f"s_ring_{k}"), 1)

            def scatter(e):
                per = len(parts) + 1
                with e.Fori(0, EC // (2 * RH)) as i:
                    for h in range(2):
                        e.wait_ge(S(f"s_ring_{k}"), i * (2 * per) + (h + 1) * per)
                        e.sem_inc(S("s_gp"), 1)
                        for t in range(RH):
                            e.indirect_dma_start(
                                out=recs[k], out_offset=bass.IndirectOffsetOnAxis(
                                    ap=pring[:, h * RH + t:h * RH + t + 1], axis=0),
                                in_=rr[:, h, t, :], in_offset=None).then_inc(slot_of[h], 16)
                for h in range(2):
                    e.wait_ge(slot_of[h], 16 * RH * (EC // (2 * RH)))
                    e.sem_inc(S("s_gp"), 1)

            phase(sync=load, vector=place, tensor=totals, scalar=fill_ring, gpsimd=scatter)

        oh_wide = gat[0:1, :, :, :].rearrange("p a b c -> p (a b c)")
        sort("d")
        sort("s")

        work = sb("work", [P, 3072])
        xs = work[:, 0:1024].rearrange("p (u c) -> p u c", u=2)
        xt = work[:, 1024:2048].rearrange("p (u c) -> p u c", u=2)
        stage = work[:, 2048:3072].rearrange("p (u c) -> p u c", u=2)
        credits = []

        def stages(tag, *names, credit=CREDIT):
            made = {}
            for n in names:
                made[n] = sem(f"{tag}_{n}")
                credits.append((made[n], credit))
            return made

        def row_bcast(src):
            return src.partition_broadcast(P)

        tile_sems = stages("tile", "copy", "turn", "xt", "mm", "evac")
        s_w = sem("tile_w")
        s_out = [sem(f"tile_out{u}") for u in range(2)]
        s_ready = sem("tile_ready")
        rounds = {"all": 0, "out": 0, "loads": 0}

        def project(tag, n_chunks, zin, loads, groups, evac, out_dma=None, prepare=None, prep_ws=None):
            s, before = tile_sems, NB * rounds["all"]
            kept = NB * rounds["out"]
            rounds["all"] += 1
            rounds["out"] += out_dma is not None
            ready = rounds["all"]
            rounds["loads"] += 16 * len(loads)
            loaded = rounds["loads"]
            wide = n_chunks * P

            def load(e):
                for dst_ap, src_ap in loads:
                    e.dma_start(dst_ap, src_ap).then_inc(s_w, 16)
                if out_dma is not None:
                    with e.Fori(0, NB // 2) as i:
                        for u in range(2):
                            m = Macro(i, u, before)
                            at = e.snap(m.index())
                            e.wait_ge(s["evac"], m.done())
                            e.sem_inc(S("s_sp"), 1)
                            out_dma(e, at, stage[:, u, :]).then_inc(s_out[u], 16)
                    for u in range(2):
                        e.wait_ge(s_out[u], 8 * (NB + kept))

            def copies(e):
                e.wait_ge(s_ready, ready)
                with e.Fori(0, NB // 2) as i:
                    for u in range(2):
                        m = Macro(i, u, before)
                        e.wait_ge(s["turn"], m.done(2))
                        G.tensor_copy(xs[:, u, 0:wide], zin[:, bass.ds(m.index(), 1), 0:wide])\
                            .then_inc(s["copy"], 1)

            def tensor(e):
                e.wait_ge(s_w, loaded)
                e.wait_ge(s_ready, ready)
                with e.Fori(0, NB // 2) as i:
                    for u in range(2):
                        m = Macro(i, u, before)
                        e.wait_ge(s["copy"], m.done())
                        e.wait_ge(s["xt"], m.done(2))
                        for c in range(n_chunks):
                            last = T.transpose(ps[:, u, c * P:(c + 1) * P], xs[:, u, c * P:(c + 1) * P],
                                               ident[:, :])
                        last.then_inc(s["turn"], 1)
                        e.wait_ge(s["xt"], m.done())
                        e.wait_ge(s["evac"], m.done(2))
                        for b, c0, c1, terms in groups:
                            for n, (c, w) in enumerate(terms):
                                last = T.matmul(ps[:, 2 + 2 * u + b, c0:c1], xt[:, u, c * P:(c + 1) * P], w,
                                                start=(n == 0), stop=(n == len(terms) - 1))
                        last.then_inc(s["mm"], 1)

            def scalar(e):
                with e.Fori(0, NB // 2) as i:
                    for u in range(2):
                        m = Macro(i, u, before)
                        e.wait_ge(s["turn"], m.done())
                        e.wait_ge(s["mm"], m.done(2))
                        A.activation(xt[:, u, 0:wide], ps[:, u, 0:wide], ACT.Copy).then_inc(s["xt"], 1)

            def vector(e):
                c = vchain(e)
                if prepare:
                    prepare(e, c)
                e.wait_ge(s_w, loaded)
                if prep_ws:
                    prep_ws(e, c)
                c.wait()
                e.sem_inc(s_ready, 1)
                with e.Fori(0, NB // 2) as i:
                    for u in range(2):
                        m = Macro(i, u, before)
                        e.wait_ge(s["mm"], m.done())
                        if out_dma is not None:
                            e.wait_ge(s_out[u], Macro(i, u, kept).turns(16, 1))
                        evac(e, m, ps[:, 2 + 2 * u:4 + 2 * u, :], stage[:, u, :]).then_inc(s["evac"], 1)

            phase(sync=load, gpsimd=copies, tensor=tensor, scalar=scalar, vector=vector)

        def store_rows(table, width):
            def go(e, m, src):
                t = table.rearrange("(j p) c -> j p c", p=P)
                return e.dma_start(t[bass.ds(m, 1)].rearrange("a p c -> p (a c)"), src[:, 0:width])
            return go

        junk = acc_raw[:, :, 0:D]

        def rstd(e, c, s_act, n, stat, scale, tmp):
            c(V.tensor_scalar(tmp, stat, scale, LN_EPS, ALU.mult, ALU.add))
            c.wait()
            e.sem_inc(s_act[0], 1)
            e.wait_ge(s_act[1], n)
            c(V.reciprocal(stat, tmp))
            c.wait()

        def layernorm(tag, before=None, after=None, roots=()):
            s_act = (sem(f"{tag}_go"), sem(f"{tag}_root"))
            mean = small[:, 0:NB]
            var = small[:, 32:32 + NB]
            tmp = small[:, 64:64 + NB]
            todo = list(roots) + [tmp]

            def vector(e):
                c = vchain(e)
                n = 0
                if before:
                    n = before(e, c, s_act)
                x = x_sb[:, :, :]
                c(V.tensor_reduce(mean, x, AX.X, ALU.add))
                c.wait()
                c(V.tensor_scalar(mean, mean, 1.0 / D, None, ALU.mult))
                c.wait()
                c(V.tensor_tensor(x, x, bcast(mean, 2, [P, NB, D]), ALU.subtract))
                c.wait()
                c(V.tensor_tensor(junk, x, x, ALU.mult))
                c.wait()
                c(V.tensor_reduce(var, junk, AX.X, ALU.add))
                c.wait()
                rstd(e, c, s_act, n + 1, var, 1.0 / D, tmp)
                c(V.tensor_tensor(x, x, bcast(var, 2, [P, NB, D]), ALU.mult))
                c.wait()
                if after:
                    after(e, c)

            def scalar(e):
                for n, t in enumerate(todo):
                    e.wait_ge(s_act[0], n + 1)
                    A.activation(t, t, ACT.Sqrt).then_inc(s_act[1], 1)

            return vector, scalar

        def macro_loops(A1, B1=None):
            def go(e):
                A1(e, Macro(0, 0))
                with e.Fori(0, NM // 2) as i:
                    for u in range(2):
                        A1(e, Macro(i, u + 1))
                        if B1:
                            B1(e, Macro(i, u))
            return go

        iota4 = bcast(iota[:, :], 1, [P, Q, P])

        def attention(L, k, table):
            W = {"d": WD, "s": WS}[k]
            timed = L == 0
            s = stages(f"a{L}", "oh", "tr", "oht", "qx", "prod", "ln", "mq", "mt", "dg", "mb",
                       "f", "ef", "p", "pv", "sum", "flush", "s3", "st", "me", "td", "sp")
            s_hm, s_hr = sem(f"a{L}_hm"), sem(f"a{L}_hr")
            credits.append((s_hr, 3))
            s_rec = [sem(f"a{L}_rec{u}") for u in range(2)]
            s_gat = [sem(f"a{L}_gat{u}") for u in range(2)]
            cB = sem(f"a{L}_cB")
            acc = acc_raw[:, :, 0:AC]
            r_sb = rec[k]
            oht = xs
            prod = big[:, 0:Q * D].rearrange("p (q c) -> p q c", q=Q)
            pvb = big[:, Q * D:Q * D + 2 * Q * AC].rearrange("p (u q c) -> p u q c", u=2, q=Q)
            col = lambda a, n: small[:, a:a + n]
            td, ab, sg, ln, pen = (col(a, 4) for a in (0, 4, 8, 12, 16))
            sc, t1, t2, sm = (col(a, 32) for a in (32, 64, 96, 128))
            mq, mn, dd, ff, mx = (col(a, 8) for a in (160, 168, 176, 184, 192))
            mr = small[0:H, 200:201]
            dg = small[0:H, 208:216]
            r1, r2 = col(224, 32), col(256, 32)
            s3 = small[:, 288:336].bitcast(BF16)
            st3 = small[:, 336:400].bitcast(BF16)
            nh = work[:, 2048:2304].bitcast(BF16)
            sel = small[:, 400:416].bitcast(BF16)
            bigI = work[:, 2304:2368].bitcast(BF16)
            w0, w1, bt4 = rows[:, 0:8], rows[:, 8:16], rows[:, 16:48]
            bank7 = ps[:, 7, :]
            psQ = [ps[:, 1 + 2 * u * timed:3 + 2 * u * timed, :].rearrange("p b c -> p (b c)")
                   for u in range(2)]
            psO = [ps[:, 5 + u if timed else 3, 0:AC] for u in range(2)]
            times = [ps[:, 5 + u, AC:AC + Q] for u in range(2)]
            q_lag, o_lag = (2, 2) if timed else (1, 1)

            def sync_a(e, m):
                at = e.snap(m.index())
                e.wait_ge(s["mq" if timed else "oh"], m.done(2))
                e.sem_inc(S("s_sp"), 1)
                e.wait_ge(s_gat[m.u], m.turns(64, 1))
                e.sem_inc(S("s_sp"), 1)
                r = recs[k].rearrange("(m p q) w -> m p (q w)", p=P, q=Q)
                e.dma_start(r_sb[:, m.u, :, :].rearrange("p q w -> p (q w)"),
                            r[bass.ds(at, 1)].rearrange("a p c -> p (a c)")).then_inc(s_rec[m.u], 16)

            def sync(e):
                if timed:
                    wt = io["L0_gnn_Wt"]
                    e.dma_start(w0, row_bcast(wt[0])).then_inc(S("s_wt"), 16)
                    e.dma_start(w1, row_bcast(wt[1])).then_inc(S("s_wt"), 16)
                    for q in range(Q):
                        e.dma_start(bt4[:, q * H:(q + 1) * H], row_bcast(io["L0_gnn_bt"])).then_inc(S("s_wt"), 16)
                    e.wait_ge(S("c_nv"), 1)
                    e.dma_start(deg[:, :], io["node_vec"]).then_inc(S("s_wt"), 16)
                macro_loops(sync_a)(e)

            def pool_a(e, m):
                e.wait_ge(s_rec[m.u], m.turns(16))
                e.sem_inc(S("s_gp"), 1)
                e.wait_ge(s["pv"], m.done(2))
                e.sem_inc(S("s_gp"), 1)
                for q in range(Q):
                    e.indirect_dma_start(
                        out=gat[:, m.u, q, :], out_offset=None, in_=table,
                        in_offset=bass.IndirectOffsetOnAxis(ap=r_sb[:, m.u, q, 0:1].bitcast(I32), axis=0),
                    ).then_inc(s_gat[m.u], 16)

            def pe_a(e, m):
                e.wait_ge(s["oh"], m.done())
                e.wait_ge(s["oht"], m.done(1))
                for q in range(Q):
                    last = T.transpose(ps[:, 0, q * P:(q + 1) * P], oh[:, m.u, q, :], ident[:, :])
                last.then_inc(s["tr"], 1)
                j = e.value_load(jmap[k][0:1, bass.ds(m.index(), 1)], min_val=0, max_val=NB - 1)
                e.wait_ge(s["oht"], m.done())
                e.wait_ge(s["prod"], m.done(q_lag))
                if timed:
                    e.wait_ge(s["flush"], m.done(2))
                for q in range(Q):
                    o = oht[:, m.u, q * P:(q + 1) * P]
                    last = T.matmul(psQ[m.u][:, q * D:(q + 1) * D], o, qz[:, bass.ds(j, 1), :], start=True, stop=True)
                    if timed:
                        last = T.matmul(times[m.u][:, q:q + 1], o, deg[:, bass.ds(j, 1)],
                                        start=True, stop=True)
                last.then_inc(s["qx"], 1)

            def pe_b(e, m):
                if timed:
                    e.wait_ge(s["mq"], m.done())
                    T.transpose(bank7[0:H, 16:16 + P], mq, ident[:, :]).then_inc(s["mt"], 1)
                    e.wait_ge(s["dg"], m.done())
                    T.matmul(bank7[:, 144:144 + H], ones[0:H, :], dg, start=True, stop=True).then_inc(s["mb"], 1)
                else:
                    e.wait_ge(s["s3"], m.done())
                    T.transpose(bank7[0:96, 192:256].bitcast(BF16), s3, identb).then_inc(s["st"], 1)
                    e.wait_ge(s["sp"], m.done())
                    for h in range(H):
                        e.wait_ge(s_hr, m.i * 16 + (m.off * H + h + 1))
                        b = 4 + (h % 3)
                        e_sum(h, b)
                    e.wait_ge(s["mq"], m.done())
                    for q in range(Q):
                        last = T.matmul(bank7[:, 152 + q * H:160 + q * H], oht[:, m.u, q * P:(q + 1) * P], mn,
                                        start=True, stop=True)
                    last.then_inc(s["me"], 1)
                e.wait_ge(s["pv"], m.done())
                e.wait_ge(s["p"], m.done())
                e.wait_ge(s["flush"], m.done(o_lag))
                for q in range(Q):
                    last = T.matmul(psO[m.u], oh[:, m.u, q, :], pvb[:, m.u, q, :], start=(q == 0), stop=(q == Q - 1))
                last.then_inc(s["sum"], 1)

            def e_sum(h, b):
                for q in range(Q):
                    c = q * H + h
                    T.matmul(ps[:, b, q * P:(q + 1) * P], sel[0:96, c:c + 1].to_broadcast([96, P]),
                             st3[0:96, :], start=(q == 0), stop=False)
                last = T.matmul(ps[:, b, :], bigI, nh, start=False, stop=True)
                last.then_inc(s_hm, 1)

            def act_a(e, m):
                e.wait_ge(s["tr"], m.done())
                e.wait_ge(s["qx"] if timed else s["me"], m.done(2))
                A.activation(oht[:, m.u, :], ps[:, 0, :], ACT.Copy).then_inc(s["oht"], 1)

            def act_b(e, m):
                if timed:
                    e.wait_ge(s["td"], m.done())
                    A.activation(ln, ab, ACT.Ln, scale=1.0 / 3600.0, bias=1.0).then_inc(s["ln"], 1)
                else:
                    e.wait_ge(s["st"], m.done())
                    A.activation(st3[0:96, :], bank7[0:96, 192:256].bitcast(BF16), ACT.Copy).then_inc(s["sp"], 1)
                e.wait_ge(s["f"], m.done())
                A.activation(ff, dd, ACT.Exp).then_inc(s["ef"], 1)
                e.wait_ge(s["sum"], m.done(2))
                A.activation(pvb[:, m.u, :, :].rearrange("p q (h c) -> p q h c", c=HC)[:, :, :, DH],
                             sm.rearrange("p (q h) -> p q h", q=Q), ACT.Exp).then_inc(s["p"], 1)

            def dve_a(e, m):
                e.wait_ge(s_rec[m.u], m.turns(16))
                e.wait_ge(s["sum"], m.done(2))
                V.tensor_tensor(oh[:, m.u, :, :], iota4, bcast(r_sb[:, m.u, :, 1], 2, [P, Q, P]), ALU.is_equal)\
                    .then_inc(s["oh"], 1)

            def dve_b(e, m, first):
                c = Chain(e, cB)
                c.n = PER * m.off
                c.enter(m.i, 2 * PER)
                n0 = c.n
                e.wait_ge(s["qx"], m.done())
                if timed:
                    c(V.tensor_tensor(td, r_sb[:, m.u, :, 2], times[m.u], ALU.subtract))
                    c.wait()
                    c(V.tensor_scalar(sg, td, 0.0, -1.0, ALU.is_gt, ALU.add))
                    c.wait()
                    c(V.scalar_tensor_tensor(sg, td, 0.0, sg, ALU.is_ge, ALU.add))
                    c.wait()
                    V.tensor_tensor(ab, td, sg, ALU.mult).then_inc(s["td"], 1)
                    c(V.tensor_scalar(pen, r_sb[:, m.u, :, 1], 0.0, NEG, ALU.is_lt, ALU.mult))
                e.wait_ge(s_gat[m.u], m.turns(64))
                V.tensor_tensor(prod, psQ[m.u].rearrange("p (q c) -> p q c", q=Q), gat[:, m.u, :, 0:D],
                                ALU.mult).then_inc(s["prod"], 1)
                e.wait_ge(s["prod"], m.done())
                c(V.tensor_reduce(sc, prod.rearrange("p q (h c) -> p (q h) c", c=DH), AX.X, ALU.add))
                v4 = lambda a: a.rearrange("p (q h) -> p q h", q=Q)
                if timed:
                    c.wait()
                    c(V.tensor_tensor(v4(t1), bcast(sg, 2, [P, Q, H]), bcast(w0, 1, [P, Q, H]), ALU.mult))
                    e.wait_ge(s["ln"], m.done())
                    c(V.tensor_tensor(v4(t2), bcast(ln, 2, [P, Q, H]), bcast(w1, 1, [P, Q, H]), ALU.mult))
                    c.wait()
                    c(V.tensor_tensor(t1, t1, t2, ALU.add))
                    c.wait()
                    c(V.tensor_tensor(t1, t1, bt4, ALU.add))
                    c.wait()
                    c(V.tensor_tensor(v4(t1), v4(t1), bcast(pen, 2, [P, Q, H]), ALU.add))
                    c.wait()
                    c(V.scalar_tensor_tensor(sc, sc, DH ** -0.5, t1, ALU.mult, ALU.add))
                    c.wait()
                    V.tensor_reduce(mq, sc.rearrange("p (q h) -> p h q", q=Q), AX.X, ALU.max).then_inc(s["mq"], 1)
                    e.wait_ge(s["mt"], m.done())
                    c(V.tensor_reduce(mr, bank7[0:H, 16:16 + P], AX.X, ALU.max))
                    c.wait()
                    V.tensor_scalar(dg, ident[0:H, 0:H], mr, None, ALU.mult).then_inc(s["dg"], 1)
                else:
                    c.wait()
                    c(V.tensor_scalar(nh, oht[:, m.u, :], -1.0, None, ALU.add))
                    c(V.tensor_scalar(sc, sc, DH ** -0.5, None, ALU.mult))
                    c.wait()
                    c(V.tensor_copy(s3[:, 0:32], sc))
                    c.wait()
                    c(V.tensor_tensor(r1, sc, s3[:, 0:32], ALU.subtract))
                    c.wait()
                    c(V.tensor_copy(s3[:, 32:64], r1))
                    c.wait()
                    c(V.tensor_tensor(r2, r1, s3[:, 32:64], ALU.subtract))
                    c.wait()
                    V.tensor_copy(s3[:, 64:96], r2).then_inc(s["s3"], 1)
                    for h in range(H):
                        e.wait_ge(s_hm, m.i * 16 + (m.off * H + h + 1))
                        V.tensor_reduce(mx[:, h:h + 1], ps[:, 4 + (h % 3), :], AX.X, ALU.max).then_inc(s_hr, 1)
                    e.wait_ge(s_hr, m.i * 16 + (m.off * H + H + 3))
                j = e.value_load(jmap[k][0:1, bass.ds(m.index(), 1)], min_val=0, max_val=NB - 1)
                mj = m_run[:, bass.ds(j, 1), :]
                if timed:
                    e.wait_ge(s["mb"], m.done())
                    c(V.tensor_tensor(mn, mj, bank7[:, 144:144 + H], ALU.max))
                    c.wait()
                else:
                    V.tensor_tensor(mn, mj, mx, ALU.max).then_inc(s["mq"], 1)
                    e.wait_ge(s["mq"], m.done())
                c(V.tensor_tensor(dd, mj, mn, ALU.subtract))
                if timed:
                    other = bcast(mn, 1, [P, Q, H])
                else:
                    e.wait_ge(s["me"], m.done())
                    other = v4(bank7[:, 152:184])
                c(V.tensor_tensor(v4(sm), v4(sc), other, ALU.subtract))
                c.wait()
                V.tensor_scalar(mj, mn, 1.0, None, ALU.mult).then_inc(s["f"], 1)
                e.wait_ge(s["f"], m.done())
                aj = acc[:, bass.ds(j, 1), :].rearrange("p a (h c) -> p (a h) c", c=HC)
                e.wait_ge(s["ef"], m.done())
                e.wait_ge(s["flush"], m.done(1))
                c(V.tensor_tensor(aj, aj, bcast(ff, 2, [P, H, HC]), ALU.mult))
                e.wait_ge(s["p"], m.done())
                pw = pvb[:, m.u, :, :].rearrange("p q (h c) -> p q h c", c=HC)
                gv = gat[:, m.u, :, D:2 * D].rearrange("p q (h c) -> p q h c", c=DH)
                V.tensor_tensor(pw[:, :, :, 0:DH], gv, pw[:, :, :, DH:HC].to_broadcast([P, Q, H, DH]),
                                ALU.mult).then_inc(s["pv"], 1)
                c.wait()
                e.wait_ge(s["sum"], m.done())
                V.tensor_tensor(aj, aj, psO[m.u].rearrange("p (h c) -> p h c", c=HC), ALU.add).then_inc(s["flush"], 1)
                used.add(c.n - n0)

            used = set()
            PER = 16 if timed else 10

            identb = work[:, 2368:2432].bitcast(BF16)

            def dve(e):
                c = vchain(e)
                c(V.memset(acc, 0.0))
                c(V.memset(m_run[:, :, :], NEG))
                if timed:
                    V.memset(deg[:, :], 0.0).then_inc(S("c_nv"), 1)
                    e.wait_ge(S("s_wt"), 16 * 7)
                else:
                    c(V.tensor_scalar(bigI, ident[:, :], -NEG, None, ALU.mult))
                    c(V.tensor_copy(identb, ident[:, :]))
                    for b in range(3):
                        c(V.tensor_copy(sel[32 * b:32 * b + 32, :], ident[32 * b:32 * b + 32, 32 * b:32 * b + 32]))
                c.wait()
                e.sem_inc(s_go, 1)
                macro_loops(dve_a, lambda e, m: dve_b(e, m, False))(e)
                assert used == {PER}, (used, PER)

            s_go = sem(f"a{L}_go")

            def after_go(fn):
                def go(e):
                    e.wait_ge(s_go, 1)
                    fn(e)
                return go

            phase(sync=sync, gpsimd=macro_loops(pool_a), scalar=after_go(macro_loops(act_a, act_b)),
                  tensor=after_go(macro_loops(pe_a, pe_b)), vector=dve)

        wk = wts[:, :].rearrange("p (c n) -> p c n", c=2)

        def halves(w):
            return w.rearrange("(c p) n -> p c n", p=P)

        def qkv(tag, L, table):
            loads = []
            for n, x in enumerate("qkv"):
                loads.append((wk[:, :, n * D:(n + 1) * D], halves(io[f"L{L}_gnn_W{x}"])))
                loads.append((rows[:, n * D:(n + 1) * D], row_bcast(io[f"L{L}_gnn_b{x}"])))
            groups = [(0, 0, D, [(c, wk[:, c, 0:D]) for c in range(2)]),
                      (1, 0, 2 * D, [(c, wk[:, c, D:3 * D]) for c in range(2)])]

            def evac(e, m, pp, st):
                V.tensor_tensor(qz[:, bass.ds(m.index(), 1), :], pp[:, 0, 0:D], rows[:, 0:D], ALU.add)
                return V.tensor_tensor(st, pp[:, 1, :], rows[:, D:3 * D], ALU.add)

            project(tag, 2, x_sb, loads, groups, evac, store_rows(table, 2 * D))

        def add_to_x(e, m, pp, st):
            xj = x_sb[:, bass.ds(m.index(), 1), :]
            return V.tensor_tensor(xj, xj, pp[:, 0, 0:D], ALU.add)

        def out_proj(tag, L, prepare=None):
            def prep(e, c):
                if prepare:
                    prepare(e, c)

            def bias(e, c):
                c(V.tensor_tensor(x_sb[:, :, :], x_sb[:, :, :], bcast(rows[:, 0:D], 1, [P, NB, D]), ALU.add))
            loads = [(wk[:, :, 0:D], halves(io[f"L{L}_gnn_Wo"])), (rows[:, 0:D], row_bcast(io[f"L{L}_gnn_bo"]))]
            project(tag, 2, qz, loads, [(0, 0, D, [(c, wk[:, c, 0:D]) for c in range(2)])], add_to_x,
                    prepare=prep, prep_ws=bias)

        acc4 = acc_raw[:, :, 0:AC].rearrange("p j (h c) -> p j h c", c=HC)
        qz4 = qz[:, :, :].rearrange("p j (h c) -> p j h c", c=DH)

        def softmax_over_edges():
            gmax = small[:, 0:H]
            F = big[:, 0:NT * H]
            Fv = F.rearrange("p (j h) -> p j h", h=H)
            den = big[:, NT * H:2 * NT * H].rearrange("p (j h) -> p j h", h=H)
            part = small[:, 8:16]
            rz = small[:, 16:24]

            def vector(e):
                c = vchain(e)
                c(V.tensor_reduce(gmax, m_run[:, 0:NT, :].rearrange("p j h -> p h j"), AX.X, ALU.max))
                c.wait()
                V.tensor_tensor(Fv, m_run[:, 0:NT, :], bcast(gmax, 1, [P, NT, H]), ALU.subtract).then_inc(S("n0_f"), 1)
                e.wait_ge(S("n0_e"), 1)
                c(V.tensor_tensor(den, acc4[:, 0:NT, :, DH], Fv, ALU.mult))
                c.wait()
                V.tensor_reduce(part, den.rearrange("p j h -> p h j"), AX.X, ALU.add).then_inc(S("n0_f"), 1)
                e.wait_ge(S("n0_z"), 1)
                c(V.reciprocal(rz, ps[:, 7, 0:H]))
                c.wait()
                c(V.tensor_tensor(Fv, Fv, bcast(rz, 1, [P, NT, H]), ALU.mult))
                c.wait()
                c(V.memset(qz[:, NT, :], 0.0))
                for h in range(H):
                    c(V.tensor_tensor(qz4[:, 0:NT, h, :], acc4[:, 0:NT, h, 0:DH],
                                      bcast(Fv[:, :, h], 2, [P, NT, DH]), ALU.mult))
                c.wait()

            def scalar(e):
                e.wait_ge(S("n0_f"), 1)
                A.activation(F, F, ACT.Exp).then_inc(S("n0_e"), 1)

            def tensor(e):
                e.wait_ge(S("n0_f"), 2)
                T.matmul(ps[:, 7, 0:H], ones[:, :], part, start=True, stop=True).then_inc(S("n0_z"), 1)

            phase(vector=vector, scalar=scalar, tensor=tensor)

        qkv("p0", 0, kv0)
        attention(0, "d", kv0)
        softmax_over_edges()
        out_proj("o0", 0)
        v_ln, a_ln = layernorm("l0")
        phase(vector=v_ln, scalar=a_ln)

        INV_SQRT3 = 3.0 ** -0.5
        y_scale = MUL ** -0.5

        def layer1():
            wy = wts[:, 0:2 * 2 * P].rearrange("p (c n) -> p c n", c=2)

            def w_blocks(c, sel_):
                return wy[:, c, sel_ * P:(sel_ + 1) * P]

            w_zero = sem("p1_zero")
            loads = []
            for c in range(2):
                for which, (ws, wv) in enumerate((("L1_gnn_w1_s", "L1_gnn_w1_v"), ("L1_gnn_wsc_s", "L1_gnn_wsc_v"))):
                    for half in range(2):
                        w = ws if c == 0 and half == 0 else wv
                        loads.append((w_blocks(c, which)[half * MUL:(half + 1) * MUL, half * MUL:(half + 1) * MUL],
                                      io[w]))
            groups = [(c, 0, 2 * P, [(c, wy[:, c, :])]) for c in range(2)]

            def split(e, c):
                c(V.tensor_copy(qz[:, :, 0:MUL], x_sb[:, :, 0:MUL]))
                for d in range(3):
                    c(V.tensor_copy(qz[:, :, (d + 1) * MUL:(d + 2) * MUL], x_sb[:, :, MUL + d::3]))
                c.wait()

            def evac(e, m, pp, st):
                V.tensor_scalar(qz[:, bass.ds(m.index(), 1), :].rearrange("p a (c n) -> p (a c) n", c=2),
                                pp[:, :, P:2 * P], y_scale, None, ALU.mult)
                return V.tensor_scalar(st[:, 0:D].rearrange("p (c n) -> p c n", c=2), pp[:, :, 0:P],
                                       y_scale, None, ALU.mult)

            def clear(e):
                V.memset(wts[:, 0:4 * P], 0.0).then_inc(w_zero, 1)
                e.wait_ge(w_zero, 1)

            phase(vector=clear)
            project("p1", 2, qz, loads, groups, evac, store_rows(y1, D), prepare=split)

            s = stages("e1", "oh", "tr", "at", "h1", "g1", "h2", "g2", "w", "wac", "wr", "msg", "sum", "flush")
            s_rec = [sem(f"e1_rec{u}") for u in range(2)]
            s_gat = [sem(f"e1_gat{u}") for u in range(2)]
            cB = sem("e1_cB")
            PER = 5
            r_sb = rec["s"]
            fc1 = rows[0:8, 0:64]
            fc2 = rows[0:64, 64:128]
            fc3 = rows[0:64, 128:384]
            at = work[0:8, 0:512]
            h1 = work[0:64, 512:1024]
            h2 = work[0:64, 1024:1536]
            wac = work[:, 1536:2048].rearrange("p (q a n) -> p q a n", q=Q, a=2)
            wb = work[:, 2048:2304].rearrange("p (q n) -> p q n", q=Q)
            dot = work[:, 2304:2560].rearrange("p (q n) -> p q n", q=Q)
            g3 = gat[:, 1, 2:4, :].rearrange("p a b -> p (a b)")[:, 0:768].rearrange("p (q d n) -> p q d n", q=Q, d=3)
            rows_y = [gat[:, 0, 2 * u:2 * u + 2, :].rearrange("p a (b c) -> p (a b) c", c=D) for u in range(2)]
            msg = [big[:, u * 2048:(u + 1) * 2048].rearrange("p (q c h n) -> p q c h n", q=Q, c=4, h=2)
                   for u in range(2)]
            psW = ps[:, 3:5, :].rearrange("p b c -> p (b c)").rearrange("p (q k n) -> p q k n", q=Q, k=4)
            psDeg = [ps[:, 2, 0:1], ps[:, 7, 0:1]]
            acc = acc_raw[:, :, 0:2 * D]

            def sync_a(e, m):
                i = e.snap(m.index())
                e.wait_ge(s["msg"], m.done(2))
                e.sem_inc(S("s_sp"), 1)
                e.wait_ge(s_gat[m.u], m.turns(64, 1))
                e.sem_inc(S("s_sp"), 1)
                r = recs["s"].rearrange("(m p q) w -> m p (q w)", p=P, q=Q)
                e.dma_start(r_sb[:, m.u, :, :].rearrange("p q w -> p (q w)"),
                            r[bass.ds(i, 1)].rearrange("a p c -> p (a c)")).then_inc(s_rec[m.u], 16)

            def sync(e):
                for dst_ap, name in ((fc1, "fc_w1"), (fc2, "fc_w2"), (fc3, "fc_w3")):
                    e.dma_start(dst_ap, io[f"L1_gnn_{name}"]).then_inc(S("e1_fc"), 16)
                macro_loops(sync_a)(e)

            def pool_a(e, m):
                e.wait_ge(s_rec[m.u], m.turns(16))
                e.sem_inc(S("s_gp"), 1)
                e.wait_ge(s["msg"], m.done(2))
                e.sem_inc(S("s_gp"), 1)
                for q in range(Q):
                    e.indirect_dma_start(
                        out=rows_y[m.u][:, q, :], out_offset=None, in_=y1,
                        in_offset=bass.IndirectOffsetOnAxis(ap=r_sb[:, m.u, q, 0:1].bitcast(I32), axis=0),
                    ).then_inc(s_gat[m.u], 16)

            def pe_b(e, m):
                e.wait_ge(s["oh"], m.done())
                e.wait_ge(s["msg"], m.done())
                e.wait_ge(s["flush"], m.done(2))
                for q in range(Q):
                    T.matmul(psDeg[m.u], oh[:, m.u, q, :], ones[:, 0:1], start=(q == 0), stop=(q == Q - 1))
                for q in range(Q):
                    last = T.matmul(ps[:, 5 + m.u, :], oh[:, m.u, q, :],
                                    msg[m.u][:, q].rearrange("p c h n -> p (c h n)"),
                                    start=(q == 0), stop=(q == Q - 1))
                last.then_inc(s["sum"], 1)

            def pe_tr(e, m):
                e.wait_ge(s_rec[m.u], m.turns(16))
                e.wait_ge(s["at"], m.done(1))
                for q in range(Q):
                    last = T.transpose(ps[0:8, 0, q * P:(q + 1) * P], r_sb[:, m.u, q, 6:14], ident[:, :])
                last.then_inc(s["tr"], 1)
                e.wait_ge(s["at"], m.done())
                e.wait_ge(s["g1"], m.done(1))
                T.matmul(ps[0:64, 1, :], fc1, at, start=True, stop=True).then_inc(s["h1"], 1)

            def pe_mlp(e, m):
                e.wait_ge(s["g1"], m.done())
                e.wait_ge(s["tr"], m.done())
                e.wait_ge(s["g2"], m.done(1))
                e.sem_inc(S("s_pe"), 1)
                T.matmul(ps[0:64, 0, :], fc2, h1, start=True, stop=True).then_inc(s["h2"], 1)
                e.wait_ge(s["g2"], m.done())
                e.wait_ge(s["wr"], m.done(1))
                for q in range(Q):
                    last = T.matmul(psW[:, q].rearrange("p k n -> p (k n)"), h2[:, q * P:(q + 1) * P], fc3,
                                    start=True, stop=True)
                last.then_inc(s["w"], 1)

            def tensor(e):
                e.wait_ge(S("e1_fc"), 48)
                e.wait_ge(S("e1_go"), 1)
                pe_tr(e, Macro(0, 0))
                pe_mlp(e, Macro(0, 0))
                with e.Fori(0, NM // 2) as i:
                    for u in range(2):
                        pe_tr(e, Macro(i, u + 1))
                        pe_b(e, Macro(i, u))
                        pe_mlp(e, Macro(i, u + 1))

            def act(e, m):
                e.wait_ge(s["tr"], m.done())
                e.wait_ge(s["h1"], m.done(1))
                A.activation(at, ps[0:8, 0, :], ACT.Copy).then_inc(s["at"], 1)
                e.wait_ge(s["h1"], m.done())
                e.wait_ge(s["h2"], m.done(1))
                A.activation(h1, ps[0:64, 1, :], ACT.Silu, scale=8.0 ** -0.5).then_inc(s["g1"], 1)
                e.wait_ge(s["h2"], m.done())
                e.wait_ge(s["w"], m.done(1))
                A.activation(h2, ps[0:64, 0, :], ACT.Silu, scale=MUL ** -0.5).then_inc(s["g2"], 1)
                e.wait_ge(s["w"], m.done())
                e.wait_ge(s["wr"], m.done(1))
                for q in range(Q):
                    last = A.activation(wac[:, q], psW[:, q, 0:3:2, :], ACT.Copy, scale=r_sb[:, m.u, q, 2:3])
                last.then_inc(s["wac"], 1)

            def dve_a(e, m):
                e.wait_ge(s_rec[m.u], m.turns(16))
                e.wait_ge(s["sum"], m.done(2))
                V.tensor_tensor(oh[:, m.u, :, :], iota4, bcast(r_sb[:, m.u, :, 1], 2, [P, Q, P]), ALU.is_equal)\
                    .then_inc(s["oh"], 1)

            seen = set()

            def dve_b(e, m):
                c = Chain(e, cB)
                c.n = PER * m.off
                c.enter(m.i, 2 * PER)
                n0 = c.n
                y = rows_y[m.u]
                yv = y[:, :, MUL:4 * MUL].rearrange("p q (d n) -> p q d n", d=3)
                shd = r_sb[:, m.u, :, 3:6]
                shb = bcast(shd, 3, [P, Q, 3, MUL])
                o = msg[m.u]
                e.wait_ge(s_gat[m.u], m.turns(64))
                c(V.tensor_tensor(g3, yv, shb, ALU.mult))
                c.wait()
                c(V.tensor_tensor(dot, g3[:, :, 0, :], g3[:, :, 1, :], ALU.add))
                c.wait()
                c(V.tensor_tensor(dot, dot, g3[:, :, 2, :], ALU.add))
                e.wait_ge(s["sum"], m.done(2))
                e.wait_ge(s["wac"], m.done())
                c(V.tensor_tensor(wb, psW[:, :, 1, :], y[:, :, 0:MUL], ALU.mult))
                c.wait()
                V.tensor_tensor(o[:, :, 0, 1, :], psW[:, :, 3, :], dot, ALU.mult)
                V.tensor_tensor(o[:, :, 0, 0, :], wac[:, :, 0, :], y[:, :, 0:MUL], ALU.mult)
                V.tensor_tensor(o[:, :, 1:4, 1, :], bcast(wac[:, :, 1, :], 2, [P, Q, 3, MUL]), yv, ALU.mult)\
                    .then_inc(s["wr"], 1)
                V.tensor_tensor(o[:, :, 1:4, 0, :], bcast(wb, 2, [P, Q, 3, MUL]), shb, ALU.mult)\
                    .then_inc(s["msg"], 1)
                j = e.value_load(jmap["s"][0:1, bass.ds(m.index(), 1)], min_val=0, max_val=NB - 1)
                e.wait_ge(s["flush"], m.done(1))
                e.wait_ge(s["sum"], m.done())
                c(V.tensor_tensor(deg[:, bass.ds(j, 1)], deg[:, bass.ds(j, 1)], psDeg[m.u], ALU.add))
                c.wait()
                aj = acc[:, bass.ds(j, 1), :]
                V.tensor_tensor(aj, aj, ps[:, 5 + m.u, :], ALU.add).then_inc(s["flush"], 1)
                seen.add(c.n - n0)

            def dve(e):
                c = vchain(e)
                c(V.memset(acc, 0.0))
                c(V.memset(deg[:, :], 0.0))
                c.wait()
                e.sem_inc(S("e1_go"), 1)
                macro_loops(dve_a, dve_b)(e)
                assert seen == {PER}, (seen, PER)

            phase(sync=sync, gpsimd=macro_loops(pool_a), scalar=macro_loops(act), tensor=tensor, vector=dve)

            w2 = wts[:, 0:P].rearrange("p (k n) -> p k n", k=2)
            s_act = (sem("o1_go"), sem("o1_root"))

            def scale(e):
                c = vchain(e)
                c(V.tensor_scalar(deg[:, :], deg[:, :], 1.0, None, ALU.max))
                c.wait()
                e.sem_inc(s_act[0], 1)
                e.wait_ge(s_act[1], 1)
                c(V.reciprocal(small[:, 0:NB], deg[:, :]))
                c.wait()
                c(V.tensor_tensor(acc, acc, bcast(small[:, 0:NB], 2, [P, NB, 2 * D]), ALU.mult))
                c.wait()

            def root(e):
                e.wait_ge(s_act[0], 1)
                A.activation(deg[:, :], deg[:, :], ACT.Sqrt).then_inc(s_act[1], 1)

            phase(vector=scale, scalar=root)

            out_scale = (2 * MUL) ** -0.5 * MUL ** -0.5

            def w_adjust(e, c):
                c(V.tensor_scalar(w2[MUL:P, 0, :], w2[MUL:P, 0, :], INV_SQRT3, None, ALU.mult))

            def evac2(e, m, pp, st):
                t = qz[:, bass.ds(m.index(), 1), :]
                return V.scalar_tensor_tensor(t, pp[:, 0, 0:D], out_scale, t, ALU.mult, ALU.add)

            project("o1", 4, acc, [(w2[:, 0, :], io["L1_gnn_w2_s"]), (w2[:, 1, :], io["L1_gnn_w2_v"]),
                                   (rows[:, 0:MUL], row_bcast(io["L1_gnn_g_s"])),
                                   (rows[:, MUL:2 * MUL], row_bcast(io["L1_gnn_g_v"]))],
                    [(0, c * MUL, (c + 1) * MUL, [(c, w2[:, min(c, 1), :])]) for c in range(4)], evac2,
                    prep_ws=w_adjust)

            def rms(e, c, s_act):
                sq = junk
                st_, tmp_ = small[:, 128:128 + 2 * NB], small[:, 192:192 + 2 * NB]
                c(V.tensor_tensor(sq, qz[:, :, :], qz[:, :, :], ALU.mult))
                c.wait()
                c(V.tensor_reduce(st_[:, 0:NB], sq[:, :, 0:MUL], AX.X, ALU.add))
                c(V.tensor_reduce(st_[:, NB:2 * NB], sq[:, :, MUL:D], AX.X, ALU.add))
                c.wait()
                c(V.tensor_scalar(st_[:, NB:2 * NB], st_[:, NB:2 * NB], 1.0 / 3.0, None, ALU.mult))
                c.wait()
                rstd(e, c, s_act, 1, st_, 1.0 / MUL, tmp_)
                zs = qz[:, :, 0:MUL]
                zv = qz[:, :, MUL:D]
                c(V.tensor_tensor(zs, zs, bcast(st_[:, 0:NB], 2, [P, NB, MUL]), ALU.mult))
                c(V.tensor_tensor(zv, zv, bcast(st_[:, NB:2 * NB], 2, [P, NB, 3 * MUL]), ALU.mult))
                c.wait()
                c(V.tensor_tensor(zs, zs, bcast(rows[:, 0:MUL], 1, [P, NB, MUL]), ALU.mult))
                for d in range(3):
                    zd = qz[:, :, (d + 1) * MUL:(d + 2) * MUL]
                    c(V.tensor_tensor(zd, zd, bcast(rows[:, MUL:2 * MUL], 1, [P, NB, MUL]), ALU.mult))
                c.wait()
                xs_ = x_sb[:, :, 0:MUL]
                c(V.tensor_tensor(xs_, xs_, zs, ALU.add))
                for d in range(3):
                    xd = x_sb[:, :, MUL + d::3]
                    c(V.tensor_tensor(xd, xd, qz[:, :, (d + 1) * MUL:(d + 2) * MUL], ALU.add))
                c.wait()
                return 1

            v1_, a1_ = layernorm("l1", before=rms, roots=[small[:, 192:192 + 2 * NB]])
            phase(vector=v1_, scalar=a1_)

        layer1()

        def softmax_by_node(e, c):
            den = acc4[:, :, :, DH]
            c(V.tensor_scalar(den, den, 1e-30, None, ALU.max))
            c.wait()
            c(V.reciprocal(big[:, 0:NB * H].rearrange("p (j h) -> p j h", h=H), den))
            c.wait()
            rden = big[:, 0:NB * H].rearrange("p (j h) -> p j h", h=H)
            for h in range(H):
                c(V.tensor_tensor(qz4[:, :, h, :], acc4[:, :, h, 0:DH], bcast(rden[:, :, h], 2, [P, NB, DH]),
                                  ALU.mult))
            c.wait()

        def layer2():
            qkv("p2", 2, kv2)
            attention(2, "s", kv2)
            out_proj("o2", 2, prepare=softmax_by_node)
            v, a = layernorm("l2")
            phase(vector=v, scalar=a)

        def layer3():
            s = stages("e3", "oh", "pv", "sum", "flush")
            s_rec = [sem(f"e3_rec{u}") for u in range(2)]
            s_gat = [sem(f"e3_gat{u}") for u in range(2)]
            r_sb = rec["d"]
            acc = acc_raw[:, :, 0:D]
            r = recs["d"].rearrange("(m p q) w -> m p (q w)", p=P, q=Q)

            def sync_a(e, m):
                i = e.snap(m.index())
                e.wait_ge(s["oh"], m.done(2))
                e.sem_inc(S("s_sp"), 1)
                e.wait_ge(s_gat[m.u], m.turns(64, 1))
                e.sem_inc(S("s_sp"), 1)
                e.dma_start(r_sb[:, m.u, :, :].rearrange("p q w -> p (q w)"),
                            r[bass.ds(i, 1)].rearrange("a p c -> p (a c)")).then_inc(s_rec[m.u], 16)

            def sync(e):
                e.dma_start(x3.rearrange("(j p) c -> p j c", p=P), x_sb[:, :, :]).then_inc(S("e3_x"), 16)
                e.wait_ge(S("e3_x"), 16)
                macro_loops(sync_a)(e)

            def pool_a(e, m):
                e.wait_ge(s_rec[m.u], m.turns(16))
                e.sem_inc(S("s_gp"), 1)
                e.wait_ge(s["sum"], m.done(2))
                e.sem_inc(S("s_gp"), 1)
                for q in range(Q):
                    e.indirect_dma_start(
                        out=gat[:, m.u, q, 0:D], out_offset=None, in_=x3,
                        in_offset=bass.IndirectOffsetOnAxis(ap=r_sb[:, m.u, q, 0:1].bitcast(I32), axis=0),
                    ).then_inc(s_gat[m.u], 16)

            def pool(e):
                e.wait_ge(S("e3_x"), 16)
                macro_loops(pool_a)(e)

            def pe(e, m):
                e.wait_ge(s["oh"], m.done())
                e.wait_ge(s_gat[m.u], m.turns(64))
                e.wait_ge(s["flush"], m.done(2))
                for q in range(Q):
                    last = T.matmul(ps[:, 5 + m.u, 0:D], oh[:, m.u, q, :], gat[:, m.u, q, 0:D],
                                    start=(q == 0), stop=(q == Q - 1))
                last.then_inc(s["sum"], 1)

            def tensor(e):
                with e.Fori(0, NM // 2) as i:
                    for u in range(2):
                        pe(e, Macro(i, u))

            def dve_a(e, m):
                e.wait_ge(s_rec[m.u], m.turns(16))
                e.wait_ge(s["sum"], m.done(2))
                for q in range(Q):
                    last = V.tensor_scalar(oh[:, m.u, q, :], iota[:, :], r_sb[:, m.u, q, 1:2],
                                           r_sb[:, m.u, q, 2:3], ALU.is_equal, ALU.mult)
                last.then_inc(s["oh"], 1)

            def dve_b(e, m):
                j = e.value_load(jmap["d"][0:1, bass.ds(m.index(), 1)], min_val=0, max_val=NB - 1)
                e.wait_ge(s["flush"], m.done(1))
                e.wait_ge(s["sum"], m.done())
                aj = acc[:, bass.ds(j, 1), :]
                V.tensor_tensor(aj, aj, ps[:, 5 + m.u, 0:D], ALU.add).then_inc(s["flush"], 1)

            def dve(e):
                V.memset(acc, 0.0).then_inc(S("e3_z"), 1)
                e.wait_ge(S("e3_z"), 1)
                macro_loops(dve_a, dve_b)(e)

            phase(sync=sync, gpsimd=pool, tensor=tensor, vector=dve)

            wide = acc_raw[:, :, 0:2 * D]
            w4 = wts[:, 0:4 * D].rearrange("p (c n) -> p c n", c=4)

            def inputs_(e, c):
                nb = wide[:, :, 0:D]
                c(V.tensor_tensor(qz[:, :, :], nb, x_sb[:, :, :], ALU.mult))
                c(V.tensor_copy(wide[:, :, D:2 * D], x_sb[:, :, :]))
                c.wait()
                c(V.tensor_tensor(nb, nb, qz[:, :, :], ALU.add))
                c.wait()

            def bias(e, c):
                c(V.tensor_tensor(rows[:, 0:D], rows[:, 0:D], rows[:, D:2 * D], ALU.add))

            def evac(e, m, pp, st):
                return V.tensor_tensor(qz[:, bass.ds(m.index(), 1), :], pp[:, 0, 0:D], rows[:, 0:D], ALU.add)

            project("o3", 4, wide, [(w4[:, 0:2, :], halves(io["L3_gnn_W2"])), (w4[:, 2:4, :], halves(io["L3_gnn_W1"])),
                                    (rows[:, 0:D], row_bcast(io["L3_gnn_b1"])),
                                    (rows[:, D:2 * D], row_bcast(io["L3_gnn_b2"]))],
                    [(0, 0, D, [(c, w4[:, c, :]) for c in range(4)])], evac, prepare=inputs_, prep_ws=bias)

            def normalize(e, c, s_act):
                z = qz[:, :, :]
                n2 = small[:, 128:128 + NB]
                c(V.scalar_tensor_tensor(z, z, 0.2, z, ALU.mult, ALU.max))
                c.wait()
                c(V.tensor_tensor(junk, z, z, ALU.mult))
                c.wait()
                c(V.tensor_reduce(n2, junk, AX.X, ALU.add))
                c.wait()
                e.sem_inc(s_act[0], 1)
                e.wait_ge(s_act[1], 1)
                c(V.tensor_scalar(n2, n2, 1e-12, None, ALU.max))
                c.wait()
                c(V.reciprocal(n2, n2))
                c.wait()
                c(V.tensor_tensor(z, z, bcast(n2, 2, [P, NB, D]), ALU.mult))
                c.wait()
                c(V.tensor_tensor(x_sb[:, :, :], x_sb[:, :, :], z, ALU.add))
                c.wait()
                return 1

            v, a = layernorm("l3", before=normalize, roots=[small[:, 128:128 + NB]])
            phase(vector=v, scalar=a)

            def store(e):
                e.dma_start(out[0:(NT - 1) * P, :].rearrange("(j p) d -> p j d", p=P), x_sb[:, 0:NT - 1, :])\
                    .then_inc(S("s_out"), 16)
                e.dma_start(out[(NT - 1) * P:N_NODES, :], x_sb[0:LAST, NT - 1, :]).then_inc(S("s_out"), 16)
                e.wait_ge(S("s_out"), 32)

            phase(sync=store)

        layer2()
        layer3()

        block = ctx.enter_context(nc.Block())

        def run(e, todo):
            for fn, meet in todo:
                if fn:
                    fn(e)
                e.drain().then_inc(s_bar, 1)
                e.wait_ge(s_bar, meet)

        @block.sync
        def _(e):
            for counter, start in credits:
                e.sem_inc(counter, start)
            run(e, programs["sync"])

        @block.gpsimd
        def _(e):
            run(e, programs["gpsimd"])

        @block.scalar
        def _(e):
            run(e, programs["scalar"])

        @block.vector
        def _(e):
            run(e, programs["vector"])

        @block.tensor
        def _(e):
            run(e, programs["tensor"])


def layout(inputs):
    def pad(a, fill):
        a = np.asarray(a)
        out = np.full((E_PAD,) + a.shape[1:], fill, a.dtype)
        out[:N_EDGES] = a
        return out.reshape((P, EC) + a.shape[1:])

    src, dst = inputs["src"], inputs["dst"]
    ins = {
        "x": inputs["x"],
        "dst_key": pad(dst, PAD_KEY), "src_idx": pad(src, 0),
        "src_key": pad(src, PAD_KEY), "dst_idx": pad(dst, 0),
        "edge_weight": pad(inputs["edge_weight"], 0),
        "edge_attr_4": pad(inputs["edge_attr_4"], 0),
        "edge_attr_8": pad(inputs["edge_attr_8"], 0),
        "node_vec": np.pad(np.asarray(inputs["node_vec"]), (0, NB * P - N_NODES)).reshape(NB, P).T,
    }
    for name, a in inputs.items():
        if name[:2] in ("L0", "L1", "L2", "L3"):
            ins[name] = np.asarray(a)
    for name in ("L3_gnn_W1", "L3_gnn_W2"):
        ins[name] = np.ascontiguousarray(ins[name].T)
    return {k: np.ascontiguousarray(a) for k, a in ins.items()}


def kernel(**inputs):
    import concourse.bacc as bacc
    from concourse.bass_utils import run_bass_kernel_spmd

    nc = bacc.Bacc("TRN2", target_bir_lowering=False, num_devices=1)
    arrays = {f"in_{name}": a for name, a in layout(inputs).items()}
    io = {name[3:]: nc.dram_tensor(name, a.shape, mybir.dt.from_np(a.dtype), kind="ExternalInput").ap()
          for name, a in arrays.items()}
    out = nc.dram_tensor("out", (N_NODES, D), F32, kind="ExternalOutput").ap()
    gnn_kernel(nc, io, out)
    return run_bass_kernel_spmd(nc, [arrays], core_ids=[0]).results[0]["out"]
```

```python
from contextlib import ExitStack

import numpy as np
import concourse.bass as bass
from concourse import mybir

F32 = mybir.dt.float32
I32 = mybir.dt.int32
BF16 = mybir.dt.bfloat16
ALU = mybir.AluOpType
ACT = mybir.ActivationFunctionType
AX = mybir.AxisListType

P = 128
N_NODES = 3125
N_EDGES = 100000
D = 256
H = 8
DH = D // H
HC = DH + 1
AC = H * HC
MUL = 64
EC = 784
E_PAD = P * EC
NT = (N_NODES + P - 1) // P
LAST = N_NODES - (NT - 1) * P
NB = NT + 1
PAD_KEY = NB * P - 1
Q = 4
ME = Q * P
NM = (E_PAD + NB * (ME - 1)) // ME
U = 4
NM += -NM % U
NMA = NM + 3
NEG = -1.0e30
LN_EPS = 1e-5
CREDIT = U


class Macro:

    def __init__(self, i, off, before=0, per=U):
        self.i, self.off, self.before, self.per = i, off, before, per
        self.u, self.v = off % per, off % 2

    def done(self, lag=0):
        return self.i * self.per + (self.off + 1 + CREDIT - lag + self.before)

    def turns(self, n, lag=0):
        return self.i * n + ((self.off // self.per + 1 - lag) * n + self.before // self.per * n)

    def index(self):
        return self.i * self.per + self.off


class Chain:

    def __init__(self, engine, sem):
        self.e, self.sem, self.n, self.i, self.per, self.at = engine, sem, 0, 0, 0, 0

    def __call__(self, ins):
        ins.then_inc(self.sem, 1)
        self.n += 1
        return self.n

    def wait(self, n=None):
        self.e.wait_ge(self.sem, self.i * self.per + (self.n if n is None else n))

    def enter(self, i, per):
        self.i, self.per, self.at = i, per, self.n

    def leave(self, times):
        assert self.n - self.at == self.per, (self.n - self.at, self.per)
        self.n = self.at + self.per * times
        self.i = self.per = 0


def bcast(ap, axis, shape):
    return ap.unsqueeze(axis).to_broadcast(shape)


def gnn_kernel(nc, io, out):
    ctx = ExitStack()
    with ctx:
        def sb(name, shape, dt=F32):
            return ctx.enter_context(nc.sbuf_tensor(name, shape, dt))

        def sem(name):
            return ctx.enter_context(nc.semaphore(name))

        def dram(name, shape, dt=F32):
            return nc.dram_tensor(name, shape, dt, kind="Internal").ap()

        WD, WS = 4, 16
        recs = {"d": dram("rec_d", [NMA * ME, WD]), "s": dram("rec_s", [NMA * ME, WS])}
        kv0 = dram("kv0", [NB * P, 2 * D])
        y1 = dram("y1", [NB * P, D])
        kv2 = dram("kv2", [NB * P, 2 * D])
        x3 = dram("x3", [NB * P, D])

        iota = sb("iota", [P, P])
        iota26 = sb("iota26", [P, NB])
        pcol = sb("pcol", [P, 1])
        ident = sb("ident", [P, P])
        ones = sb("ones", [P, P])
        tri = sb("tri", [P, P])
        x_sb = sb("x_sb", [P, NB, D])
        qz = sb("qz", [P, NB, D])
        acc_raw = sb("acc", [P, NB, 2 * D + 2])
        m_run = sb("m_run", [P, NB, H])
        jmap = {"d": sb("jmap_d", [1, NMA], I32), "s": sb("jmap_s", [1, NMA], I32)}
        deg = sb("deg", [P, NB])
        rec = {"d": sb("rec_sb_d", [P, U, Q, WD]), "s": sb("rec_sb_s", [P, U, Q, WS])}
        gat = sb("gat", [P, U, Q, 2 * D])
        oh = sb("oh", [P, U, Q, P])
        big = sb("big", [P, 4 * Q * D])
        small = sb("small", [P, 640])
        wts = sb("wts", [P, 3 * 2 * D])
        rows = sb("rows", [P, 3 * D])
        xs = sb("xs", [P, 2, 2 * D])
        xt = sb("xt", [P, 2, 2 * D])
        stage = sb("stage", [P, 2, 2 * D])

        ps = ctx.enter_context(nc.psum_tensor("ps", [P, 8, 512], F32))

        sems = {}
        credits = []

        def S(name):
            if name not in sems:
                sems[name] = sem(name)
            return sems[name]

        T = nc.tensor
        V = nc.vector
        A = nc.scalar
        G = nc.gpsimd

        s_bar = sem("s_bar")
        the_vchain = Chain(None, S("c_vector"))

        def vchain(e):
            the_vchain.e = e
            return the_vchain

        bars = [0]
        programs = {k: [] for k in ("sync", "gpsimd", "scalar", "vector", "tensor")}

        def phase(**fns):
            bars[0] += 1
            meet = 5 * bars[0]
            for name, todo in programs.items():
                todo.append((fns.get(name), meet))

        ai = acc_raw[:, :, :].rearrange("p a b -> p (a b)")
        FREE = {"at": 0}

        def scratch(cols, dt=F32, shape=None):
            at = FREE["at"]
            FREE["at"] += cols
            assert FREE["at"] <= NB * (2 * D + 2), FREE["at"]
            v = ai[:, at:at + cols]
            return v if dt == F32 else v.bitcast(dt)

        key_i = scratch(EC, I32)
        tmp_i = scratch(EC, I32)
        bkt = scratch(EC)
        rel = scratch(EC)
        idx_i = scratch(EC, I32)
        mask = qz[:, :, :].rearrange("p a b -> p (a b)")[:, 0:EC]
        scan = qz[:, :, :].rearrange("p a b -> p (a b)")[:, EC:2 * EC]
        pos = qz[:, :, :].rearrange("p a b -> p (a b)")[:, 2 * EC:3 * EC]
        zero = qz[:, :, :].rearrange("p a b -> p (a b)")[:, 3 * EC:4 * EC]
        pos_i = qz[:, :, :].rearrange("p a b -> p (a b)")[:, 4 * EC:5 * EC].bitcast(I32)
        attr = scratch(12 * EC)
        cnt = small[:, 0:NB]
        tot = small[:, 32:32 + NB]
        tot_i = small[:, 64:64 + NB].bitcast(I32)
        mac = small[:, 96:96 + NB]
        inc = small[:, 128:128 + NB]
        offs = small[:, 160:160 + NB]
        zero26 = small[:, 192:192 + NB]
        ring = wts[:, 0:2 * 8 * WS]
        pring = rows[:, 0:16].bitcast(I32)
        RH = 8
        jcmp = big[0:1, :]

        def consts_vector(e):
            c = vchain(e)
            c(V.memset(zero, 0.0))
            c(V.memset(x_sb[:, NT - 1:NB, :], 0.0))
            c(V.memset(zero26, 0.0))
            c(V.memset(ones[:, :], 1.0))
            e.wait_ge(S("s_iota"), 4)
            c(V.tensor_scalar(ident[:, :], iota[:, :], pcol[:, 0:1], None, ALU.is_equal))
            c(V.tensor_scalar(tri[:, :], iota[:, :], pcol[:, 0:1], None, ALU.is_gt))
            fill = gat[:, :, :, :].rearrange("p a b c -> p (a b c)")
            c(V.memset(fill[:, 0:FR * WS], 0.0))
            c.wait()
            for w, part in ((WD, fill[:, 0:FR * WD]), (WS, fill[:, 0:FR * WS])):
                v = part.rearrange("p (r w) -> p r w", w=w)
                e.wait_ge(S("s_fill"), 0 if w == WD else 16 * (NMA * ME // P // FR))
                c(V.memset(part, 0.0))
                c.wait()
                if w == WD:
                    c(V.memset(v[:, :, 3:4], NEG))
                V.memset(v[:, :, 1:2], -1.0).then_inc(S("s_fillv"), 1)
                e.wait_ge(S("s_fillv"), 1 if w == WD else 2)

        FR = NMA
        assert (NMA * ME // P) % FR == 0

        def consts_sync(e):
            x_in = io["x"]
            e.wait_ge(S("c_vector"), 2)
            e.dma_start(x_sb[:, 0:NT - 1, :],
                        x_in[0:(NT - 1) * P, :].rearrange("(j p) d -> p j d", p=P)).then_inc(S("s_x"), 16)
            e.dma_start(x_sb[0:LAST, NT - 1, :], x_in[(NT - 1) * P:N_NODES, :]).then_inc(S("s_x"), 16)
            fill = gat[:, :, :, :].rearrange("p a b c -> p (a b c)")
            n = 0
            for w, k in ((WD, "d"), (WS, "s")):
                e.wait_ge(S("s_fillv"), 1 if w == WD else 2)
                r = recs[k].rearrange("(c p r) w -> c p (r w)", p=P, r=FR)
                for b in range(NMA * ME // P // FR):
                    e.dma_start(r[b], fill[:, 0:FR * w]).then_inc(S("s_fill"), 16)
                    n += 16
            e.wait_ge(S("s_fill"), n)
            e.wait_ge(S("s_x"), 32)

        def consts_gpsimd(e):
            G.iota(iota[:, :], [[1, P]], base=0, channel_multiplier=0,
                   allow_small_or_imprecise_dtypes=True).then_inc(S("s_iota"), 1)
            G.iota(iota26[:, :], [[1, NB]], base=0, channel_multiplier=0,
                   allow_small_or_imprecise_dtypes=True).then_inc(S("s_iota"), 1)
            G.iota(pcol[:, :], [[1, 1]], base=0, channel_multiplier=1,
                   allow_small_or_imprecise_dtypes=True).then_inc(S("s_iota"), 1)
            G.iota(jcmp[:, 0:NMA], [[1, NMA]], base=0, channel_multiplier=0,
                   allow_small_or_imprecise_dtypes=True).then_inc(S("s_iota"), 1)

        phase(sync=consts_sync, vector=consts_vector, gpsimd=consts_gpsimd)

        def sort(k):
            W = {"d": WD, "s": WS}[k]
            key_in, idx_in = (io["dst_key"], io["src_idx"]) if k == "d" else (io["src_key"], io["dst_idx"])
            if k == "d":
                ew = attr[:, 0:EC]
                parts = [(0, 1, idx_i), (1, 1, rel), (2, 1, ew)]
            else:
                a4 = attr[:, 0:4 * EC].rearrange("p (t w) -> p t w", w=4)
                a8 = attr[:, 4 * EC:12 * EC].rearrange("p (t w) -> p t w", w=8)
                parts = [(0, 1, idx_i), (1, 1, rel), (2, 4, a4), (6, 8, a8)]
            n_in = 3 if k == "d" else 4
            s_in = S(f"s_in_{k}")

            def load(e):
                e.dma_start(key_i, key_in).then_inc(s_in, 16)
                e.dma_start(idx_i, idx_in).then_inc(s_in, 16)
                if k == "d":
                    e.dma_start(ew, io["edge_weight"]).then_inc(s_in, 16)
                else:
                    e.dma_start(a4, io["edge_attr_4"]).then_inc(s_in, 16)
                    e.dma_start(a8, io["edge_attr_8"]).then_inc(s_in, 16)

            def place(e):
                c = vchain(e)
                e.wait_ge(s_in, 16 * n_in)
                c(V.tensor_scalar(tmp_i, key_i, 7, None, ALU.arith_shift_right))
                c.wait()
                c(V.tensor_copy(bkt, tmp_i))
                c.wait()
                c(V.tensor_scalar(tmp_i, key_i, P - 1, None, ALU.bitwise_and))
                c.wait()
                c(V.tensor_copy(rel, tmp_i))
                c(V.memset(pos, 0.0))
                with e.Fori(0, NB) as b:
                    c.enter(b, 2)
                    c.wait()
                    c(V.tensor_scalar(mask, bkt, iota26[:, bass.ds(b, 1)], None, ALU.is_equal))
                    c.wait()
                    c(V.tensor_reduce(cnt[:, bass.ds(b, 1)], mask, AX.X, ALU.add))
                c.leave(NB)
                c.wait()
                e.drain().then_inc(S(f"s_cnt_{k}"), 1)
                e.wait_ge(S(f"s_tot_{k}"), 1)
                c(V.tensor_copy(tot, ps[:, 0, 0:NB]))
                c(V.tensor_copy(offs, ps[:, 1, 0:NB]))
                c.wait()
                c(V.tensor_scalar(tot_i, tot, float(ME - 1), None, ALU.add))
                c.wait()
                c(V.tensor_scalar(tot_i, tot_i, ME.bit_length() - 1, None, ALU.arith_shift_right))
                c.wait()
                c(V.tensor_copy(mac, tot_i))
                c.wait()
                c(V.tensor_tensor_scan(inc, mac, zero26, 0.0, ALU.add, ALU.add))
                c.wait()
                c(V.tensor_tensor(mac, inc, mac, ALU.subtract))
                c.wait()
                c(V.scalar_tensor_tensor(offs, mac, float(ME), offs, ALU.mult, ALU.add))
                c.wait()
                c(V.tensor_scalar(offs, offs, 1.0, None, ALU.subtract))
                jf = jcmp[:, NMA:2 * NMA]
                wide = oh_wide[:, 0:NMA * NB].rearrange("p (m b) -> p m b", b=NB)
                c(V.tensor_tensor(wide, bcast(jcmp[:, 0:NMA], 2, [1, NMA, NB]),
                                  bcast(inc[0:1, :], 1, [1, NMA, NB]), ALU.is_ge))
                c.wait()
                c(V.tensor_reduce(jf, wide, AX.X, ALU.add))
                c.wait()
                c(V.tensor_scalar(jmap[k][:, :], jf, float(NB - 1), None, ALU.min))
                with e.Fori(0, NB) as b:
                    c.enter(b, 4)
                    c.wait()
                    c(V.tensor_scalar(mask, bkt, iota26[:, bass.ds(b, 1)], None, ALU.is_equal))
                    c.wait()
                    c(V.tensor_tensor_scan(scan, mask, zero, offs[:, bass.ds(b, 1)], ALU.add, ALU.add))
                    c.wait()
                    c(V.tensor_tensor(scan, scan, mask, ALU.mult))
                    c.wait()
                    c(V.tensor_tensor(pos, pos, scan, ALU.add))
                c.leave(NB)
                c.wait()
                V.tensor_copy(pos_i, pos).then_inc(S(f"s_pos_{k}"), 1)

            def totals(e):
                e.wait_ge(S(f"s_cnt_{k}"), 1)
                T.matmul(ps[:, 0, 0:NB], ones[:, :], cnt, start=True, stop=True)
                T.matmul(ps[:, 1, 0:NB], tri[:, :], cnt, start=True, stop=True).then_inc(S(f"s_tot_{k}"), 1)

            slot_of = [S(f"s_put_{k}{h}") for h in range(2)]
            rr = ring[:, 0:2 * RH * W].rearrange("p (h t w) -> p h t w", h=2, t=RH)

            def fill_ring(e):
                c = Chain(e, S(f"c_ring_{k}"))
                c(A.activation(ring[:, 0:2 * RH * W], zero[:, 0:2 * RH * W], ACT.Copy))
                c.wait()
                e.wait_ge(S(f"s_pos_{k}"), 1)

                def turn(i, at_i):
                    for h in range(2):
                        if at_i is not None:
                            e.wait_ge(slot_of[h], at_i * (16 * RH) + 16 * RH)
                        at = i * (2 * RH) + h * RH
                        for w, n, col in parts:
                            o = rr[:, h, :, w:w + n]
                            s = col[:, bass.ds(at, RH)] if n == 1 else col[:, bass.ds(at, RH), :]
                            if n == 1:
                                o = rr[:, h, :, w]
                            if w == 0:
                                o = o.bitcast(I32)
                            A.activation(o, s, ACT.Copy).then_inc(S(f"s_ring_{k}"), 1)
                        A.activation(pring[:, h * RH:(h + 1) * RH], pos_i[:, bass.ds(at, RH)], ACT.Copy)\
                            .then_inc(S(f"s_ring_{k}"), 1)

                turn(0, None)
                with e.Fori(0, EC // (2 * RH) - 1) as i:
                    turn(i + 1, i)

            def scatter(e):
                per = len(parts) + 1
                with e.Fori(0, EC // (2 * RH)) as i:
                    for h in range(2):
                        e.wait_ge(S(f"s_ring_{k}"), i * (2 * per) + (h + 1) * per)
                        e.sem_inc(S("s_gp"), 1)
                        for t in range(RH):
                            e.indirect_dma_start(
                                out=recs[k], out_offset=bass.IndirectOffsetOnAxis(
                                    ap=pring[:, h * RH + t:h * RH + t + 1], axis=0),
                                in_=rr[:, h, t, :], in_offset=None).then_inc(slot_of[h], 16)
                for h in range(2):
                    e.wait_ge(slot_of[h], 16 * RH * (EC // (2 * RH)))
                    e.sem_inc(S("s_gp"), 1)

            phase(sync=load, vector=place, tensor=totals, scalar=fill_ring, gpsimd=scatter)

        oh_wide = gat[0:1, :, :, :].rearrange("p a b c -> p (a b c)")
        sort("d")
        sort("s")

        work = sb("work", [P, 3072])
        xs = work[:, 0:1024].rearrange("p (u c) -> p u c", u=2)
        xt = work[:, 1024:2048].rearrange("p (u c) -> p u c", u=2)
        stage = work[:, 2048:3072].rearrange("p (u c) -> p u c", u=2)

        def stages(tag, *names, credit=CREDIT):
            made = {}
            for n in names:
                made[n] = sem(f"{tag}_{n}")
                credits.append((made[n], credit))
            return made

        def row_bcast(src):
            return src.partition_broadcast(P)

        tile_sems = stages("tile", "copy", "turn", "xt", "mm", "evac")
        s_w = sem("tile_w")
        s_out = [sem(f"tile_out{u}") for u in range(2)]
        credits += [(one, 1) for one in s_out]
        s_ready = sem("tile_ready")
        rounds = {"all": 0, "out": 0, "loads": 0}

        def project(tag, n_chunks, zin, loads, groups, evac, out_dma=None, prepare=None, prep_ws=None):
            s, before = tile_sems, NB * rounds["all"]
            kept = NB * rounds["out"]
            rounds["all"] += 1
            rounds["out"] += out_dma is not None
            ready = rounds["all"]
            rounds["loads"] += 16 * len(loads)
            loaded = rounds["loads"]
            wide = n_chunks * P

            def load(e):
                for dst_ap, src_ap in loads:
                    e.dma_start(dst_ap, src_ap).then_inc(s_w, 16)
                if out_dma is not None:
                    with e.Fori(0, NB // 2) as i:
                        for u in range(2):
                            m = Macro(i, u, before, 2)
                            at = e.snap(m.index())
                            e.wait_ge(s["evac"], m.done())
                            e.sem_inc(S("s_sp"), 1)
                            out_dma(e, at, stage[:, u, :]).then_inc(s_out[u], 16)
                    for u in range(2):
                        e.wait_ge(s_out[u], 8 * (NB + kept) + 1)

            def copies(e):
                e.wait_ge(s_ready, ready)
                with e.Fori(0, NB // 2) as i:
                    for u in range(2):
                        m = Macro(i, u, before, 2)
                        e.wait_ge(s["turn"], m.done(2))
                        G.tensor_copy(xs[:, u, 0:wide], zin[:, bass.ds(m.index(), 1), 0:wide])\
                            .then_inc(s["copy"], 1)

            def tensor(e):
                e.wait_ge(s_w, loaded)
                e.wait_ge(s_ready, ready)
                with e.Fori(0, NB // 2) as i:
                    for u in range(2):
                        m = Macro(i, u, before, 2)
                        e.wait_ge(s["copy"], m.done())
                        e.wait_ge(s["xt"], m.done(2))
                        for c in range(n_chunks):
                            last = T.transpose(ps[:, u, c * P:(c + 1) * P], xs[:, u, c * P:(c + 1) * P],
                                               ident[:, :])
                        last.then_inc(s["turn"], 1)
                        e.wait_ge(s["xt"], m.done())
                        e.wait_ge(s["evac"], m.done(2))
                        for b, c0, c1, terms in groups:
                            for n, (c, w) in enumerate(terms):
                                last = T.matmul(ps[:, 2 + 2 * u + b, c0:c1], xt[:, u, c * P:(c + 1) * P], w,
                                                start=(n == 0), stop=(n == len(terms) - 1))
                        last.then_inc(s["mm"], 1)

            def scalar(e):
                with e.Fori(0, NB // 2) as i:
                    for u in range(2):
                        m = Macro(i, u, before, 2)
                        e.wait_ge(s["turn"], m.done())
                        e.wait_ge(s["mm"], m.done(2))
                        A.activation(xt[:, u, 0:wide], ps[:, u, 0:wide], ACT.Copy).then_inc(s["xt"], 1)

            def vector(e):
                c = vchain(e)
                if prepare:
                    prepare(e, c)
                e.wait_ge(s_w, loaded)
                if prep_ws:
                    prep_ws(e, c)
                c.wait()
                e.sem_inc(s_ready, 1)
                with e.Fori(0, NB // 2) as i:
                    for u in range(2):
                        m = Macro(i, u, before, 2)
                        e.wait_ge(s["mm"], m.done())
                        if out_dma is not None:
                            e.wait_ge(s_out[u], Macro(i, u, kept, 2).turns(16, 1) + 1)
                        evac(e, m, ps[:, 2 + 2 * u:4 + 2 * u, :], stage[:, u, :]).then_inc(s["evac"], 1)

            phase(sync=load, gpsimd=copies, tensor=tensor, scalar=scalar, vector=vector)

        def store_rows(table, width):
            def go(e, m, src):
                t = table.rearrange("(j p) c -> j p c", p=P)
                return e.dma_start(t[bass.ds(m, 1)].rearrange("a p c -> p (a c)"), src[:, 0:width])
            return go

        junk = acc_raw[:, :, 0:D]

        def rstd(e, c, s_act, n, stat, scale, tmp):
            c(V.tensor_scalar(tmp, stat, scale, LN_EPS, ALU.mult, ALU.add))
            c.wait()
            e.sem_inc(s_act[0], 1)
            e.wait_ge(s_act[1], n)
            c(V.reciprocal(stat, tmp))
            c.wait()

        def layernorm(tag, before=None, after=None, roots=()):
            s_act = (sem(f"{tag}_go"), sem(f"{tag}_root"))
            mean = small[:, 0:NB]
            var = small[:, 32:32 + NB]
            tmp = small[:, 64:64 + NB]
            todo = list(roots) + [tmp]

            def vector(e):
                c = vchain(e)
                n = 0
                if before:
                    n = before(e, c, s_act)
                x = x_sb[:, :, :]
                c(V.tensor_reduce(mean, x, AX.X, ALU.add))
                c.wait()
                c(V.tensor_scalar(mean, mean, 1.0 / D, None, ALU.mult))
                c.wait()
                c(V.tensor_tensor(x, x, bcast(mean, 2, [P, NB, D]), ALU.subtract))
                c.wait()
                c(V.tensor_tensor(junk, x, x, ALU.mult))
                c.wait()
                c(V.tensor_reduce(var, junk, AX.X, ALU.add))
                c.wait()
                rstd(e, c, s_act, n + 1, var, 1.0 / D, tmp)
                c(V.tensor_tensor(x, x, bcast(var, 2, [P, NB, D]), ALU.mult))
                c.wait()
                if after:
                    after(e, c)

            def scalar(e):
                for n, t in enumerate(todo):
                    e.wait_ge(s_act[0], n + 1)
                    A.activation(t, t, ACT.Sqrt).then_inc(s_act[1], 1)

            return vector, scalar

        def macro_loops(ahead, first, body, after=None):
            def go(e):
                for m in range(ahead):
                    first(e, Macro(0, m))
                with e.Fori(0, NM // U) as i:
                    for u in range(U):
                        body(e, lambda lag, i=i, u=u: Macro(i, u + lag))
                if after:
                    after(e)
            return go

        iota4 = bcast(iota[:, :], 1, [P, Q, P])

        def attention(L, k, table):
            timed = L == 0
            s = stages(f"a{L}", "oh", "tr", "oht", "qx", "prod", "ln", "mq", "mt", "dg", "mb",
                       "f", "ef", "p", "pv", "sum", "flush", "s3", "st", "me", "td", "sp")
            s_hm, s_hr = sem(f"a{L}_hm"), sem(f"a{L}_hr")
            credits.append((s_hr, 3))
            s_rec = [sem(f"a{L}_rec{u}") for u in range(U)]
            s_gat = [sem(f"a{L}_gat{u}") for u in range(U)]
            s_go = sem(f"a{L}_go")
            cB = sem(f"a{L}_cB")
            AHEAD = 3
            acc = acc_raw[:, :, 0:AC]
            r_sb = rec[k]
            oht = xs
            prod = big[:, 0:Q * D].rearrange("p (q c) -> p q c", q=Q)
            pvb = big[:, Q * D:Q * D + 2 * Q * AC].rearrange("p (u q c) -> p u q c", u=2, q=Q)
            col = lambda a, n: small[:, a:a + n]
            v4 = lambda a: a.rearrange("p (q h) -> p q h", q=Q)
            td, ab, sg, ln = (col(a, 4) for a in (0, 4, 8, 12))
            sc, t1, t2, sm = (col(a, 32) for a in (32, 64, 96, 128))
            mq, mn, dd, ff, mx = (col(a, 8) for a in (160, 168, 176, 184, 192))
            mr = small[0:H, 200:201]
            dg = small[0:H, 208:216]
            r1 = col(224, 32)
            s3 = small[:, 288:336].bitcast(BF16)
            st3 = small[:, 336:400].bitcast(BF16)
            nh = work[:, 2048:2304].bitcast(BF16)
            sel = small[:, 400:416].bitcast(BF16)
            bigI = work[:, 2304:2368].bitcast(BF16)
            identb = work[:, 2368:2432].bitcast(BF16)
            w0, w1, bt4 = rows[:, 0:8], rows[:, 8:16], rows[:, 16:48]
            bank7 = ps[:, 7, :]
            psQ = [ps[:, 1 + 2 * v * timed:3 + 2 * v * timed, :].rearrange("p b c -> p (b c)")
                   for v in range(2)]
            psO = [ps[:, 5 + v if timed else 3, 0:AC] for v in range(2)]
            times = [ps[:, 5 + v, AC:AC + Q] for v in range(2)]
            q_lag, o_lag = (2, 2) if timed else (1, 1)
            r = recs[k].rearrange("(m p q) w -> m p (q w)", p=P, q=Q)

            def sync_a(e, m):
                at = e.snap(m.index())
                e.wait_ge(s["mq" if timed else "prod"], m.done(U))
                e.sem_inc(S("s_sp"), 1)
                e.dma_start(r_sb[:, m.u, :, :].rearrange("p q w -> p (q w)"),
                            r[bass.ds(at, 1)].rearrange("a p c -> p (a c)")).then_inc(s_rec[m.u], 16)

            def sync(e):
                if timed:
                    wt = io["L0_gnn_Wt"]
                    e.dma_start(w0, row_bcast(wt[0])).then_inc(S("s_wt"), 16)
                    e.dma_start(w1, row_bcast(wt[1])).then_inc(S("s_wt"), 16)
                    for q in range(Q):
                        e.dma_start(bt4[:, q * H:(q + 1) * H], row_bcast(io["L0_gnn_bt"])).then_inc(S("s_wt"), 16)
                    e.dma_start(deg[:, :], io["node_vec"]).then_inc(S("s_wt"), 16)
                macro_loops(AHEAD, sync_a, lambda e, M: sync_a(e, M(AHEAD)))(e)

            def pool_a(e, m):
                e.wait_ge(s_rec[m.u], m.turns(16))
                e.sem_inc(S("s_gp"), 1)
                e.wait_ge(s["pv"], m.done(U))
                e.sem_inc(S("s_gp"), 1)
                for q in range(Q):
                    e.indirect_dma_start(
                        out=gat[:, m.u, q, :], out_offset=None, in_=table,
                        in_offset=bass.IndirectOffsetOnAxis(ap=r_sb[:, m.u, q, 0:1].bitcast(I32), axis=0),
                    ).then_inc(s_gat[m.u], 16)

            def transposes(e, m):
                e.wait_ge(s["oh"], m.done())
                e.wait_ge(s["oht"], m.done(1))
                for q in range(Q):
                    last = T.transpose(ps[:, 0, q * P:(q + 1) * P], oh[:, m.u, q, :], ident[:, :])
                last.then_inc(s["tr"], 1)

            def queries(e, m):
                j = e.value_load(jmap[k][0:1, bass.ds(m.index(), 1)], min_val=0, max_val=NB - 1)
                e.wait_ge(s["oht"], m.done())
                e.wait_ge(s["prod"], m.done(q_lag))
                if timed:
                    e.wait_ge(s["flush"], m.done(2))
                for q in range(Q):
                    o = oht[:, m.v, q * P:(q + 1) * P]
                    last = T.matmul(psQ[m.v][:, q * D:(q + 1) * D], o, qz[:, bass.ds(j, 1), :], start=True, stop=True)
                    if timed:
                        last = T.matmul(times[m.v][:, q:q + 1], o, deg[:, bass.ds(j, 1)],
                                        start=True, stop=True)
                last.then_inc(s["qx"], 1)

            def maxima(e, m):
                if timed:
                    e.wait_ge(s["mq"], m.done())
                    T.transpose(bank7[0:H, 16:16 + P], mq, ident[:, :]).then_inc(s["mt"], 1)
                    e.wait_ge(s["dg"], m.done())
                    T.matmul(bank7[:, 144:144 + H], ones[0:H, :], dg, start=True, stop=True).then_inc(s["mb"], 1)
                else:
                    e.wait_ge(s["s3"], m.done())
                    T.transpose(bank7[0:96, 192:256].bitcast(BF16), s3, identb).then_inc(s["st"], 1)
                    e.wait_ge(s["sp"], m.done())
                    for h in range(H):
                        e.wait_ge(s_hr, m.i * (U * H) + (m.off * H + h + 1))
                        node_scores(h, 4 + h % 3)
                    e.wait_ge(s["mq"], m.done())
                    for q in range(Q):
                        last = T.matmul(bank7[:, 152 + q * H:160 + q * H], oht[:, m.v, q * P:(q + 1) * P], mn,
                                        start=True, stop=True)
                    last.then_inc(s["me"], 1)

            def sums(e, m):
                e.wait_ge(s["p"], m.done())
                e.wait_ge(s["pv"], m.done())
                e.wait_ge(s["flush"], m.done(o_lag))
                for q in range(Q):
                    last = T.matmul(psO[m.v], oh[:, m.u, q, :], pvb[:, m.v, q, :], start=(q == 0), stop=(q == Q - 1))
                last.then_inc(s["sum"], 1)

            def node_scores(h, b):
                for q in range(Q):
                    c = q * H + h
                    T.matmul(ps[:, b, q * P:(q + 1) * P], sel[0:96, c:c + 1].to_broadcast([96, P]),
                             st3[0:96, :], start=(q == 0), stop=False)
                T.matmul(ps[:, b, :], bigI, nh, start=False, stop=True).then_inc(s_hm, 1)

            def tensor(e):
                e.wait_ge(s_go, 1)
                transposes(e, Macro(0, 0))
                queries(e, Macro(0, 0))
                transposes(e, Macro(0, 1))
                maxima(e, Macro(0, 0))
                queries(e, Macro(0, 1))
                transposes(e, Macro(0, 2))

                def turn(e, M):
                    sums(e, M(0))
                    maxima(e, M(1))
                    queries(e, M(2))
                    transposes(e, M(3))
                macro_loops(0, None, turn)(e)

            def evac(e, m):
                e.wait_ge(s["tr"], m.done())
                e.wait_ge(s["qx"] if timed else s["me"], m.done(2))
                A.activation(oht[:, m.v, :], ps[:, 0, :], ACT.Copy).then_inc(s["oht"], 1)

            def act(e, m):
                if timed:
                    e.wait_ge(s["td"], m.done())
                    A.activation(ln, ab, ACT.Ln, scale=1.0 / 3600.0, bias=1.0).then_inc(s["ln"], 1)
                else:
                    e.wait_ge(s["st"], m.done())
                    A.activation(st3[0:96, :], bank7[0:96, 192:256].bitcast(BF16), ACT.Copy).then_inc(s["sp"], 1)
                e.wait_ge(s["f"], m.done())
                e.wait_ge(s["sum"], m.done(2))
                A.activation(pvb[:, m.v, :, :].rearrange("p q (h c) -> p q h c", c=HC)[:, :, :, DH],
                             v4(sm), ACT.Exp).then_inc(s["p"], 1)
                A.activation(ff, dd, ACT.Exp).then_inc(s["ef"], 1)

            def scalar(e):
                e.wait_ge(s_go, 1)
                evac(e, Macro(0, 0))
                evac(e, Macro(0, 1))
                act(e, Macro(0, 0))
                evac(e, Macro(0, 2))
                macro_loops(0, None, lambda e, M: (act(e, M(1)), evac(e, M(3))))(e)

            def one_hot(e, m, q):
                if q == 0:
                    e.wait_ge(s_rec[m.u], m.turns(16))
                    e.wait_ge(s["sum"], m.done(U))
                ins = V.tensor_scalar(oh[:, m.u, q, :], iota[:, :], r_sb[:, m.u, q, 1:2], None, ALU.is_equal)
                if q == Q - 1:
                    ins.then_inc(s["oh"], 1)

            def bucket(e, m):
                return e.value_load(jmap[k][0:1, bass.ds(m.index(), 1)], min_val=0, max_val=NB - 1)

            def score_timed(c, e, a, z, nxt):
                jz = None
                if z:
                    jz = bucket(e, z)
                    weight_values(e, z)
                e.wait_ge(s["qx"], a.done())
                k_td = c(V.tensor_tensor(td, r_sb[:, a.u, :, 2], times[a.v], ALU.subtract))
                multiply(e, a)
                c.wait(k_td)
                k_sg = c(V.tensor_scalar(sg, td, 0.0, -1.0, ALU.is_gt, ALU.add))
                c.wait(k_sg)
                k_sg = c(V.scalar_tensor_tensor(sg, td, 0.0, sg, ALU.is_ge, ALU.add))
                c.wait(k_sg)
                V.tensor_tensor(ab, td, sg, ALU.mult).then_inc(s["td"], 1)
                k1 = c(V.tensor_tensor(v4(t1), bcast(sg, 2, [P, Q, H]), bcast(w0, 1, [P, Q, H]), ALU.mult))
                c.wait(k1)
                k1 = c(V.tensor_tensor(t1, t1, bt4, ALU.add))
                e.wait_ge(s["prod"], a.done())
                k_sc = c(V.tensor_reduce(sc, prod.rearrange("p q (h c) -> p (q h) c", c=DH), AX.X, ALU.add))
                e.wait_ge(s["ln"], a.done())
                k2 = c(V.tensor_tensor(v4(t2), bcast(ln, 2, [P, Q, H]), bcast(w1, 1, [P, Q, H]), ALU.mult))
                c.wait(k2)
                k1 = c(V.tensor_tensor(t1, t1, t2, ALU.add))
                if z:
                    k_fl = rescale(c, e, z, jz)
                c.wait(k1)
                k1 = c(V.tensor_tensor(v4(t1), v4(t1), bcast(r_sb[:, a.u, :, 3], 2, [P, Q, H]), ALU.add))
                c.wait(k1)
                k_sc = c(V.scalar_tensor_tensor(sc, sc, DH ** -0.5, t1, ALU.mult, ALU.add))
                c.wait(k_sc)
                V.tensor_reduce(mq, sc.rearrange("p (q h) -> p h q", q=Q), AX.X, ALU.max).then_inc(s["mq"], 1)
                if z:
                    add_sums(c, e, z, jz, k_fl)
                ja = bucket(e, a)
                one_hot(e, nxt, 0)
                e.wait_ge(s["mt"], a.done())
                k_mr = c(V.tensor_reduce(mr, bank7[0:H, 16:16 + P], AX.X, ALU.max))
                one_hot(e, nxt, 1)
                c.wait(k_mr)
                V.tensor_scalar(dg, ident[0:H, 0:H], mr, None, ALU.mult).then_inc(s["dg"], 1)
                one_hot(e, nxt, 2)
                mj = m_run[:, bass.ds(ja, 1), :]
                e.wait_ge(s["mb"], a.done())
                k_mn = c(V.tensor_tensor(mn, mj, bank7[:, 144:144 + H], ALU.max))
                one_hot(e, nxt, 3)
                c.wait(k_mn)
                c(V.tensor_tensor(v4(sm), v4(sc), bcast(mn, 1, [P, Q, H]), ALU.subtract))
                k_dd = c(V.tensor_tensor(dd, mj, mn, ALU.subtract))
                c.wait(k_dd)
                V.tensor_scalar(mj, mn, 1.0, None, ALU.mult).then_inc(s["f"], 1)

            def score_plain(c, e, a, z, nxt):
                jz = bucket(e, z) if z else None
                if z:
                    weight_values(e, z)
                e.wait_ge(s["qx"], a.done())
                multiply(e, a)
                c(V.tensor_scalar(nh, oht[:, a.v, :], -1.0, None, ALU.add))
                e.wait_ge(s["prod"], a.done())
                k_sc = c(V.tensor_reduce(sc, prod.rearrange("p q (h c) -> p (q h) c", c=DH), AX.X, ALU.add))
                if z:
                    k_fl = rescale(c, e, z, jz)
                c.wait(k_sc)
                k = c(V.tensor_copy(s3[:, 0:32], sc))
                one_hot(e, nxt, 0)
                c.wait(k)
                k = c(V.tensor_tensor(r1, sc, s3[:, 0:32], ALU.subtract))
                one_hot(e, nxt, 1)
                c.wait(k)
                k = c(V.tensor_copy(s3[:, 32:64], r1))
                one_hot(e, nxt, 2)
                c.wait(k)
                V.tensor_tensor(s3[:, 64:96], r1, s3[:, 32:64], ALU.subtract).then_inc(s["s3"], 1)
                ja = bucket(e, a)
                one_hot(e, nxt, 3)
                if z:
                    add_sums(c, e, z, jz, k_fl)
                for h in range(H):
                    e.wait_ge(s_hm, a.i * (U * H) + (a.off * H + h + 1))
                    V.tensor_reduce(mx[:, h:h + 1], ps[:, 4 + h % 3, :], AX.X, ALU.max)\
                        .then_inc(s_hr, 1)
                mj = m_run[:, bass.ds(ja, 1), :]
                e.wait_ge(s_hr, a.i * (U * H) + (a.off * H + H + 3))
                V.tensor_tensor(mn, mj, mx, ALU.max).then_inc(s["mq"], 1)
                e.wait_ge(s["mq"], a.done())
                k_dd = c(V.tensor_tensor(dd, mj, mn, ALU.subtract))
                e.wait_ge(s["me"], a.done())
                c(V.tensor_tensor(v4(sm), v4(sc), v4(bank7[:, 152:184]), ALU.subtract))
                c.wait(k_dd)
                V.tensor_scalar(mj, mn, 1.0, None, ALU.mult).then_inc(s["f"], 1)

            def multiply(e, m):
                e.wait_ge(s_gat[m.u], m.turns(64))
                V.tensor_tensor(prod, psQ[m.v].rearrange("p (q c) -> p q c", q=Q), gat[:, m.u, :, 0:D],
                                ALU.mult).then_inc(s["prod"], 1)

            def weight_values(e, m):
                e.wait_ge(s["p"], m.done())
                pw = pvb[:, m.v, :, :].rearrange("p q (h c) -> p q h c", c=HC)
                gv = gat[:, m.u, :, D:2 * D].rearrange("p q (h c) -> p q h c", c=DH)
                V.tensor_tensor(pw[:, :, :, 0:DH], gv, pw[:, :, :, DH:HC].to_broadcast([P, Q, H, DH]),
                                ALU.mult).then_inc(s["pv"], 1)

            def rescale(c, e, m, j):
                aj = acc[:, bass.ds(j, 1), :].rearrange("p a (h c) -> p (a h) c", c=HC)
                e.wait_ge(s["ef"], m.done())
                e.wait_ge(s["flush"], m.done(1))
                return c(V.tensor_tensor(aj, aj, bcast(ff, 2, [P, H, HC]), ALU.mult))

            def add_sums(c, e, m, j, k_fl):
                aj = acc[:, bass.ds(j, 1), :].rearrange("p a (h c) -> p (a h) c", c=HC)
                c.wait(k_fl)
                e.wait_ge(s["sum"], m.done())
                V.tensor_tensor(aj, aj, psO[m.v].rearrange("p (h c) -> p h c", c=HC), ALU.add).then_inc(s["flush"], 1)

            def dve(e):
                c = vchain(e)
                c(V.memset(acc, 0.0))
                c(V.memset(m_run[:, :, :], NEG))
                if timed:
                    e.sem_inc(S("c_nv"), 1)
                    e.wait_ge(S("s_wt"), 16 * 7)
                else:
                    c(V.tensor_scalar(qz[:, :, :], qz[:, :, :], DH ** -0.5, None, ALU.mult))
                    c(V.tensor_scalar(bigI, ident[:, :], -NEG, None, ALU.mult))
                    c(V.tensor_copy(identb, ident[:, :]))
                    for b in range(3):
                        c(V.tensor_copy(sel[32 * b:32 * b + 32, :], ident[32 * b:32 * b + 32, 32 * b:32 * b + 32]))
                c.wait()
                e.sem_inc(s_go, 1)
                score = score_timed if timed else score_plain
                cc = Chain(e, cB)
                for m in range(2):
                    for q in range(Q):
                        one_hot(e, Macro(0, m), q)
                score(cc, e, Macro(0, 0), None, Macro(0, 2))
                first = cc.n
                per = cc_per[L]
                at = [0]

                def turn(e, M):
                    c = Chain(e, cB)
                    z = M(0)
                    c.n = first + z.off * per
                    c.enter(z.i, U * per)
                    score(c, e, M(1), z, M(3))
                    assert c.n - c.at == per, (L, c.n - c.at)
                macro_loops(0, None, turn)(e)

            phase(sync=sync, gpsimd=macro_loops(AHEAD, pool_a, lambda e, M: pool_a(e, M(AHEAD))),
                  scalar=scalar, tensor=tensor, vector=dve)

        cc_per = {0: 15, 2: 8}

        wk = wts[:, :].rearrange("p (c n) -> p c n", c=2)

        def halves(w):
            return w.rearrange("(c p) n -> p c n", p=P)

        def qkv(tag, L, table):
            loads = []
            for n, x in enumerate("qkv"):
                loads.append((wk[:, :, n * D:(n + 1) * D], halves(io[f"L{L}_gnn_W{x}"])))
                loads.append((rows[:, n * D:(n + 1) * D], row_bcast(io[f"L{L}_gnn_b{x}"])))
            groups = [(0, 0, D, [(c, wk[:, c, 0:D]) for c in range(2)]),
                      (1, 0, 2 * D, [(c, wk[:, c, D:3 * D]) for c in range(2)])]

            def evac(e, m, pp, st):
                V.tensor_tensor(qz[:, bass.ds(m.index(), 1), :], pp[:, 0, 0:D], rows[:, 0:D], ALU.add)
                return V.tensor_tensor(st, pp[:, 1, :], rows[:, D:3 * D], ALU.add)

            project(tag, 2, x_sb, loads, groups, evac, store_rows(table, 2 * D))

        def add_to_x(e, m, pp, st):
            xj = x_sb[:, bass.ds(m.index(), 1), :]
            return V.tensor_tensor(xj, xj, pp[:, 0, 0:D], ALU.add)

        def out_proj(tag, L, prepare=None):
            def prep(e, c):
                if prepare:
                    prepare(e, c)

            def bias(e, c):
                c(V.tensor_tensor(x_sb[:, :, :], x_sb[:, :, :], bcast(rows[:, 0:D], 1, [P, NB, D]), ALU.add))
            loads = [(wk[:, :, 0:D], halves(io[f"L{L}_gnn_Wo"])), (rows[:, 0:D], row_bcast(io[f"L{L}_gnn_bo"]))]
            project(tag, 2, qz, loads, [(0, 0, D, [(c, wk[:, c, 0:D]) for c in range(2)])], add_to_x,
                    prepare=prep, prep_ws=bias)

        acc4 = acc_raw[:, :, 0:AC].rearrange("p j (h c) -> p j h c", c=HC)
        qz4 = qz[:, :, :].rearrange("p j (h c) -> p j h c", c=DH)

        def softmax_over_edges():
            gmax = small[:, 0:H]
            F = big[:, 0:NT * H]
            Fv = F.rearrange("p (j h) -> p j h", h=H)
            den = big[:, NT * H:2 * NT * H].rearrange("p (j h) -> p j h", h=H)
            part = small[:, 8:16]
            rz = small[:, 16:24]

            def vector(e):
                c = vchain(e)
                c(V.tensor_reduce(gmax, m_run[:, 0:NT, :].rearrange("p j h -> p h j"), AX.X, ALU.max))
                c.wait()
                V.tensor_tensor(Fv, m_run[:, 0:NT, :], bcast(gmax, 1, [P, NT, H]), ALU.subtract).then_inc(S("n0_f"), 1)
                e.wait_ge(S("n0_e"), 1)
                c(V.tensor_tensor(den, acc4[:, 0:NT, :, DH], Fv, ALU.mult))
                c.wait()
                V.tensor_reduce(part, den.rearrange("p j h -> p h j"), AX.X, ALU.add).then_inc(S("n0_f"), 1)
                e.wait_ge(S("n0_z"), 1)
                c(V.reciprocal(rz, ps[:, 7, 0:H]))
                c.wait()
                c(V.tensor_tensor(Fv, Fv, bcast(rz, 1, [P, NT, H]), ALU.mult))
                c.wait()
                c(V.memset(qz[:, NT, :], 0.0))
                for h in range(H):
                    c(V.tensor_tensor(qz4[:, 0:NT, h, :], acc4[:, 0:NT, h, 0:DH],
                                      bcast(Fv[:, :, h], 2, [P, NT, DH]), ALU.mult))
                c.wait()

            def scalar(e):
                e.wait_ge(S("n0_f"), 1)
                A.activation(F, F, ACT.Exp).then_inc(S("n0_e"), 1)

            def tensor(e):
                e.wait_ge(S("n0_f"), 2)
                T.matmul(ps[:, 7, 0:H], ones[:, :], part, start=True, stop=True).then_inc(S("n0_z"), 1)

            phase(vector=vector, scalar=scalar, tensor=tensor)

        qkv("p0", 0, kv0)
        attention(0, "d", kv0)
        softmax_over_edges()
        out_proj("o0", 0)
        v_ln, a_ln = layernorm("l0")
        phase(vector=v_ln, scalar=a_ln)

        INV_SQRT3 = 3.0 ** -0.5
        y_scale = MUL ** -0.5

        def layer1():
            wy = wts[:, 0:2 * 2 * P].rearrange("p (c n) -> p c n", c=2)

            def w_blocks(c, sel_):
                return wy[:, c, sel_ * P:(sel_ + 1) * P]

            w_zero = sem("p1_zero")
            loads = []
            for c in range(2):
                for which, (ws, wv) in enumerate((("L1_gnn_w1_s", "L1_gnn_w1_v"), ("L1_gnn_wsc_s", "L1_gnn_wsc_v"))):
                    for half in range(2):
                        w = ws if c == 0 and half == 0 else wv
                        loads.append((w_blocks(c, which)[half * MUL:(half + 1) * MUL, half * MUL:(half + 1) * MUL],
                                      io[w]))
            groups = [(c, 0, 2 * P, [(c, wy[:, c, :])]) for c in range(2)]

            def split(e, c):
                c(V.tensor_copy(qz[:, :, 0:MUL], x_sb[:, :, 0:MUL]))
                for d in range(3):
                    c(V.tensor_copy(qz[:, :, (d + 1) * MUL:(d + 2) * MUL], x_sb[:, :, MUL + d::3]))
                c.wait()

            def evac(e, m, pp, st):
                V.tensor_scalar(qz[:, bass.ds(m.index(), 1), :].rearrange("p a (c n) -> p (a c) n", c=2),
                                pp[:, :, P:2 * P], y_scale, None, ALU.mult)
                return V.tensor_scalar(st[:, 0:D].rearrange("p (c n) -> p c n", c=2), pp[:, :, 0:P],
                                       y_scale, None, ALU.mult)

            def clear(e):
                V.memset(wts[:, 0:4 * P], 0.0).then_inc(w_zero, 1)
                e.wait_ge(w_zero, 1)

            phase(vector=clear)
            project("p1", 2, qz, loads, groups, evac, store_rows(y1, D), prepare=split)

            s = stages("e1", "oh", "tr", "at", "h1", "g1", "h2", "g2", "w", "wac", "wr", "msg", "sum", "flush")
            s_rec = [sem(f"e1_rec{u}") for u in range(U)]
            s_gat = [sem(f"e1_gat{u}") for u in range(U)]
            cB = sem("e1_cB")
            r_sb = rec["s"]
            fc1 = rows[0:8, 0:64]
            fc2 = rows[0:64, 64:128]
            fc3 = rows[0:64, 128:384]
            at = work[0:8, 0:512]
            h1 = work[0:64, 512:1024]
            h2 = work[0:64, 1024:1536]
            wac = work[:, 1536:2048].rearrange("p (q a n) -> p q a n", q=Q, a=2)
            wb = work[:, 2048:2304].rearrange("p (q n) -> p q n", q=Q)
            dot = work[:, 2304:2560].rearrange("p (q n) -> p q n", q=Q)
            g3 = gat[:, 1, 2:4, :].rearrange("p a b -> p (a b)")[:, 0:768].rearrange("p (q d n) -> p q d n", q=Q, d=3)
            rows_y = [gat[:, u, 0:2, :].rearrange("p a (b c) -> p (a b) c", c=D) for u in range(U)]
            msg = [big[:, u * 2048:(u + 1) * 2048].rearrange("p (q c h n) -> p q c h n", q=Q, c=4, h=2)
                   for u in range(2)]
            psW = ps[:, 3:5, :].rearrange("p b c -> p (b c)").rearrange("p (q k n) -> p q k n", q=Q, k=4)
            psDeg = [ps[:, 2, 0:1], ps[:, 7, 0:1]]
            acc = acc_raw[:, :, 0:2 * D]

            def sync_a(e, m):
                i = e.snap(m.index())
                e.wait_ge(s["msg"], m.done(U))
                e.sem_inc(S("s_sp"), 1)
                r = recs["s"].rearrange("(m p q) w -> m p (q w)", p=P, q=Q)
                e.dma_start(r_sb[:, m.u, :, :].rearrange("p q w -> p (q w)"),
                            r[bass.ds(i, 1)].rearrange("a p c -> p (a c)")).then_inc(s_rec[m.u], 16)

            def sync(e):
                for dst_ap, name in ((fc1, "fc_w1"), (fc2, "fc_w2"), (fc3, "fc_w3")):
                    e.dma_start(dst_ap, io[f"L1_gnn_{name}"]).then_inc(S("e1_fc"), 16)
                macro_loops(3, sync_a, lambda e, M: sync_a(e, M(3)))(e)

            def pool_a(e, m):
                e.wait_ge(s_rec[m.u], m.turns(16))
                e.sem_inc(S("s_gp"), 1)
                e.wait_ge(s["msg"], m.done(U))
                e.sem_inc(S("s_gp"), 1)
                for q in range(Q):
                    e.indirect_dma_start(
                        out=rows_y[m.u][:, q, :], out_offset=None, in_=y1,
                        in_offset=bass.IndirectOffsetOnAxis(ap=r_sb[:, m.u, q, 0:1].bitcast(I32), axis=0),
                    ).then_inc(s_gat[m.u], 16)

            def transposes(e, m):
                e.wait_ge(s_rec[m.u], m.turns(16))
                e.wait_ge(s["g2"], m.done(1))
                for q in range(Q):
                    last = T.transpose(ps[0:8, 0, q * P:(q + 1) * P], r_sb[:, m.u, q, 6:14], ident[:, :])
                last.then_inc(s["tr"], 1)

            def layer_1(e, m):
                e.wait_ge(s["at"], m.done())
                e.wait_ge(s["g1"], m.done(1))
                T.matmul(ps[0:64, 1, :], fc1, at, start=True, stop=True).then_inc(s["h1"], 1)

            def layer_2(e, m):
                e.wait_ge(s["g1"], m.done())
                e.wait_ge(s["g2"], m.done(1))
                e.sem_inc(S("s_pe"), 1)
                T.matmul(ps[0:64, 0, :], fc2, h1, start=True, stop=True).then_inc(s["h2"], 1)

            def layer_3(e, m):
                e.wait_ge(s["g2"], m.done())
                e.wait_ge(s["wr"], m.done(1))
                for q in range(Q):
                    last = T.matmul(psW[:, q].rearrange("p k n -> p (k n)"), h2[:, q * P:(q + 1) * P], fc3,
                                    start=True, stop=True)
                last.then_inc(s["w"], 1)

            def sums(e, m, q):
                if q == 0:
                    e.wait_ge(s["oh"], m.done())
                    e.wait_ge(s["msg"], m.done())
                    e.wait_ge(s["flush"], m.done(2))
                T.matmul(psDeg[m.v], oh[:, m.u, q, :], ones[:, 0:1], start=(q == 0), stop=(q == Q - 1))
                ins = T.matmul(ps[:, 5 + m.v, :], oh[:, m.u, q, :],
                               msg[m.v][:, q].rearrange("p c h n -> p (c h n)"),
                               start=(q == 0), stop=(q == Q - 1))
                if q == Q - 1:
                    ins.then_inc(s["sum"], 1)

            def tensor(e):
                e.wait_ge(S("e1_fc"), 48)
                e.wait_ge(S("e1_go"), 1)
                for m in range(2):
                    for part in (transposes, layer_1, layer_2, layer_3):
                        part(e, Macro(0, m))

                def turn(e, M):
                    transposes(e, M(2))
                    sums(e, M(0), 0)
                    layer_1(e, M(2))
                    sums(e, M(0), 1)
                    layer_2(e, M(2))
                    sums(e, M(0), 2)
                    sums(e, M(0), 3)
                    layer_3(e, M(2))
                macro_loops(0, None, turn)(e)

            def act(e, m):
                e.wait_ge(s["tr"], m.done())
                e.wait_ge(s["h1"], m.done(1))
                A.activation(at, ps[0:8, 0, :], ACT.Copy).then_inc(s["at"], 1)
                e.wait_ge(s["h1"], m.done())
                e.wait_ge(s["h2"], m.done(1))
                A.activation(h1, ps[0:64, 1, :], ACT.Silu, scale=8.0 ** -0.5).then_inc(s["g1"], 1)
                e.wait_ge(s["h2"], m.done())
                e.wait_ge(s["w"], m.done(1))
                A.activation(h2, ps[0:64, 0, :], ACT.Silu, scale=MUL ** -0.5).then_inc(s["g2"], 1)
                e.wait_ge(s["w"], m.done())
                e.wait_ge(s["wr"], m.done(1))
                for q in range(Q):
                    last = A.activation(wac[:, q], psW[:, q, 0:3:2, :], ACT.Copy, scale=r_sb[:, m.u, q, 2:3])
                last.then_inc(s["wac"], 1)

            def one_hot(e, m, q):
                if q == 0:
                    e.wait_ge(s_rec[m.u], m.turns(16))
                    e.wait_ge(s["sum"], m.done(U))
                ins = V.tensor_scalar(oh[:, m.u, q, :], iota[:, :], r_sb[:, m.u, q, 1:2], None, ALU.is_equal)
                if q == Q - 1:
                    ins.then_inc(s["oh"], 1)

            def messages(c, e, m, nxt):
                y = rows_y[m.u]
                yv = y[:, :, MUL:4 * MUL].rearrange("p q (d n) -> p q d n", d=3)
                shd = r_sb[:, m.u, :, 3:6]
                shb = bcast(shd, 3, [P, Q, 3, MUL])
                o = msg[m.v]
                e.wait_ge(s_gat[m.u], m.turns(64))
                k = c(V.tensor_tensor(g3, yv, shb, ALU.mult))
                one_hot(e, nxt, 0)
                one_hot(e, nxt, 1)
                c.wait(k)
                k = c(V.tensor_tensor(dot, g3[:, :, 0, :], g3[:, :, 1, :], ALU.add))
                one_hot(e, nxt, 2)
                c.wait(k)
                k_dot = c(V.tensor_tensor(dot, dot, g3[:, :, 2, :], ALU.add))
                one_hot(e, nxt, 3)
                e.wait_ge(s["sum"], m.done(2))
                e.wait_ge(s["wac"], m.done())
                k_wb = c(V.tensor_tensor(wb, psW[:, :, 1, :], y[:, :, 0:MUL], ALU.mult))
                c.wait(k_dot)
                V.tensor_tensor(o[:, :, 0, 1, :], psW[:, :, 3, :], dot, ALU.mult)
                V.tensor_tensor(o[:, :, 0, 0, :], wac[:, :, 0, :], y[:, :, 0:MUL], ALU.mult)
                V.tensor_tensor(o[:, :, 1:4, 1, :], bcast(wac[:, :, 1, :], 2, [P, Q, 3, MUL]), yv, ALU.mult)\
                    .then_inc(s["wr"], 1)
                c.wait(k_wb)
                V.tensor_tensor(o[:, :, 1:4, 0, :], bcast(wb, 2, [P, Q, 3, MUL]), shb, ALU.mult)\
                    .then_inc(s["msg"], 1)

            def add_sums(c, e, m):
                j = e.value_load(jmap["s"][0:1, bass.ds(m.index(), 1)], min_val=0, max_val=NB - 1)
                e.wait_ge(s["flush"], m.done(1))
                e.wait_ge(s["sum"], m.done())
                dj, aj = deg[:, bass.ds(j, 1)], acc[:, bass.ds(j, 1), :]
                V.tensor_tensor(dj, dj, psDeg[m.v], ALU.add)
                V.tensor_tensor(aj, aj, ps[:, 5 + m.v, :], ALU.add).then_inc(s["flush"], 1)

            def dve(e):
                c = vchain(e)
                c(V.memset(acc, 0.0))
                c(V.memset(deg[:, :], 0.0))
                c.wait()
                e.sem_inc(S("e1_go"), 1)
                for m in range(2):
                    for q in range(Q):
                        one_hot(e, Macro(0, m), q)
                cc = Chain(e, cB)
                messages(cc, e, Macro(0, 0), Macro(0, 2))
                per = cc.n

                def turn(e, M):
                    c = Chain(e, cB)
                    c.n = per * M(1).off
                    c.enter(M(1).i, U * per)
                    messages(c, e, M(1), M(3))
                    assert c.n - c.at == per
                    add_sums(c, e, M(0))
                macro_loops(0, None, turn)(e)

            phase(sync=sync, gpsimd=macro_loops(3, pool_a, lambda e, M: pool_a(e, M(3))),
                  scalar=macro_loops(2, act, lambda e, M: act(e, M(2))), tensor=tensor, vector=dve)

            w2 = wts[:, 0:P].rearrange("p (k n) -> p k n", k=2)
            s_act = (sem("o1_go"), sem("o1_root"))

            def scale(e):
                c = vchain(e)
                c(V.tensor_scalar(deg[:, :], deg[:, :], 1.0, None, ALU.max))
                c.wait()
                e.sem_inc(s_act[0], 1)
                e.wait_ge(s_act[1], 1)
                c(V.reciprocal(small[:, 0:NB], deg[:, :]))
                c.wait()
                c(V.tensor_tensor(acc, acc, bcast(small[:, 0:NB], 2, [P, NB, 2 * D]), ALU.mult))
                c.wait()

            def root(e):
                e.wait_ge(s_act[0], 1)
                A.activation(deg[:, :], deg[:, :], ACT.Sqrt).then_inc(s_act[1], 1)

            phase(vector=scale, scalar=root)

            out_scale = (2 * MUL) ** -0.5 * MUL ** -0.5

            def w_adjust(e, c):
                c(V.tensor_scalar(w2[MUL:P, 0, :], w2[MUL:P, 0, :], INV_SQRT3, None, ALU.mult))

            def evac2(e, m, pp, st):
                t = qz[:, bass.ds(m.index(), 1), :]
                return V.scalar_tensor_tensor(t, pp[:, 0, 0:D], out_scale, t, ALU.mult, ALU.add)

            project("o1", 4, acc, [(w2[:, 0, :], io["L1_gnn_w2_s"]), (w2[:, 1, :], io["L1_gnn_w2_v"]),
                                   (rows[:, 0:MUL], row_bcast(io["L1_gnn_g_s"])),
                                   (rows[:, MUL:2 * MUL], row_bcast(io["L1_gnn_g_v"]))],
                    [(0, c * MUL, (c + 1) * MUL, [(c, w2[:, min(c, 1), :])]) for c in range(4)], evac2,
                    prep_ws=w_adjust)

            def rms(e, c, s_act):
                sq = junk
                st_, tmp_ = small[:, 128:128 + 2 * NB], small[:, 192:192 + 2 * NB]
                c(V.tensor_tensor(sq, qz[:, :, :], qz[:, :, :], ALU.mult))
                c.wait()
                c(V.tensor_reduce(st_[:, 0:NB], sq[:, :, 0:MUL], AX.X, ALU.add))
                c(V.tensor_reduce(st_[:, NB:2 * NB], sq[:, :, MUL:D], AX.X, ALU.add))
                c.wait()
                c(V.tensor_scalar(st_[:, NB:2 * NB], st_[:, NB:2 * NB], 1.0 / 3.0, None, ALU.mult))
                c.wait()
                rstd(e, c, s_act, 1, st_, 1.0 / MUL, tmp_)
                zs = qz[:, :, 0:MUL]
                zv = qz[:, :, MUL:D]
                c(V.tensor_tensor(zs, zs, bcast(st_[:, 0:NB], 2, [P, NB, MUL]), ALU.mult))
                c(V.tensor_tensor(zv, zv, bcast(st_[:, NB:2 * NB], 2, [P, NB, 3 * MUL]), ALU.mult))
                c.wait()
                c(V.tensor_tensor(zs, zs, bcast(rows[:, 0:MUL], 1, [P, NB, MUL]), ALU.mult))
                for d in range(3):
                    zd = qz[:, :, (d + 1) * MUL:(d + 2) * MUL]
                    c(V.tensor_tensor(zd, zd, bcast(rows[:, MUL:2 * MUL], 1, [P, NB, MUL]), ALU.mult))
                c.wait()
                xs_ = x_sb[:, :, 0:MUL]
                c(V.tensor_tensor(xs_, xs_, zs, ALU.add))
                for d in range(3):
                    xd = x_sb[:, :, MUL + d::3]
                    c(V.tensor_tensor(xd, xd, qz[:, :, (d + 1) * MUL:(d + 2) * MUL], ALU.add))
                c.wait()
                return 1

            v1_, a1_ = layernorm("l1", before=rms, roots=[small[:, 192:192 + 2 * NB]])
            phase(vector=v1_, scalar=a1_)

        layer1()

        def softmax_by_node(e, c):
            den = acc4[:, :, :, DH]
            c(V.tensor_scalar(den, den, 1e-30, None, ALU.max))
            c.wait()
            c(V.reciprocal(big[:, 0:NB * H].rearrange("p (j h) -> p j h", h=H), den))
            c.wait()
            rden = big[:, 0:NB * H].rearrange("p (j h) -> p j h", h=H)
            for h in range(H):
                c(V.tensor_tensor(qz4[:, :, h, :], acc4[:, :, h, 0:DH], bcast(rden[:, :, h], 2, [P, NB, DH]),
                                  ALU.mult))
            c.wait()

        def layer2():
            qkv("p2", 2, kv2)
            attention(2, "s", kv2)
            out_proj("o2", 2, prepare=softmax_by_node)
            v, a = layernorm("l2")
            phase(vector=v, scalar=a)

        def layer3():
            s = stages("e3", "oh", "pv", "sum", "flush")
            s_rec = [sem(f"e3_rec{u}") for u in range(U)]
            s_gat = [sem(f"e3_gat{u}") for u in range(U)]
            r_sb = rec["d"]
            acc = acc_raw[:, :, 0:D]
            r = recs["d"].rearrange("(m p q) w -> m p (q w)", p=P, q=Q)

            def sync_a(e, m):
                i = e.snap(m.index())
                e.wait_ge(s["sum"], m.done(U))
                e.sem_inc(S("s_sp"), 1)
                e.dma_start(r_sb[:, m.u, :, :].rearrange("p q w -> p (q w)"),
                            r[bass.ds(i, 1)].rearrange("a p c -> p (a c)")).then_inc(s_rec[m.u], 16)

            def sync(e):
                e.dma_start(x3.rearrange("(j p) c -> p j c", p=P), x_sb[:, :, :]).then_inc(S("e3_x"), 16)
                e.wait_ge(S("e3_x"), 16)
                macro_loops(3, sync_a, lambda e, M: sync_a(e, M(3)))(e)

            def pool_a(e, m):
                e.wait_ge(s_rec[m.u], m.turns(16))
                e.sem_inc(S("s_gp"), 1)
                e.wait_ge(s["sum"], m.done(U))
                e.sem_inc(S("s_gp"), 1)
                for q in range(Q):
                    e.indirect_dma_start(
                        out=gat[:, m.u, q, 0:D], out_offset=None, in_=x3,
                        in_offset=bass.IndirectOffsetOnAxis(ap=r_sb[:, m.u, q, 0:1].bitcast(I32), axis=0),
                    ).then_inc(s_gat[m.u], 16)

            def pool(e):
                e.wait_ge(S("e3_x"), 16)
                macro_loops(3, pool_a, lambda e, M: pool_a(e, M(3)))(e)

            def pe(e, m):
                e.wait_ge(s["oh"], m.done())
                e.wait_ge(s_gat[m.u], m.turns(64))
                e.wait_ge(s["flush"], m.done(2))
                for q in range(Q):
                    last = T.matmul(ps[:, 5 + m.v, 0:D], oh[:, m.u, q, :], gat[:, m.u, q, 0:D],
                                    start=(q == 0), stop=(q == Q - 1))
                last.then_inc(s["sum"], 1)

            def tensor(e):
                macro_loops(0, None, lambda e, M: pe(e, M(0)))(e)

            def dve_a(e, m):
                e.wait_ge(s_rec[m.u], m.turns(16))
                e.wait_ge(s["sum"], m.done(U))
                for q in range(Q):
                    last = V.tensor_scalar(oh[:, m.u, q, :], iota[:, :], r_sb[:, m.u, q, 1:2],
                                           r_sb[:, m.u, q, 2:3], ALU.is_equal, ALU.mult)
                last.then_inc(s["oh"], 1)

            def dve_b(e, m):
                j = e.value_load(jmap["d"][0:1, bass.ds(m.index(), 1)], min_val=0, max_val=NB - 1)
                e.wait_ge(s["flush"], m.done(1))
                e.wait_ge(s["sum"], m.done())
                aj = acc[:, bass.ds(j, 1), :]
                V.tensor_tensor(aj, aj, ps[:, 5 + m.v, 0:D], ALU.add).then_inc(s["flush"], 1)

            def dve(e):
                V.memset(acc, 0.0).then_inc(S("e3_z"), 1)
                e.wait_ge(S("e3_z"), 1)
                macro_loops(3, dve_a, lambda e, M: (dve_a(e, M(3)), dve_b(e, M(0))))(e)

            phase(sync=sync, gpsimd=pool, tensor=tensor, vector=dve)

            wide = acc_raw[:, :, 0:2 * D]
            w4 = wts[:, 0:4 * D].rearrange("p (c n) -> p c n", c=4)

            def inputs_(e, c):
                nb = wide[:, :, 0:D]
                c(V.tensor_tensor(qz[:, :, :], nb, x_sb[:, :, :], ALU.mult))
                c(V.tensor_copy(wide[:, :, D:2 * D], x_sb[:, :, :]))
                c.wait()
                c(V.tensor_tensor(nb, nb, qz[:, :, :], ALU.add))
                c.wait()

            def bias(e, c):
                c(V.tensor_tensor(rows[:, 0:D], rows[:, 0:D], rows[:, D:2 * D], ALU.add))

            def evac(e, m, pp, st):
                return V.tensor_tensor(qz[:, bass.ds(m.index(), 1), :], pp[:, 0, 0:D], rows[:, 0:D], ALU.add)

            project("o3", 4, wide, [(w4[:, 0:2, :], halves(io["L3_gnn_W2"])), (w4[:, 2:4, :], halves(io["L3_gnn_W1"])),
                                    (rows[:, 0:D], row_bcast(io["L3_gnn_b1"])),
                                    (rows[:, D:2 * D], row_bcast(io["L3_gnn_b2"]))],
                    [(0, 0, D, [(c, w4[:, c, :]) for c in range(4)])], evac, prepare=inputs_, prep_ws=bias)

            def normalize(e, c, s_act):
                z = qz[:, :, :]
                n2 = small[:, 128:128 + NB]
                c(V.scalar_tensor_tensor(z, z, 0.2, z, ALU.mult, ALU.max))
                c.wait()
                c(V.tensor_tensor(junk, z, z, ALU.mult))
                c.wait()
                c(V.tensor_reduce(n2, junk, AX.X, ALU.add))
                c.wait()
                e.sem_inc(s_act[0], 1)
                e.wait_ge(s_act[1], 1)
                c(V.tensor_scalar(n2, n2, 1e-12, None, ALU.max))
                c.wait()
                c(V.reciprocal(n2, n2))
                c.wait()
                c(V.tensor_tensor(z, z, bcast(n2, 2, [P, NB, D]), ALU.mult))
                c.wait()
                c(V.tensor_tensor(x_sb[:, :, :], x_sb[:, :, :], z, ALU.add))
                c.wait()
                return 1

            v, a = layernorm("l3", before=normalize, roots=[small[:, 128:128 + NB]])
            phase(vector=v, scalar=a)

            def store(e):
                e.dma_start(out[0:(NT - 1) * P, :].rearrange("(j p) d -> p j d", p=P), x_sb[:, 0:NT - 1, :])\
                    .then_inc(S("s_out"), 16)
                e.dma_start(out[(NT - 1) * P:N_NODES, :], x_sb[0:LAST, NT - 1, :]).then_inc(S("s_out"), 16)
                e.wait_ge(S("s_out"), 32)

            phase(sync=store)

        layer2()
        layer3()

        block = ctx.enter_context(nc.Block())

        def run(e, todo):
            for fn, meet in todo:
                if fn:
                    fn(e)
                e.drain().then_inc(s_bar, 1)
                e.wait_ge(s_bar, meet)

        @block.sync
        def _(e):
            for counter, start in credits:
                e.sem_inc(counter, start)
            run(e, programs["sync"])

        @block.gpsimd
        def _(e):
            run(e, programs["gpsimd"])

        @block.scalar
        def _(e):
            run(e, programs["scalar"])

        @block.vector
        def _(e):
            run(e, programs["vector"])

        @block.tensor
        def _(e):
            run(e, programs["tensor"])


def layout(inputs):
    def pad(a, fill):
        a = np.asarray(a)
        out = np.full((E_PAD,) + a.shape[1:], fill, a.dtype)
        out[:N_EDGES] = a
        return out.reshape((P, EC) + a.shape[1:])

    src, dst = inputs["src"], inputs["dst"]
    ins = {
        "x": inputs["x"],
        "dst_key": pad(dst, PAD_KEY), "src_idx": pad(src, 0),
        "src_key": pad(src, PAD_KEY), "dst_idx": pad(dst, 0),
        "edge_weight": pad(inputs["edge_weight"], 0),
        "edge_attr_4": pad(inputs["edge_attr_4"], 0),
        "edge_attr_8": pad(inputs["edge_attr_8"], 0),
        "node_vec": np.pad(np.asarray(inputs["node_vec"]), (0, NB * P - N_NODES)).reshape(NB, P).T,
    }
    for name, a in inputs.items():
        if name[:2] in ("L0", "L1", "L2", "L3"):
            ins[name] = np.asarray(a)
    for name in ("L3_gnn_W1", "L3_gnn_W2"):
        ins[name] = np.ascontiguousarray(ins[name].T)
    return {k: np.ascontiguousarray(a) for k, a in ins.items()}


def kernel(**inputs):
    import concourse.bacc as bacc
    from concourse.bass_utils import run_bass_kernel_spmd

    nc = bacc.Bacc("TRN2", target_bir_lowering=False, num_devices=1)
    arrays = {f"in_{name}": a for name, a in layout(inputs).items()}
    io = {name[3:]: nc.dram_tensor(name, a.shape, mybir.dt.from_np(a.dtype), kind="ExternalInput").ap()
          for name, a in arrays.items()}
    out = nc.dram_tensor("out", (N_NODES, D), F32, kind="ExternalOutput").ap()
    gnn_kernel(nc, io, out)
    return run_bass_kernel_spmd(nc, [arrays], core_ids=[0]).results[0]["out"]
```

```python
from contextlib import ExitStack

import numpy as np
import concourse.bass as bass
from concourse import mybir

F32 = mybir.dt.float32
I32 = mybir.dt.int32
BF16 = mybir.dt.bfloat16
ALU = mybir.AluOpType
ACT = mybir.ActivationFunctionType
AX = mybir.AxisListType

P = 128
N_NODES = 3125
N_EDGES = 100000
D = 256
H = 8
DH = D // H
HC = DH + 1
AC = H * HC
MUL = 64
EC = 784
E_PAD = P * EC
NT = (N_NODES + P - 1) // P
LAST = N_NODES - (NT - 1) * P
NB = NT + 1
PAD_KEY = NB * P - 1
Q = 4
ME = Q * P
NM = (E_PAD + NB * (ME - 1)) // ME
U = 4
NM += -NM % U
NMA = NM + 4
NEG = -1.0e30
LN_EPS = 1e-5
CREDIT = U


class Macro:

    def __init__(self, i, off, before=0, per=U):
        self.i, self.off, self.before, self.per = i, off, before, per
        self.u, self.v = off % per, off % 2

    def done(self, lag=0):
        return self.i * self.per + (self.off + 1 + CREDIT - lag + self.before)

    def turns(self, n, lag=0):
        return self.i * n + ((self.off // self.per + 1 - lag) * n + self.before // self.per * n)

    def index(self):
        return self.i * self.per + self.off


class Chain:

    def __init__(self, engine, sem):
        self.e, self.sem, self.n, self.i, self.per, self.at = engine, sem, 0, 0, 0, 0

    def __call__(self, ins):
        ins.then_inc(self.sem, 1)
        self.n += 1
        return self.n

    def wait(self, n=None):
        self.e.wait_ge(self.sem, self.i * self.per + (self.n if n is None else n))

    def enter(self, i, per):
        self.i, self.per, self.at = i, per, self.n

    def leave(self, times):
        assert self.n - self.at == self.per, (self.n - self.at, self.per)
        self.n = self.at + self.per * times
        self.i = self.per = 0


def top(ap):
    return ap.bitcast(BF16)[..., 1::2]


def bcast(ap, axis, shape):
    return ap.unsqueeze(axis).to_broadcast(shape)


def gnn_kernel(nc, io, out):
    ctx = ExitStack()
    with ctx:
        def sb(name, shape, dt=F32):
            return ctx.enter_context(nc.sbuf_tensor(name, shape, dt))

        def sem(name):
            return ctx.enter_context(nc.semaphore(name))

        def dram(name, shape, dt=F32):
            return nc.dram_tensor(name, shape, dt, kind="Internal").ap()

        WD, WS = 4, 16
        recs = {"d": dram("rec_d", [NMA * ME, WD]), "s": dram("rec_s", [NMA * ME, WS])}
        kv0 = dram("kv0", [NB * P, 2 * D])
        y1 = dram("y1", [NB * P, D])
        kv2 = dram("kv2", [NB * P, 2 * D])
        x3 = dram("x3", [NB * P, D])

        iota = sb("iota", [P, P])
        iota26 = sb("iota26", [P, NB])
        pcol = sb("pcol", [P, 1])
        ident = sb("ident", [P, P])
        ones = sb("ones", [P, P])
        tri = sb("tri", [P, P])
        x_sb = sb("x_sb", [P, NB, D])
        qz = sb("qz", [P, NB, D])
        acc_raw = sb("acc", [P, NB, AC + D])
        qp = acc_raw[:, :, AC:AC + D].bitcast(BF16)
        m_run = sb("m_run", [P, NB, H])
        jmap = {"d": sb("jmap_d", [1, NMA], I32), "s": sb("jmap_s", [1, NMA], I32)}
        deg = sb("deg", [P, NB])
        rec = {"d": sb("rec_sb_d", [P, U, Q, WD]), "s": sb("rec_sb_s", [P, U, Q, WS])}
        gat = sb("gat", [P, U, Q, 2 * D])
        oh = sb("oh", [P, U, Q, P])
        big = sb("big", [P, 4 * Q * D])
        small = sb("small", [P, 640])
        wts = sb("wts", [P, 3 * 2 * D])
        rows = sb("rows", [P, 3 * D])
        by_src = sb("by_src", [P, 3, EC + EC // (NM // U)])

        ps = ctx.enter_context(nc.psum_tensor("ps", [P, 8, 512], F32))

        sems = {}
        credits = []

        def S(name):
            if name not in sems:
                sems[name] = sem(name)
            return sems[name]

        T = nc.tensor
        V = nc.vector
        A = nc.scalar
        G = nc.gpsimd

        s_bar = sem("s_bar")
        the_vchain = Chain(None, S("c_vector"))

        def vchain(e):
            the_vchain.e = e
            return the_vchain

        bars = [0]
        programs = {k: [] for k in ("sync", "gpsimd", "scalar", "vector", "tensor")}

        def phase(**fns):
            bars[0] += 1
            meet = 5 * bars[0]
            for name, todo in programs.items():
                todo.append((fns.get(name), meet))

        ai = acc_raw[:, :, :].rearrange("p a b -> p (a b)")
        FREE = {"at": 0}

        def scratch(cols, dt=F32, shape=None):
            at = FREE["at"]
            FREE["at"] += cols
            assert FREE["at"] <= NB * (AC + D), FREE["at"]
            v = ai[:, at:at + cols]
            return v if dt == F32 else v.bitcast(dt)

        key_i = scratch(EC, I32)
        tmp_i = scratch(EC, I32)
        bkt = scratch(EC)
        rels = {"d": scratch(EC), "s": by_src[:, 1, 0:EC]}
        idxs = {"d": scratch(EC, I32), "s": by_src[:, 0, 0:EC].bitcast(I32)}
        mask = qz[:, :, :].rearrange("p a b -> p (a b)")[:, 0:EC]
        scan = qz[:, :, :].rearrange("p a b -> p (a b)")[:, EC:2 * EC]
        pos = qz[:, :, :].rearrange("p a b -> p (a b)")[:, 2 * EC:3 * EC]
        zero = qz[:, :, :].rearrange("p a b -> p (a b)")[:, 3 * EC:4 * EC]
        slots = {"d": scratch(EC, I32), "s": by_src[:, 2, 0:EC].bitcast(I32)}
        ew = scratch(EC)
        cnt = small[:, 0:NB]
        tot = small[:, 32:32 + NB]
        tot_i = small[:, 64:64 + NB].bitcast(I32)
        mac = small[:, 96:96 + NB]
        inc = small[:, 128:128 + NB]
        offs = small[:, 160:160 + NB]
        zero26 = small[:, 192:192 + NB]
        ring = wts[:, 0:2 * 8 * WS]
        pring = rows[:, 0:16].bitcast(I32)
        RH = 8
        jcmp = big[0:1, :]

        def consts_vector(e):
            c = vchain(e)
            c(V.memset(zero, 0.0))
            c(V.memset(x_sb[:, NT - 1:NB, :], 0.0))
            c(V.memset(zero26, 0.0))
            c(V.memset(ones[:, :], 1.0))
            e.wait_ge(S("s_iota"), 4)
            c(V.tensor_scalar(ident[:, :], iota[:, :], pcol[:, 0:1], None, ALU.is_equal))
            c(V.tensor_scalar(tri[:, :], iota[:, :], pcol[:, 0:1], None, ALU.is_gt))
            fill = gat[:, :, :, :].rearrange("p a b c -> p (a b c)")
            c(V.memset(fill[:, 0:FR * WS], 0.0))
            c.wait()
            for w, part in ((WD, fill[:, 0:FR * WD]), (WS, fill[:, 0:FR * WS])):
                v = part.rearrange("p (r w) -> p r w", w=w)
                e.wait_ge(S("s_fill"), 0 if w == WD else 16 * (NMA * ME // P // FR))
                c(V.memset(part, 0.0))
                c.wait()
                if w == WD:
                    c(V.memset(v[:, :, 3:4], NEG))
                V.memset(v[:, :, 1:2], -1.0).then_inc(S("s_fillv"), 1)
                e.wait_ge(S("s_fillv"), 1 if w == WD else 2)

        FR = NMA
        assert (NMA * ME // P) % FR == 0

        def consts_sync(e):
            x_in = io["x"]
            e.wait_ge(S("c_vector"), 2)
            e.dma_start(x_sb[:, 0:NT - 1, :],
                        x_in[0:(NT - 1) * P, :].rearrange("(j p) d -> p j d", p=P)).then_inc(S("s_x"), 16)
            e.dma_start(x_sb[0:LAST, NT - 1, :], x_in[(NT - 1) * P:N_NODES, :]).then_inc(S("s_x"), 16)
            fill = gat[:, :, :, :].rearrange("p a b c -> p (a b c)")
            n = 0
            for w, k in ((WD, "d"), (WS, "s")):
                e.wait_ge(S("s_fillv"), 1 if w == WD else 2)
                r = recs[k].rearrange("(c p r) w -> c p (r w)", p=P, r=FR)
                for b in range(NMA * ME // P // FR):
                    e.dma_start(r[b], fill[:, 0:FR * w]).then_inc(S("s_fill"), 16)
                    n += 16
            e.wait_ge(S("s_fill"), n)
            e.wait_ge(S("s_x"), 32)

        def consts_gpsimd(e):
            G.iota(iota[:, :], [[1, P]], base=0, channel_multiplier=0,
                   allow_small_or_imprecise_dtypes=True).then_inc(S("s_iota"), 1)
            G.iota(iota26[:, :], [[1, NB]], base=0, channel_multiplier=0,
                   allow_small_or_imprecise_dtypes=True).then_inc(S("s_iota"), 1)
            G.iota(pcol[:, :], [[1, 1]], base=0, channel_multiplier=1,
                   allow_small_or_imprecise_dtypes=True).then_inc(S("s_iota"), 1)
            G.iota(jcmp[:, 0:NMA], [[1, NMA]], base=0, channel_multiplier=0,
                   allow_small_or_imprecise_dtypes=True).then_inc(S("s_iota"), 1)

        phase(sync=consts_sync, vector=consts_vector, gpsimd=consts_gpsimd)

        def sort(k):
            key_in, idx_in = (io["dst_key"], io["src_idx"]) if k == "d" else (io["src_key"], io["dst_idx"])
            rel, idx_i, pos_i = rels[k], idxs[k], slots[k]
            n_in = 3 if k == "d" else 2
            s_in = S(f"s_in_{k}")

            def load(e):
                e.dma_start(key_i, key_in).then_inc(s_in, 16)
                e.dma_start(idx_i, idx_in).then_inc(s_in, 16)
                if k == "d":
                    e.dma_start(ew, io["edge_weight"]).then_inc(s_in, 16)

            def place(e):
                c = vchain(e)
                e.wait_ge(s_in, 16 * n_in)
                c(V.tensor_scalar(tmp_i, key_i, 7, None, ALU.arith_shift_right))
                c.wait()
                c(V.tensor_copy(bkt, tmp_i))
                c.wait()
                c(V.tensor_scalar(tmp_i, key_i, P - 1, None, ALU.bitwise_and))
                c.wait()
                c(V.tensor_copy(rel, tmp_i))
                c(V.memset(pos, 0.0))
                if k == "s":
                    c(V.memset(by_src[:, :, EC:], 0.0))
                with e.Fori(0, NB) as b:
                    c.enter(b, 2)
                    c.wait()
                    c(V.tensor_scalar(mask, bkt, iota26[:, bass.ds(b, 1)], None, ALU.is_equal))
                    c.wait()
                    c(V.tensor_reduce(cnt[:, bass.ds(b, 1)], mask, AX.X, ALU.add))
                c.leave(NB)
                c.wait()
                e.drain().then_inc(S(f"s_cnt_{k}"), 1)
                e.wait_ge(S(f"s_tot_{k}"), 1)
                c(V.tensor_copy(tot, ps[:, 0, 0:NB]))
                c(V.tensor_copy(offs, ps[:, 1, 0:NB]))
                c.wait()
                c(V.tensor_scalar(tot_i, tot, float(ME - 1), None, ALU.add))
                c.wait()
                c(V.tensor_scalar(tot_i, tot_i, ME.bit_length() - 1, None, ALU.arith_shift_right))
                c.wait()
                c(V.tensor_copy(mac, tot_i))
                c.wait()
                c(V.tensor_tensor_scan(inc, mac, zero26, 0.0, ALU.add, ALU.add))
                c.wait()
                c(V.tensor_tensor(mac, inc, mac, ALU.subtract))
                c.wait()
                c(V.scalar_tensor_tensor(offs, mac, float(ME), offs, ALU.mult, ALU.add))
                c.wait()
                c(V.tensor_scalar(offs, offs, 1.0, None, ALU.subtract))
                jf = jcmp[:, NMA:2 * NMA]
                wide = oh_wide[:, 0:NMA * NB].rearrange("p (m b) -> p m b", b=NB)
                c(V.tensor_tensor(wide, bcast(jcmp[:, 0:NMA], 2, [1, NMA, NB]),
                                  bcast(inc[0:1, :], 1, [1, NMA, NB]), ALU.is_ge))
                c.wait()
                c(V.tensor_reduce(jf, wide, AX.X, ALU.add))
                c.wait()
                c(V.tensor_scalar(jmap[k][:, :], jf, float(NB - 1), None, ALU.min))
                with e.Fori(0, NB) as b:
                    c.enter(b, 4)
                    c.wait()
                    c(V.tensor_scalar(mask, bkt, iota26[:, bass.ds(b, 1)], None, ALU.is_equal))
                    c.wait()
                    c(V.tensor_tensor_scan(scan, mask, zero, offs[:, bass.ds(b, 1)], ALU.add, ALU.add))
                    c.wait()
                    c(V.tensor_tensor(scan, scan, mask, ALU.mult))
                    c.wait()
                    c(V.tensor_tensor(pos, pos, scan, ALU.add))
                c.leave(NB)
                c.wait()
                V.tensor_copy(pos_i, pos).then_inc(S(f"s_pos_{k}"), 1)

            def totals(e):
                e.wait_ge(S(f"s_cnt_{k}"), 1)
                T.matmul(ps[:, 0, 0:NB], ones[:, :], cnt, start=True, stop=True)
                T.matmul(ps[:, 1, 0:NB], tri[:, :], cnt, start=True, stop=True).then_inc(S(f"s_tot_{k}"), 1)

            return load, place, totals

        def write_by_dst():
            slot_of = [S(f"s_put_d{h}") for h in range(2)]
            rr = ring[:, 0:2 * RH * WD].rearrange("p (h t w) -> p h t w", h=2, t=RH)
            pos_i = slots["d"]
            parts = ((0, idxs["d"]), (1, rels["d"]), (2, ew))

            def fill_ring(e):
                c = Chain(e, S("c_ring_d"))
                c(A.activation(ring[:, 0:2 * RH * WD], zero[:, 0:2 * RH * WD], ACT.Copy))
                c.wait()
                e.wait_ge(S("s_pos_d"), 1)

                def turn(i, at_i):
                    for h in range(2):
                        if at_i is not None:
                            e.wait_ge(slot_of[h], at_i * (16 * RH) + 16 * RH)
                        at = i * (2 * RH) + h * RH
                        for w, col in parts:
                            o = rr[:, h, :, w]
                            if w == 0:
                                o = o.bitcast(I32)
                            A.activation(o, col[:, bass.ds(at, RH)], ACT.Copy).then_inc(S("s_ring_d"), 1)
                        A.activation(pring[:, h * RH:(h + 1) * RH], pos_i[:, bass.ds(at, RH)], ACT.Copy)\
                            .then_inc(S("s_ring_d"), 1)

                turn(0, None)
                with e.Fori(0, EC // (2 * RH) - 1) as i:
                    turn(i + 1, i)

            def scatter(e):
                per = len(parts) + 1
                with e.Fori(0, EC // (2 * RH)) as i:
                    for h in range(2):
                        e.wait_ge(S("s_ring_d"), i * (2 * per) + (h + 1) * per)
                        e.sem_inc(S("s_gp"), 1)
                        for t in range(RH):
                            e.indirect_dma_start(
                                out=recs["d"], out_offset=bass.IndirectOffsetOnAxis(
                                    ap=pring[:, h * RH + t:h * RH + t + 1], axis=0),
                                in_=rr[:, h, t, :], in_offset=None).then_inc(slot_of[h], 16)
                for h in range(2):
                    e.wait_ge(slot_of[h], 16 * RH * (EC // (2 * RH)))
                    e.sem_inc(S("s_gp"), 1)

            return fill_ring, scatter

        def write_by_src():
            group = EC // (NM // U) // 2
            assert group * 2 * (NM // U) == EC and 2 * group * WS <= 2 * D
            put = [S(f"s_put_s{g}") for g in range(2)]
            filled = [S(f"s_ring_s{g}") for g in range(2)]
            came = [S(f"s_attr_s{g}") for g in range(2)]
            rr = wts[:, 0:2 * group * WS].rearrange("p (g t w) -> p g t w", g=2, t=group)
            pr = rows[:, 128:128 + 2 * group].bitcast(I32)
            n = 16 * group

            def attrs(e, i, g, before=None):
                if before is not None:
                    e.wait_ge(put[g], before)
                    e.sem_inc(S("s_sp"), 1)
                for w0, w1, name in ((2, 6, "edge_attr_4"), (6, 14, "edge_attr_8")):
                    e.dma_start(rr[:, g, :, w0:w1], io[name][:, bass.ds(i, group), :]).then_inc(came[g], 16)

            def fill(e, i, g, before=None):
                if before is not None:
                    e.wait_ge(put[g], before)
                for w in range(2):
                    A.activation(rr[:, g, :, w], by_src[:, w, bass.ds(i, group)], ACT.Copy)\
                        .then_inc(filled[g], 1)
                A.activation(pr[:, g * group:(g + 1) * group], by_src[:, 2, bass.ds(i, group)].bitcast(I32), ACT.Copy)\
                    .then_inc(filled[g], 1)

            def ahead(fn):
                def go(e, i, u):
                    if u >= 2:
                        g = u - 2
                        at = e.snap(i * (2 * group) + (2 + g) * group)
                        fn(e, at, g, i * n + n)
                return go

            def write(e, i, u):
                if u >= 2:
                    return
                e.wait_ge(filled[u], i * 3 + 3)
                e.sem_inc(S("s_gp"), 1)
                e.wait_ge(came[u], i * 32 + 32)
                e.sem_inc(S("s_gp"), 1)
                for t in range(group):
                    e.indirect_dma_start(
                        out=recs["s"], out_offset=bass.IndirectOffsetOnAxis(
                            ap=pr[:, u * group + t:u * group + t + 1], axis=0),
                        in_=rr[:, u, t, :], in_offset=None).then_inc(put[u], 16)

            def written(e):
                for g in range(2):
                    e.wait_ge(put[g], n * (NM // U))
                    e.sem_inc(S("s_gp"), 1)

            def first(fn):
                return lambda e: [fn(e, g * group, g) for g in range(2)]

            return dict(sync=(first(attrs), ahead(attrs), lambda e: [e.wait_ge(came[g], 32 * (NM // U + 1)) for g in range(2)]),
                        scalar=(first(fill), ahead(fill), None),
                        gpsimd=(None, write, written))

        oh_wide = gat[0:1, :, :, :].rearrange("p a b c -> p (a b c)")
        load, place, totals = sort("d")
        phase(sync=load, vector=place, tensor=totals)
        fill_ring, scatter = write_by_dst()
        load, place, totals = sort("s")
        phase(sync=load, vector=place, tensor=totals, scalar=fill_ring, gpsimd=scatter)

        work = sb("work", [P, 3072])
        xs = work[:, 0:1024].rearrange("p (u c) -> p u c", u=2)
        xt = work[:, 1024:2048].rearrange("p (u c) -> p u c", u=2)
        stage = work[:, 2048:3072].rearrange("p (u c) -> p u c", u=2)

        def stages(tag, *names, credit=CREDIT):
            made = {}
            for n in names:
                made[n] = sem(f"{tag}_{n}")
                credits.append((made[n], credit))
            return made

        def row_bcast(src):
            return src.partition_broadcast(P)

        tile_sems = stages("tile", "copy", "turn", "xt", "mm", "evac")
        s_w = sem("tile_w")
        s_out = [sem(f"tile_out{u}") for u in range(2)]
        credits += [(one, 1) for one in s_out]
        s_ready = sem("tile_ready")
        rounds = {"all": 0, "out": 0, "loads": 0}

        def project(tag, n_chunks, zin, loads, groups, evac, out_dma=None, prepare=None, prep_ws=None):
            s, before = tile_sems, NB * rounds["all"]
            kept = NB * rounds["out"]
            rounds["all"] += 1
            rounds["out"] += out_dma is not None
            ready = rounds["all"]
            rounds["loads"] += 16 * len(loads)
            loaded = rounds["loads"]
            wide = n_chunks * P

            def load(e):
                for dst_ap, src_ap in loads:
                    e.dma_start(dst_ap, src_ap).then_inc(s_w, 16)
                if out_dma is not None:
                    with e.Fori(0, NB // 2) as i:
                        for u in range(2):
                            m = Macro(i, u, before, 2)
                            at = e.snap(m.index())
                            e.wait_ge(s["evac"], m.done())
                            e.sem_inc(S("s_sp"), 1)
                            out_dma(e, at, stage[:, u, :]).then_inc(s_out[u], 16)
                    for u in range(2):
                        e.wait_ge(s_out[u], 8 * (NB + kept) + 1)

            def copies(e):
                e.wait_ge(s_ready, ready)
                with e.Fori(0, NB // 2) as i:
                    for u in range(2):
                        m = Macro(i, u, before, 2)
                        e.wait_ge(s["turn"], m.done(2))
                        G.tensor_copy(xs[:, u, 0:wide], zin[:, bass.ds(m.index(), 1), 0:wide])\
                            .then_inc(s["copy"], 1)

            def tensor(e):
                e.wait_ge(s_w, loaded)
                e.wait_ge(s_ready, ready)
                with e.Fori(0, NB // 2) as i:
                    for u in range(2):
                        m = Macro(i, u, before, 2)
                        e.wait_ge(s["copy"], m.done())
                        e.wait_ge(s["xt"], m.done(2))
                        for c in range(n_chunks):
                            last = T.transpose(ps[:, u, c * P:(c + 1) * P], xs[:, u, c * P:(c + 1) * P],
                                               ident[:, :])
                        last.then_inc(s["turn"], 1)
                        e.wait_ge(s["xt"], m.done())
                        e.wait_ge(s["evac"], m.done(2))
                        for b, c0, c1, terms in groups:
                            for n, (c, w) in enumerate(terms):
                                last = T.matmul(ps[:, 2 + 2 * u + b, c0:c1], xt[:, u, c * P:(c + 1) * P], w,
                                                start=(n == 0), stop=(n == len(terms) - 1))
                        last.then_inc(s["mm"], 1)

            def scalar(e):
                with e.Fori(0, NB // 2) as i:
                    for u in range(2):
                        m = Macro(i, u, before, 2)
                        e.wait_ge(s["turn"], m.done())
                        e.wait_ge(s["mm"], m.done(2))
                        A.activation(xt[:, u, 0:wide], ps[:, u, 0:wide], ACT.Copy).then_inc(s["xt"], 1)

            def vector(e):
                c = vchain(e)
                if prepare:
                    prepare(e, c)
                e.wait_ge(s_w, loaded)
                if prep_ws:
                    prep_ws(e, c)
                c.wait()
                e.sem_inc(s_ready, 1)
                with e.Fori(0, NB // 2) as i:
                    for u in range(2):
                        m = Macro(i, u, before, 2)
                        e.wait_ge(s["mm"], m.done())
                        if out_dma is not None:
                            e.wait_ge(s_out[u], Macro(i, u, kept, 2).turns(16, 1) + 1)
                        evac(e, m, ps[:, 2 + 2 * u:4 + 2 * u, :], stage[:, u, :]).then_inc(s["evac"], 1)

            phase(sync=load, gpsimd=copies, tensor=tensor, scalar=scalar, vector=vector)

        def store_rows(table, width):
            def go(e, m, src):
                t = table.rearrange("(j p) c -> j p c", p=P)
                return e.dma_start(t[bass.ds(m, 1)].rearrange("a p c -> p (a c)"), src[:, 0:width])
            return go

        junk = acc_raw[:, :, 0:D]

        def rstd(e, c, s_act, n, stat, scale, tmp):
            c(V.tensor_scalar(tmp, stat, scale, LN_EPS, ALU.mult, ALU.add))
            c.wait()
            e.sem_inc(s_act[0], 1)
            e.wait_ge(s_act[1], n)
            c(V.reciprocal(stat, tmp))
            c.wait()

        def layernorm(tag, before=None, after=None, roots=()):
            s_act = (sem(f"{tag}_go"), sem(f"{tag}_root"))
            mean = small[:, 0:NB]
            var = small[:, 32:32 + NB]
            tmp = small[:, 64:64 + NB]
            todo = list(roots) + [tmp]

            def vector(e):
                c = vchain(e)
                n = 0
                if before:
                    n = before(e, c, s_act)
                x = x_sb[:, :, :]
                c(V.tensor_reduce(mean, x, AX.X, ALU.add))
                c.wait()
                c(V.tensor_scalar(mean, mean, 1.0 / D, None, ALU.mult))
                c.wait()
                c(V.tensor_tensor(x, x, bcast(mean, 2, [P, NB, D]), ALU.subtract))
                c.wait()
                c(V.tensor_tensor(junk, x, x, ALU.mult))
                c.wait()
                c(V.tensor_reduce(var, junk, AX.X, ALU.add))
                c.wait()
                rstd(e, c, s_act, n + 1, var, 1.0 / D, tmp)
                c(V.tensor_tensor(x, x, bcast(var, 2, [P, NB, D]), ALU.mult))
                c.wait()
                if after:
                    after(e, c)

            def scalar(e):
                for n, t in enumerate(todo):
                    e.wait_ge(s_act[0], n + 1)
                    A.activation(t, t, ACT.Sqrt).then_inc(s_act[1], 1)

            return vector, scalar

        def macro_loops(ahead, first, body, after=None, start=0, side=None):
            def go(e):
                for m in range(ahead):
                    first(e, Macro(0, m))
                if side and side[0]:
                    side[0](e)
                for m in range(start):
                    body(e, lambda lag, m=m: Macro(0, m + lag))
                with e.Fori(0, NM // U) as i:
                    for u in range(U):
                        body(e, lambda lag, i=i, u=u + start: Macro(i, u + lag))
                        if side:
                            side[1](e, i, u)
                if side and side[2]:
                    side[2](e)
                if after:
                    after(e)
            return go

        iota4 = bcast(iota[:, :], 1, [P, Q, P])

        def attention(L, k, table):
            timed = L == 0
            only = ("ln", "mt", "dg", "mb", "td", "tx", "warm") if timed else ("s3", "st", "sp", "me")
            s = stages(f"a{L}", "oh", "tr", "oht", "qx", "prod", "mq", "f", "ef", "p", "pv", "sum", "flush", *only)
            if not timed:
                s_hm, s_hr = sem(f"a{L}_hm"), sem(f"a{L}_hr")
                credits.append((s_hr, 3))
            s_rec = [sem(f"a{L}_rec{u}") for u in range(U)]
            s_gat = [sem(f"a{L}_gat{u}") for u in range(U)]
            s_go = sem(f"a{L}_go")
            cB = sem(f"a{L}_cB")
            AHEAD = 3
            START = 1
            side = write_by_src() if timed else {}
            acc = acc_raw[:, :, 0:AC]
            r_sb = rec[k]
            oht = xs
            prod = big[:, 0:Q * D].rearrange("p (q c) -> p q c", q=Q)
            pvb = big[:, Q * D:Q * D + 2 * Q * AC].rearrange("p (u q c) -> p u q c", u=2, q=Q)
            col = lambda a, n: small[:, a:a + n]
            v4 = lambda a: a.rearrange("p (q h) -> p q h", q=Q)
            td, ab, sg, ln = (col(a, 4) for a in (0, 4, 8, 12))
            sc, t1, t2, sm = (col(a, 32) for a in (32, 64, 96, 128))
            ff = [col(a, 8) for a in (184, 416)]
            mq, mn, dd, mx = (col(a, 8) for a in (160, 168, 176, 192))
            mr = small[0:H, 200:201]
            warm = small[:, 280:281]
            dg = small[0:H, 208:216]
            r1 = col(224, 32)
            s3 = small[:, 288:336].bitcast(BF16)
            st3 = small[:, 336:400].bitcast(BF16)
            nh = [work[:, c:c + 256].bitcast(BF16) for c in (2048, 1024)]
            sel = small[:, 400:416].bitcast(BF16)
            bigI = work[:, 2304:2368].bitcast(BF16)
            identb = work[:, 2368:2432].bitcast(BF16)
            w0, w1, bt4 = rows[:, 0:8], rows[:, 8:16], rows[:, 16:48]
            bank7 = ps[:, 7, :]
            psQ = [ps[:, 1 + 2 * v * timed:3 + 2 * v * timed, :].rearrange("p b c -> p (b c)")
                   for v in range(2)]
            psO = [ps[:, 5 + v if timed else 3, 0:AC] for v in range(2)]
            times = bank7[:, 280:280 + 3 * Q].rearrange("p (q t) -> p q t", t=3)
            tp = rows[:, 64:64 + 3 * NB // 2].bitcast(BF16).rearrange("p (j t) -> p j t", t=3)
            tps = small[:, 256:268].rearrange("p (q t) -> p q t", t=3)
            turned = ps[:, 0, 0:Q * P // 2].bitcast(BF16)
            q_lag, o_lag = (2, 2) if timed else (1, 1)
            r = recs[k].rearrange("(m p q) w -> m p (q w)", p=P, q=Q)

            def sync_a(e, m):
                at = e.snap(m.index())
                e.wait_ge(s["mq" if timed else "prod"], m.done(U))
                e.sem_inc(S("s_sp"), 1)
                e.dma_start(r_sb[:, m.u, :, :].rearrange("p q w -> p (q w)"),
                            r[bass.ds(at, 1)].rearrange("a p c -> p (a c)")).then_inc(s_rec[m.u], 16)

            def sync(e):
                if timed:
                    wt = io["L0_gnn_Wt"]
                    e.dma_start(w0, row_bcast(wt[0])).then_inc(S("s_wt"), 16)
                    e.dma_start(w1, row_bcast(wt[1])).then_inc(S("s_wt"), 16)
                    for q in range(Q):
                        e.dma_start(bt4[:, q * H:(q + 1) * H], row_bcast(io["L0_gnn_bt"])).then_inc(S("s_wt"), 16)
                    e.dma_start(deg[:, :], io["node_vec"]).then_inc(S("s_wt"), 16)
                if timed:
                    e.wait_ge(s_go, 1)
                macro_loops(AHEAD, sync_a, lambda e, M: sync_a(e, M(AHEAD)), start=START, side=side.get("sync"))(e)

            def pool_a(e, m):
                e.wait_ge(s_rec[m.u], m.turns(16))
                e.sem_inc(S("s_gp"), 1)
                e.wait_ge(s["pv"], m.done(U))
                e.sem_inc(S("s_gp"), 1)
                for q in range(Q):
                    e.indirect_dma_start(
                        out=gat[:, m.u, q, :], out_offset=None, in_=table,
                        in_offset=bass.IndirectOffsetOnAxis(ap=r_sb[:, m.u, q, 0:1].bitcast(I32), axis=0),
                    ).then_inc(s_gat[m.u], 16)

            def pool(e):
                side_work = side.get("gpsimd")
                if timed:
                    macro_loops(AHEAD, pool_a, lambda e, M: pool_a(e, M(AHEAD)), start=START, side=side_work)(e)
                else:
                    def turn(e, M):
                        pool_a(e, M(AHEAD))
                        e.wait_ge(s_gat[M(0).u], M(0).turns(64))
                        weight_values(e, M(0), G)
                    macro_loops(AHEAD, pool_a, turn, start=START)(e)

            def transposes(e, m):
                e.wait_ge(s["oh"], m.done())
                e.wait_ge(s["oht"], m.done(1))
                for q in range(Q):
                    last = T.transpose(turned[:, q * P:(q + 1) * P], top(oh[:, m.u, q, :]), identb)
                last.then_inc(s["tr"], 1)

            def queries(e, m, some=range(Q), j=None):
                j = bucket(e, m) if j is None else j
                if some[0] == 0:
                    e.wait_ge(s["oht"], m.done())
                    e.wait_ge(s["prod"], m.done(q_lag))
                for q in some:
                    o = top(oht[:, m.v, q * P:(q + 1) * P])
                    to = psQ[m.v][:, q * D:(q + 1) * D]
                    T.matmul(to, o, qp[:, bass.ds(j, 1), 0:D], start=True, stop=False)
                    T.matmul(to, o, qp[:, bass.ds(j, 1), D:2 * D], start=False, stop=False)
                    last = T.matmul(to, o, top(qz[:, bass.ds(j, 1), :]), start=False, stop=True)
                if some[-1] == Q - 1:
                    last.then_inc(s["qx"], 1)

            def node_times(e, m):
                j = bucket(e, m)
                e.wait_ge(s["oht"], m.done())
                e.wait_ge(s["td"], m.done(1))
                e.wait_ge(s["f"], m.done(2))
                for q in range(Q):
                    last = T.matmul(times[:, q, :], top(oht[:, m.v, q * P:(q + 1) * P]), tp[:, bass.ds(j, 1), :],
                                    start=True, stop=True)
                last.then_inc(s["tx"], 1)

            def maxima(e, m, z=None, ahead=None):
                if timed:
                    e.wait_ge(s["mq"], m.done())
                    T.transpose(bank7[0:H, 16:16 + P], mq, ident[:, :]).then_inc(s["mt"], 1)
                    if z:
                        sums(e, z, range(2))
                    e.wait_ge(s["dg"], m.done())
                    T.matmul(bank7[:, 144:144 + H], ones[0:H, :], dg, start=True, stop=True).then_inc(s["mb"], 1)
                else:
                    j = bucket(e, ahead)
                    e.wait_ge(s["s3"], m.done())
                    T.transpose(bank7[0:96, 192:256].bitcast(BF16), s3, identb).then_inc(s["st"], 1)
                    e.wait_ge(s["sp"], m.done())
                    for h in range(H):
                        e.wait_ge(s_hr, m.i * (U * H) + (m.off * H + h + 1))
                        node_scores(h, 4 + h % 3, m.v)
                        if h % 2:
                            queries(e, ahead, range(h // 2, h // 2 + 1), j)
                    e.wait_ge(s["mq"], m.done())
                    for q in range(Q):
                        last = T.matmul(bank7[:, 152 + q * H:160 + q * H], oht[:, m.v, q * P:(q + 1) * P], mn,
                                        start=True, stop=True)
                    last.then_inc(s["me"], 1)

            def sums(e, m, some=range(Q)):
                if some[0] == 0:
                    e.wait_ge(s["p"], m.done())
                    e.wait_ge(s["pv"], m.done())
                    e.wait_ge(s["flush"], m.done(o_lag))
                for q in some:
                    last = T.matmul(psO[m.v], oh[:, m.u, q, :], pvb[:, m.v, q, :], start=(q == 0), stop=(q == Q - 1))
                if some[-1] == Q - 1:
                    last.then_inc(s["sum"], 1)

            def node_scores(h, b, v):
                for q in range(Q):
                    c = q * H + h
                    T.matmul(ps[:, b, q * P:(q + 1) * P], sel[0:96, c:c + 1].to_broadcast([96, P]),
                             st3[0:96, :], start=(q == 0), stop=False)
                T.matmul(ps[:, b, :], bigI, nh[v], start=False, stop=True).then_inc(s_hm, 1)

            def tensor(e):
                e.wait_ge(s_go, 1)
                transposes(e, Macro(0, 0))
                if timed:
                    node_times(e, Macro(0, 0))
                queries(e, Macro(0, 0))
                transposes(e, Macro(0, 1))
                if timed:
                    node_times(e, Macro(0, 1))
                if timed:
                    queries(e, Macro(0, 1))
                    maxima(e, Macro(0, 0))
                    transposes(e, Macro(0, 2))
                    node_times(e, Macro(0, 2))
                    queries(e, Macro(0, 2))
                else:
                    maxima(e, Macro(0, 0), ahead=Macro(0, 1))
                    transposes(e, Macro(0, 2))

                def turn(e, M):
                    if timed:
                        maxima(e, M(1), M(0))
                        sums(e, M(0), range(2, 3))
                        transposes(e, M(3))
                        sums(e, M(0), range(3, Q))
                        node_times(e, M(3))
                        queries(e, M(3))
                    else:
                        maxima(e, M(1), ahead=M(2))
                        transposes(e, M(3))
                        sums(e, M(0))
                macro_loops(0, None, turn, start=START)(e)

            def evac(e, m):
                e.wait_ge(s["tr"], m.done())
                e.wait_ge(s["qx"] if timed else s["me"], m.done(2))
                if not timed:
                    A.activation(nh[m.v], turned, ACT.Identity, scale=-1.0, bias=1.0)
                A.activation(oht[:, m.v, :], turned, ACT.Copy).then_inc(s["oht"], 1)

            def log_times(e, m):
                e.wait_ge(s["td"], m.done())
                A.activation(ln, ab, ACT.Ln, scale=1.0 / 3600.0, bias=1.0).then_inc(s["ln"], 1)

            def preload(e, m):
                e.wait_ge(s["warm"], m.done(1))
                A.activation(warm, ones[:, 0:1], ACT.Exp).then_inc(s["warm"], 1)

            def act(e, m):
                if not timed:
                    e.wait_ge(s["st"], m.done())
                    A.activation(st3[0:96, :], bank7[0:96, 192:256].bitcast(BF16), ACT.Copy).then_inc(s["sp"], 1)
                e.wait_ge(s["f"], m.done())
                e.wait_ge(s["sum"], m.done(2))
                A.activation(pvb[:, m.v, :, :].rearrange("p q (h c) -> p q h c", c=HC)[:, :, :, DH],
                             v4(sm), ACT.Exp).then_inc(s["p"], 1)
                A.activation(ff[m.v], dd, ACT.Exp).then_inc(s["ef"], 1)

            def scalar(e):
                e.wait_ge(s_go, 1)
                evac(e, Macro(0, 0))
                evac(e, Macro(0, 1))
                if timed:
                    log_times(e, Macro(0, 0))
                    preload(e, Macro(0, 0))
                    evac(e, Macro(0, 2))
                    act(e, Macro(0, 0))
                    log_times(e, Macro(0, 1))
                else:
                    act(e, Macro(0, 0))
                    evac(e, Macro(0, 2))

                def turn(e, M):
                    if timed:
                        preload(e, M(1))
                        evac(e, M(3))
                        act(e, M(1))
                        log_times(e, M(2))
                    else:
                        act(e, M(1))
                        evac(e, M(3))
                macro_loops(0, None, turn, start=START, side=side.get("scalar"))(e)

            def one_hot(e, m, q):
                if q == 0:
                    e.wait_ge(s_rec[m.u], m.turns(16))
                    e.wait_ge(s["sum"], m.done(U))
                ins = V.tensor_scalar(oh[:, m.u, q, :], iota[:, :], r_sb[:, m.u, q, 1:2], None, ALU.is_equal)
                if q == Q - 1:
                    ins.then_inc(s["oh"], 1)

            def bucket(e, m):
                return e.value_load(jmap[k][0:1, bass.ds(m.index(), 1)], min_val=0, max_val=NB - 1)

            def times_1(c, e, b):
                e.wait_ge(s["tx"], b.done())
                k = c(V.tensor_reduce(tps[:, :, 0], times, AX.X, ALU.add))
                yield
                c.wait(k)
                k = c(V.tensor_tensor(td, r_sb[:, b.u, :, 2], tps[:, :, 0], ALU.subtract))
                yield
                c.wait(k)
                k = c(V.tensor_scalar(sg, td, 0.0, -1.0, ALU.is_gt, ALU.add))
                yield
                c.wait(k)
                k = c(V.scalar_tensor_tensor(sg, td, 0.0, sg, ALU.is_ge, ALU.add))
                yield
                c.wait(k)
                V.tensor_tensor(ab, td, sg, ALU.mult).then_inc(s["td"], 1)
                k = c(V.tensor_tensor(v4(t1), bcast(sg, 2, [P, Q, H]), bcast(w0, 1, [P, Q, H]), ALU.mult))
                yield
                c.wait(k)
                k = c(V.tensor_tensor(t1, t1, bt4, ALU.add))
                yield
                c.wait(k)
                c(V.tensor_tensor(v4(t1), v4(t1), bcast(r_sb[:, b.u, :, 3], 2, [P, Q, H]), ALU.add))
                yield

            def score_timed(c, e, a, z, nxt, b, y):
                e.wait_ge(s["qx"], a.done())
                multiply(e, a)
                jy = bucket(e, y) if y else None
                if z:
                    weight_values(e, z)
                e.wait_ge(s["prod"], a.done())
                k_sc = c(V.tensor_reduce(sc, prod.rearrange("p q (h c) -> p (q h) c", c=DH), AX.X, ALU.add))
                more = times_1(c, e, b)
                next(more)
                e.wait_ge(s["ln"], a.done())
                k2 = c(V.tensor_tensor(v4(t2), bcast(ln, 2, [P, Q, H]), bcast(w1, 1, [P, Q, H]), ALU.mult))
                if y:
                    k_fl = rescale(c, e, y, jy)
                c.wait(k2)
                k1 = c(V.tensor_tensor(t1, t1, t2, ALU.add))
                c.wait(k1)
                k_sc = c(V.scalar_tensor_tensor(sc, sc, DH ** -0.5, t1, ALU.mult, ALU.add))
                c.wait(k_sc)
                V.tensor_reduce(mq, sc.rearrange("p (q h) -> p h q", q=Q), AX.X, ALU.max).then_inc(s["mq"], 1)
                if y:
                    add_sums(c, e, y, jy, k_fl)
                ja = bucket(e, a)
                one_hot(e, nxt, 0)
                next(more)
                e.wait_ge(s["mt"], a.done())
                k_mr = c(V.tensor_reduce(mr, bank7[0:H, 16:16 + P], AX.X, ALU.max))
                next(more)
                one_hot(e, nxt, 1)
                c.wait(k_mr)
                V.tensor_scalar(dg, ident[0:H, 0:H], mr, None, ALU.mult).then_inc(s["dg"], 1)
                next(more)
                one_hot(e, nxt, 2)
                next(more)
                mj = m_run[:, bass.ds(ja, 1), :]
                e.wait_ge(s["mb"], a.done())
                k_mn = c(V.tensor_tensor(mn, mj, bank7[:, 144:144 + H], ALU.max))
                one_hot(e, nxt, 3)
                c.wait(k_mn)
                c(V.tensor_tensor(v4(sm), v4(sc), bcast(mn, 1, [P, Q, H]), ALU.subtract))
                k_dd = c(V.tensor_tensor(dd, mj, mn, ALU.subtract))
                next(more)
                c.wait(k_dd)
                V.tensor_scalar(mj, mn, 1.0, None, ALU.mult).then_inc(s["f"], 1)
                next(more)

            def score_plain(c, e, a, _z, nxt, _b, y):
                e.wait_ge(s["qx"], a.done())
                multiply(e, a)
                jy = bucket(e, y) if y else None
                e.wait_ge(s["prod"], a.done())
                k_sc = c(V.tensor_reduce(sc, prod.rearrange("p q (h c) -> p (q h) c", c=DH), AX.X, ALU.add))
                one_hot(e, nxt, 0)
                c.wait(k_sc)
                k = c(V.tensor_copy(s3[:, 0:32], sc))
                one_hot(e, nxt, 1)
                c.wait(k)
                k = c(V.tensor_tensor(r1, sc, s3[:, 0:32], ALU.subtract))
                one_hot(e, nxt, 2)
                c.wait(k)
                k = c(V.tensor_copy(s3[:, 32:64], r1))
                one_hot(e, nxt, 3)
                c.wait(k)
                V.tensor_tensor(s3[:, 64:96], r1, s3[:, 32:64], ALU.subtract).then_inc(s["s3"], 1)
                ja = bucket(e, a)
                if y:
                    k_fl = rescale(c, e, y, jy)
                for h in range(H):
                    e.wait_ge(s_hm, a.i * (U * H) + (a.off * H + h + 1))
                    V.tensor_reduce(mx[:, h:h + 1], ps[:, 4 + h % 3, :], AX.X, ALU.max)\
                        .then_inc(s_hr, 1)
                mj = m_run[:, bass.ds(ja, 1), :]
                e.wait_ge(s_hr, a.i * (U * H) + (a.off * H + H + 3))
                V.tensor_tensor(mn, mj, mx, ALU.max).then_inc(s["mq"], 1)
                if y:
                    add_sums(c, e, y, jy, k_fl)
                e.wait_ge(s["mq"], a.done())
                k_dd = c(V.tensor_tensor(dd, mj, mn, ALU.subtract))
                e.wait_ge(s["me"], a.done())
                c(V.tensor_tensor(v4(sm), v4(sc), v4(bank7[:, 152:184]), ALU.subtract))
                c.wait(k_dd)
                V.tensor_scalar(mj, mn, 1.0, None, ALU.mult).then_inc(s["f"], 1)

            def multiply(e, m):
                e.wait_ge(s_gat[m.u], m.turns(64))
                V.tensor_tensor(prod, psQ[m.v].rearrange("p (q c) -> p q c", q=Q), gat[:, m.u, :, 0:D],
                                ALU.mult).then_inc(s["prod"], 1)

            def weight_values(e, m, engine=V):
                e.wait_ge(s["p"], m.done())
                pw = pvb[:, m.v, :, :].rearrange("p q (h c) -> p q h c", c=HC)
                gv = gat[:, m.u, :, D:2 * D].rearrange("p q (h c) -> p q h c", c=DH)
                engine.tensor_tensor(pw[:, :, :, 0:DH], gv, pw[:, :, :, DH:HC].to_broadcast([P, Q, H, DH]),
                                ALU.mult).then_inc(s["pv"], 1)

            def rescale(c, e, m, j):
                aj = acc[:, bass.ds(j, 1), :].rearrange("p a (h c) -> p (a h) c", c=HC)
                e.wait_ge(s["ef"], m.done())
                e.wait_ge(s["flush"], m.done(1))
                return c(V.tensor_tensor(aj, aj, bcast(ff[m.v], 2, [P, H, HC]), ALU.mult))

            def add_sums(c, e, m, j, k_fl):
                aj = acc[:, bass.ds(j, 1), :].rearrange("p a (h c) -> p (a h) c", c=HC)
                c.wait(k_fl)
                e.wait_ge(s["sum"], m.done())
                V.tensor_tensor(aj, aj, psO[m.v].rearrange("p (h c) -> p h c", c=HC), ALU.add).then_inc(s["flush"], 1)

            def dve(e):
                c = vchain(e)
                c(V.memset(acc, 0.0))
                c(V.memset(m_run[:, :, :], NEG))
                c(V.tensor_copy(identb, ident[:, :]))
                if not timed:
                    c(V.tensor_scalar(qz[:, :, :], qz[:, :, :], DH ** -0.5, None, ALU.mult))
                for part in range(2):
                    c.wait()
                    c(V.tensor_copy(qp[:, :, part * D:(part + 1) * D], qz[:, :, :]))
                    c.wait()
                    c(V.tensor_tensor(qz[:, :, :], qz[:, :, :], qp[:, :, part * D:(part + 1) * D], ALU.subtract))
                if timed:
                    e.sem_inc(S("c_nv"), 1)
                    c(V.memset(wts[:, :], 0.0))
                    e.wait_ge(S("s_wt"), 16 * 7)
                    left = small[:, 0:NB]
                    c(V.tensor_copy(tp[:, :, 0], deg[:, :]))
                    c.wait()
                    c(V.tensor_tensor(left, deg[:, :], tp[:, :, 0], ALU.subtract))
                    c.wait()
                    c(V.tensor_copy(tp[:, :, 1], left))
                    c.wait()
                    c(V.tensor_tensor(tp[:, :, 2], left, tp[:, :, 1], ALU.subtract))
                else:
                    c(V.tensor_scalar(bigI, ident[:, :], NEG, None, ALU.mult))
                    for b in range(3):
                        c(V.tensor_copy(sel[32 * b:32 * b + 32, :], ident[32 * b:32 * b + 32, 32 * b:32 * b + 32]))
                c.wait()
                e.sem_inc(s_go, 1)
                score = score_timed if timed else score_plain
                cc = Chain(e, cB)
                for m in range(AHEAD - 1):
                    for q in range(Q):
                        one_hot(e, Macro(0, m), q)
                if timed:
                    for _ in times_1(cc, e, Macro(0, 0)):
                        pass
                score(cc, e, Macro(0, 0), None, Macro(0, AHEAD - 1), Macro(0, 1), None)
                if START:
                    score(cc, e, Macro(0, 1), Macro(0, 0), Macro(0, 3), Macro(0, 2), None)
                first = cc.n
                per = cc_per[L]

                def turn(e, M):
                    c = Chain(e, cB)
                    z = M(START)
                    c.n = first + (z.off - START) * per
                    c.enter(z.i, U * per)
                    score(c, e, M(1 + START), z, M(AHEAD + START), M(2 + START), M(START - 1))
                    assert c.n - c.at == per, (L, c.n - c.at)
                macro_loops(0, None, turn)(e)

            phase(sync=sync, gpsimd=pool, scalar=scalar, tensor=tensor, vector=dve)

        cc_per = {0: 16, 2: 7}

        wk = wts[:, :].rearrange("p (c n) -> p c n", c=2)

        def halves(w):
            return w.rearrange("(c p) n -> p c n", p=P)

        def qkv(tag, L, table):
            loads = []
            for n, x in enumerate("qkv"):
                loads.append((wk[:, :, n * D:(n + 1) * D], halves(io[f"L{L}_gnn_W{x}"])))
                loads.append((rows[:, n * D:(n + 1) * D], row_bcast(io[f"L{L}_gnn_b{x}"])))
            groups = [(0, 0, D, [(c, wk[:, c, 0:D]) for c in range(2)]),
                      (1, 0, 2 * D, [(c, wk[:, c, D:3 * D]) for c in range(2)])]

            def evac(e, m, pp, st):
                V.tensor_tensor(qz[:, bass.ds(m.index(), 1), :], pp[:, 0, 0:D], rows[:, 0:D], ALU.add)
                return V.tensor_tensor(st, pp[:, 1, :], rows[:, D:3 * D], ALU.add)

            project(tag, 2, x_sb, loads, groups, evac, store_rows(table, 2 * D))

        def add_to_x(e, m, pp, st):
            xj = x_sb[:, bass.ds(m.index(), 1), :]
            return V.tensor_tensor(xj, xj, pp[:, 0, 0:D], ALU.add)

        def out_proj(tag, L, prepare=None):
            def prep(e, c):
                if prepare:
                    prepare(e, c)

            def bias(e, c):
                c(V.tensor_tensor(x_sb[:, :, :], x_sb[:, :, :], bcast(rows[:, 0:D], 1, [P, NB, D]), ALU.add))
            loads = [(wk[:, :, 0:D], halves(io[f"L{L}_gnn_Wo"])), (rows[:, 0:D], row_bcast(io[f"L{L}_gnn_bo"]))]
            project(tag, 2, qz, loads, [(0, 0, D, [(c, wk[:, c, 0:D]) for c in range(2)])], add_to_x,
                    prepare=prep, prep_ws=bias)

        acc4 = acc_raw[:, :, 0:AC].rearrange("p j (h c) -> p j h c", c=HC)
        qz4 = qz[:, :, :].rearrange("p j (h c) -> p j h c", c=DH)

        def softmax_over_edges():
            gmax = small[:, 0:H]
            F = big[:, 0:NT * H]
            Fv = F.rearrange("p (j h) -> p j h", h=H)
            den = big[:, NT * H:2 * NT * H].rearrange("p (j h) -> p j h", h=H)
            part = small[:, 8:16]
            rz = small[:, 16:24]

            def vector(e):
                c = vchain(e)
                c(V.tensor_reduce(gmax, m_run[:, 0:NT, :].rearrange("p j h -> p h j"), AX.X, ALU.max))
                c.wait()
                V.tensor_tensor(Fv, m_run[:, 0:NT, :], bcast(gmax, 1, [P, NT, H]), ALU.subtract).then_inc(S("n0_f"), 1)
                e.wait_ge(S("n0_e"), 1)
                c(V.tensor_tensor(den, acc4[:, 0:NT, :, DH], Fv, ALU.mult))
                c.wait()
                V.tensor_reduce(part, den.rearrange("p j h -> p h j"), AX.X, ALU.add).then_inc(S("n0_f"), 1)
                e.wait_ge(S("n0_z"), 1)
                c(V.reciprocal(rz, ps[:, 7, 0:H]))
                c.wait()
                c(V.tensor_tensor(Fv, Fv, bcast(rz, 1, [P, NT, H]), ALU.mult))
                c.wait()
                c(V.memset(qz[:, NT, :], 0.0))
                for h in range(H):
                    c(V.tensor_tensor(qz4[:, 0:NT, h, :], acc4[:, 0:NT, h, 0:DH],
                                      bcast(Fv[:, :, h], 2, [P, NT, DH]), ALU.mult))
                c.wait()

            def scalar(e):
                e.wait_ge(S("n0_f"), 1)
                A.activation(F, F, ACT.Exp).then_inc(S("n0_e"), 1)

            def tensor(e):
                e.wait_ge(S("n0_f"), 2)
                T.matmul(ps[:, 7, 0:H], ones[:, :], part, start=True, stop=True).then_inc(S("n0_z"), 1)

            phase(vector=vector, scalar=scalar, tensor=tensor)

        qkv("p0", 0, kv0)
        attention(0, "d", kv0)
        softmax_over_edges()
        out_proj("o0", 0)
        v_ln, a_ln = layernorm("l0")
        phase(vector=v_ln, scalar=a_ln)

        INV_SQRT3 = 3.0 ** -0.5
        y_scale = MUL ** -0.5

        def layer1():
            wy = wts[:, 0:2 * 2 * P].rearrange("p (c n) -> p c n", c=2)

            def w_blocks(c, sel_):
                return wy[:, c, sel_ * P:(sel_ + 1) * P]

            w_zero = sem("p1_zero")
            loads = []
            for c in range(2):
                for which, (ws, wv) in enumerate((("L1_gnn_w1_s", "L1_gnn_w1_v"), ("L1_gnn_wsc_s", "L1_gnn_wsc_v"))):
                    for half in range(2):
                        w = ws if c == 0 and half == 0 else wv
                        loads.append((w_blocks(c, which)[half * MUL:(half + 1) * MUL, half * MUL:(half + 1) * MUL],
                                      io[w]))
            groups = [(c, 0, 2 * P, [(c, wy[:, c, :])]) for c in range(2)]

            def split(e, c):
                c(V.tensor_copy(qz[:, :, 0:MUL], x_sb[:, :, 0:MUL]))
                for d in range(3):
                    c(V.tensor_copy(qz[:, :, (d + 1) * MUL:(d + 2) * MUL], x_sb[:, :, MUL + d::3]))
                c.wait()

            def evac(e, m, pp, st):
                V.tensor_scalar(qz[:, bass.ds(m.index(), 1), :].rearrange("p a (c n) -> p (a c) n", c=2),
                                pp[:, :, P:2 * P], y_scale, None, ALU.mult)
                return V.tensor_scalar(st[:, 0:D].rearrange("p (c n) -> p c n", c=2), pp[:, :, 0:P],
                                       y_scale, None, ALU.mult)

            def clear(e):
                V.memset(wts[:, 0:4 * P], 0.0).then_inc(w_zero, 1)
                e.wait_ge(w_zero, 1)

            phase(vector=clear)
            project("p1", 2, qz, loads, groups, evac, store_rows(y1, D), prepare=split)

            s = stages("e1", "oh", "tr", "at", "h1", "g1", "h2", "g2", "w", "wac", "wr", "msg", "sum", "flush")
            s_rec = [sem(f"e1_rec{u}") for u in range(U)]
            s_gat = [sem(f"e1_gat{u}") for u in range(U)]
            cB = sem("e1_cB")
            r_sb = rec["s"]
            fc1 = rows[0:8, 0:64]
            fc2 = rows[0:64, 64:128]
            fc3 = rows[0:64, 128:384]
            at = work[0:8, 0:512]
            h1 = work[0:64, 512:1024]
            h2 = work[0:64, 1024:1536]
            wac = work[:, 1536:2048].rearrange("p (q a n) -> p q a n", q=Q, a=2)
            wb = work[:, 2048:2304].rearrange("p (q n) -> p q n", q=Q)
            dot = work[:, 2304:2560].rearrange("p (q n) -> p q n", q=Q)
            g3 = gat[:, 1, 2:4, :].rearrange("p a b -> p (a b)")[:, 0:768].rearrange("p (q d n) -> p q d n", q=Q, d=3)
            rows_y = [gat[:, u, 0:2, :].rearrange("p a (b c) -> p (a b) c", c=D) for u in range(U)]
            msg = [big[:, u * 2048:(u + 1) * 2048].rearrange("p (q c h n) -> p q c h n", q=Q, c=4, h=2)
                   for u in range(2)]
            psW = ps[:, 3:5, :].rearrange("p b c -> p (b c)").rearrange("p (q k n) -> p q k n", q=Q, k=4)
            psDeg = [ps[:, 2, 0:1], ps[:, 7, 0:1]]
            acc = acc_raw[:, :, 0:2 * D]

            def sync_a(e, m):
                i = e.snap(m.index())
                e.wait_ge(s["msg"], m.done(U))
                e.sem_inc(S("s_sp"), 1)
                r = recs["s"].rearrange("(m p q) w -> m p (q w)", p=P, q=Q)
                e.dma_start(r_sb[:, m.u, :, :].rearrange("p q w -> p (q w)"),
                            r[bass.ds(i, 1)].rearrange("a p c -> p (a c)")).then_inc(s_rec[m.u], 16)

            def sync(e):
                for dst_ap, name in ((fc1, "fc_w1"), (fc2, "fc_w2"), (fc3, "fc_w3")):
                    e.dma_start(dst_ap, io[f"L1_gnn_{name}"]).then_inc(S("e1_fc"), 16)
                macro_loops(3, sync_a, lambda e, M: sync_a(e, M(3)))(e)

            def pool_a(e, m):
                e.wait_ge(s_rec[m.u], m.turns(16))
                e.sem_inc(S("s_gp"), 1)
                e.wait_ge(s["msg"], m.done(U))
                e.sem_inc(S("s_gp"), 1)
                for q in range(Q):
                    e.indirect_dma_start(
                        out=rows_y[m.u][:, q, :], out_offset=None, in_=y1,
                        in_offset=bass.IndirectOffsetOnAxis(ap=r_sb[:, m.u, q, 0:1].bitcast(I32), axis=0),
                    ).then_inc(s_gat[m.u], 16)

            def transposes(e, m):
                e.wait_ge(s_rec[m.u], m.turns(16))
                e.wait_ge(s["g2"], m.done(1))
                for q in range(Q):
                    last = T.transpose(ps[0:8, 0, q * P:(q + 1) * P], r_sb[:, m.u, q, 6:14], ident[:, :])
                last.then_inc(s["tr"], 1)

            def layer_1(e, m):
                e.wait_ge(s["at"], m.done())
                e.wait_ge(s["g1"], m.done(1))
                T.matmul(ps[0:64, 1, :], fc1, at, start=True, stop=True).then_inc(s["h1"], 1)

            def layer_2(e, m):
                e.wait_ge(s["g1"], m.done())
                e.wait_ge(s["g2"], m.done(1))
                e.sem_inc(S("s_pe"), 1)
                T.matmul(ps[0:64, 0, :], fc2, h1, start=True, stop=True).then_inc(s["h2"], 1)

            def layer_3(e, m):
                e.wait_ge(s["g2"], m.done())
                e.wait_ge(s["wr"], m.done(1))
                for q in range(Q):
                    last = T.matmul(psW[:, q].rearrange("p k n -> p (k n)"), h2[:, q * P:(q + 1) * P], fc3,
                                    start=True, stop=True)
                last.then_inc(s["w"], 1)

            def sums(e, m, q):
                if q == 0:
                    e.wait_ge(s["oh"], m.done())
                    e.wait_ge(s["msg"], m.done())
                    e.wait_ge(s["flush"], m.done(2))
                T.matmul(psDeg[m.v], top(oh[:, m.u, q, :]), top(ones[:, 0:1]), start=(q == 0), stop=(q == Q - 1))
                ins = T.matmul(ps[:, 5 + m.v, :], oh[:, m.u, q, :],
                               msg[m.v][:, q].rearrange("p c h n -> p (c h n)"),
                               start=(q == 0), stop=(q == Q - 1))
                if q == Q - 1:
                    ins.then_inc(s["sum"], 1)

            def tensor(e):
                e.wait_ge(S("e1_fc"), 48)
                e.wait_ge(S("e1_go"), 1)
                for m in range(2):
                    for part in (transposes, layer_1, layer_2, layer_3):
                        part(e, Macro(0, m))

                def turn(e, M):
                    transposes(e, M(2))
                    sums(e, M(0), 0)
                    layer_1(e, M(2))
                    sums(e, M(0), 1)
                    layer_2(e, M(2))
                    sums(e, M(0), 2)
                    sums(e, M(0), 3)
                    layer_3(e, M(2))
                macro_loops(0, None, turn)(e)

            def act(e, m):
                e.wait_ge(s["tr"], m.done())
                e.wait_ge(s["h1"], m.done(1))
                A.activation(at, ps[0:8, 0, :], ACT.Copy).then_inc(s["at"], 1)
                e.wait_ge(s["h1"], m.done())
                e.wait_ge(s["h2"], m.done(1))
                A.activation(h1, ps[0:64, 1, :], ACT.Silu, scale=8.0 ** -0.5).then_inc(s["g1"], 1)
                e.wait_ge(s["h2"], m.done())
                e.wait_ge(s["w"], m.done(1))
                A.activation(h2, ps[0:64, 0, :], ACT.Silu, scale=MUL ** -0.5).then_inc(s["g2"], 1)
                e.wait_ge(s["w"], m.done())
                e.wait_ge(s["wr"], m.done(1))
                for q in range(Q):
                    last = A.activation(wac[:, q], psW[:, q, 0:3:2, :], ACT.Copy, scale=r_sb[:, m.u, q, 2:3])
                last.then_inc(s["wac"], 1)

            def one_hot(e, m, q):
                if q == 0:
                    e.wait_ge(s_rec[m.u], m.turns(16))
                    e.wait_ge(s["sum"], m.done(U))
                ins = V.tensor_scalar(oh[:, m.u, q, :], iota[:, :], r_sb[:, m.u, q, 1:2], None, ALU.is_equal)
                if q == Q - 1:
                    ins.then_inc(s["oh"], 1)

            def messages(c, e, m, nxt):
                y = rows_y[m.u]
                yv = y[:, :, MUL:4 * MUL].rearrange("p q (d n) -> p q d n", d=3)
                shd = r_sb[:, m.u, :, 3:6]
                shb = bcast(shd, 3, [P, Q, 3, MUL])
                o = msg[m.v]
                e.wait_ge(s_gat[m.u], m.turns(64))
                k = c(V.tensor_tensor(g3, yv, shb, ALU.mult))
                one_hot(e, nxt, 0)
                one_hot(e, nxt, 1)
                c.wait(k)
                k = c(V.tensor_tensor(dot, g3[:, :, 0, :], g3[:, :, 1, :], ALU.add))
                one_hot(e, nxt, 2)
                c.wait(k)
                k_dot = c(V.tensor_tensor(dot, dot, g3[:, :, 2, :], ALU.add))
                one_hot(e, nxt, 3)
                e.wait_ge(s["sum"], m.done(2))
                e.wait_ge(s["wac"], m.done())
                k_wb = c(V.tensor_tensor(wb, psW[:, :, 1, :], y[:, :, 0:MUL], ALU.mult))
                c.wait(k_dot)
                V.tensor_tensor(o[:, :, 0, 1, :], psW[:, :, 3, :], dot, ALU.mult)
                V.tensor_tensor(o[:, :, 0, 0, :], wac[:, :, 0, :], y[:, :, 0:MUL], ALU.mult)
                V.tensor_tensor(o[:, :, 1:4, 1, :], bcast(wac[:, :, 1, :], 2, [P, Q, 3, MUL]), yv, ALU.mult)\
                    .then_inc(s["wr"], 1)
                c.wait(k_wb)
                V.tensor_tensor(o[:, :, 1:4, 0, :], bcast(wb, 2, [P, Q, 3, MUL]), shb, ALU.mult)\
                    .then_inc(s["msg"], 1)

            def add_sums(c, e, m):
                j = e.value_load(jmap["s"][0:1, bass.ds(m.index(), 1)], min_val=0, max_val=NB - 1)
                e.wait_ge(s["flush"], m.done(1))
                e.wait_ge(s["sum"], m.done())
                dj, aj = deg[:, bass.ds(j, 1)], acc[:, bass.ds(j, 1), :]
                V.tensor_tensor(dj, dj, psDeg[m.v], ALU.add)
                V.tensor_tensor(aj, aj, ps[:, 5 + m.v, :], ALU.add).then_inc(s["flush"], 1)

            def dve(e):
                c = vchain(e)
                c(V.memset(acc, 0.0))
                c(V.memset(deg[:, :], 0.0))
                c.wait()
                e.sem_inc(S("e1_go"), 1)
                for m in range(2):
                    for q in range(Q):
                        one_hot(e, Macro(0, m), q)
                cc = Chain(e, cB)
                messages(cc, e, Macro(0, 0), Macro(0, 2))
                per = cc.n

                def turn(e, M):
                    c = Chain(e, cB)
                    c.n = per * M(1).off
                    c.enter(M(1).i, U * per)
                    messages(c, e, M(1), M(3))
                    assert c.n - c.at == per
                    add_sums(c, e, M(0))
                macro_loops(0, None, turn)(e)

            phase(sync=sync, gpsimd=macro_loops(3, pool_a, lambda e, M: pool_a(e, M(3))),
                  scalar=macro_loops(2, act, lambda e, M: act(e, M(2))), tensor=tensor, vector=dve)

            w2 = wts[:, 0:P].rearrange("p (k n) -> p k n", k=2)
            s_act = (sem("o1_go"), sem("o1_root"))

            def scale(e):
                c = vchain(e)
                c(V.tensor_scalar(deg[:, :], deg[:, :], 1.0, None, ALU.max))
                c.wait()
                e.sem_inc(s_act[0], 1)
                e.wait_ge(s_act[1], 1)
                c(V.reciprocal(small[:, 0:NB], deg[:, :]))
                c.wait()
                c(V.tensor_tensor(acc, acc, bcast(small[:, 0:NB], 2, [P, NB, 2 * D]), ALU.mult))
                c.wait()

            def root(e):
                e.wait_ge(s_act[0], 1)
                A.activation(deg[:, :], deg[:, :], ACT.Sqrt).then_inc(s_act[1], 1)

            phase(vector=scale, scalar=root)

            out_scale = (2 * MUL) ** -0.5 * MUL ** -0.5

            def w_adjust(e, c):
                c(V.tensor_scalar(w2[MUL:P, 0, :], w2[MUL:P, 0, :], INV_SQRT3, None, ALU.mult))

            def evac2(e, m, pp, st):
                t = qz[:, bass.ds(m.index(), 1), :]
                return V.scalar_tensor_tensor(t, pp[:, 0, 0:D], out_scale, t, ALU.mult, ALU.add)

            project("o1", 4, acc, [(w2[:, 0, :], io["L1_gnn_w2_s"]), (w2[:, 1, :], io["L1_gnn_w2_v"]),
                                   (rows[:, 0:MUL], row_bcast(io["L1_gnn_g_s"])),
                                   (rows[:, MUL:2 * MUL], row_bcast(io["L1_gnn_g_v"]))],
                    [(0, c * MUL, (c + 1) * MUL, [(c, w2[:, min(c, 1), :])]) for c in range(4)], evac2,
                    prep_ws=w_adjust)

            def rms(e, c, s_act):
                sq = junk
                st_, tmp_ = small[:, 128:128 + 2 * NB], small[:, 192:192 + 2 * NB]
                c(V.tensor_tensor(sq, qz[:, :, :], qz[:, :, :], ALU.mult))
                c.wait()
                c(V.tensor_reduce(st_[:, 0:NB], sq[:, :, 0:MUL], AX.X, ALU.add))
                c(V.tensor_reduce(st_[:, NB:2 * NB], sq[:, :, MUL:D], AX.X, ALU.add))
                c.wait()
                c(V.tensor_scalar(st_[:, NB:2 * NB], st_[:, NB:2 * NB], 1.0 / 3.0, None, ALU.mult))
                c.wait()
                rstd(e, c, s_act, 1, st_, 1.0 / MUL, tmp_)
                zs = qz[:, :, 0:MUL]
                zv = qz[:, :, MUL:D]
                c(V.tensor_tensor(zs, zs, bcast(st_[:, 0:NB], 2, [P, NB, MUL]), ALU.mult))
                c(V.tensor_tensor(zv, zv, bcast(st_[:, NB:2 * NB], 2, [P, NB, 3 * MUL]), ALU.mult))
                c.wait()
                c(V.tensor_tensor(zs, zs, bcast(rows[:, 0:MUL], 1, [P, NB, MUL]), ALU.mult))
                for d in range(3):
                    zd = qz[:, :, (d + 1) * MUL:(d + 2) * MUL]
                    c(V.tensor_tensor(zd, zd, bcast(rows[:, MUL:2 * MUL], 1, [P, NB, MUL]), ALU.mult))
                c.wait()
                xs_ = x_sb[:, :, 0:MUL]
                c(V.tensor_tensor(xs_, xs_, zs, ALU.add))
                for d in range(3):
                    xd = x_sb[:, :, MUL + d::3]
                    c(V.tensor_tensor(xd, xd, qz[:, :, (d + 1) * MUL:(d + 2) * MUL], ALU.add))
                c.wait()
                return 1

            v1_, a1_ = layernorm("l1", before=rms, roots=[small[:, 192:192 + 2 * NB]])
            phase(vector=v1_, scalar=a1_)

        layer1()

        def softmax_by_node(e, c):
            den = acc4[:, :, :, DH]
            c(V.tensor_scalar(den, den, 1e-30, None, ALU.max))
            c.wait()
            c(V.reciprocal(big[:, 0:NB * H].rearrange("p (j h) -> p j h", h=H), den))
            c.wait()
            rden = big[:, 0:NB * H].rearrange("p (j h) -> p j h", h=H)
            for h in range(H):
                c(V.tensor_tensor(qz4[:, :, h, :], acc4[:, :, h, 0:DH], bcast(rden[:, :, h], 2, [P, NB, DH]),
                                  ALU.mult))
            c.wait()

        def layer2():
            qkv("p2", 2, kv2)
            attention(2, "s", kv2)
            out_proj("o2", 2, prepare=softmax_by_node)
            v, a = layernorm("l2")
            phase(vector=v, scalar=a)

        def layer3():
            s = stages("e3", "oh", "pv", "sum", "flush")
            s_rec = [sem(f"e3_rec{u}") for u in range(U)]
            s_gat = [sem(f"e3_gat{u}") for u in range(U)]
            r_sb = rec["d"]
            acc = acc_raw[:, :, 0:D]
            r = recs["d"].rearrange("(m p q) w -> m p (q w)", p=P, q=Q)

            def sync_a(e, m):
                i = e.snap(m.index())
                e.wait_ge(s["sum"], m.done(U))
                e.sem_inc(S("s_sp"), 1)
                e.dma_start(r_sb[:, m.u, :, :].rearrange("p q w -> p (q w)"),
                            r[bass.ds(i, 1)].rearrange("a p c -> p (a c)")).then_inc(s_rec[m.u], 16)

            def sync(e):
                e.dma_start(x3.rearrange("(j p) c -> p j c", p=P), x_sb[:, :, :]).then_inc(S("e3_x"), 16)
                e.wait_ge(S("e3_x"), 16)
                macro_loops(3, sync_a, lambda e, M: sync_a(e, M(3)))(e)

            def pool_a(e, m):
                e.wait_ge(s_rec[m.u], m.turns(16))
                e.sem_inc(S("s_gp"), 1)
                e.wait_ge(s["sum"], m.done(U))
                e.sem_inc(S("s_gp"), 1)
                for q in range(Q):
                    e.indirect_dma_start(
                        out=gat[:, m.u, q, 0:D], out_offset=None, in_=x3,
                        in_offset=bass.IndirectOffsetOnAxis(ap=r_sb[:, m.u, q, 0:1].bitcast(I32), axis=0),
                    ).then_inc(s_gat[m.u], 16)

            def pool(e):
                e.wait_ge(S("e3_x"), 16)
                macro_loops(3, pool_a, lambda e, M: pool_a(e, M(3)))(e)

            def pe(e, m):
                e.wait_ge(s["oh"], m.done())
                e.wait_ge(s_gat[m.u], m.turns(64))
                e.wait_ge(s["flush"], m.done(2))
                for q in range(Q):
                    last = T.matmul(ps[:, 5 + m.v, 0:D], oh[:, m.u, q, :], gat[:, m.u, q, 0:D],
                                    start=(q == 0), stop=(q == Q - 1))
                last.then_inc(s["sum"], 1)

            def tensor(e):
                macro_loops(0, None, lambda e, M: pe(e, M(0)))(e)

            def dve_a(e, m):
                e.wait_ge(s_rec[m.u], m.turns(16))
                e.wait_ge(s["sum"], m.done(U))
                for q in range(Q):
                    last = V.tensor_scalar(oh[:, m.u, q, :], iota[:, :], r_sb[:, m.u, q, 1:2],
                                           r_sb[:, m.u, q, 2:3], ALU.is_equal, ALU.mult)
                last.then_inc(s["oh"], 1)

            def dve_b(e, m):
                j = e.value_load(jmap["d"][0:1, bass.ds(m.index(), 1)], min_val=0, max_val=NB - 1)
                e.wait_ge(s["flush"], m.done(1))
                e.wait_ge(s["sum"], m.done())
                aj = acc[:, bass.ds(j, 1), :]
                V.tensor_tensor(aj, aj, ps[:, 5 + m.v, 0:D], ALU.add).then_inc(s["flush"], 1)

            def dve(e):
                V.memset(acc, 0.0).then_inc(S("e3_z"), 1)
                e.wait_ge(S("e3_z"), 1)
                macro_loops(3, dve_a, lambda e, M: (dve_a(e, M(3)), dve_b(e, M(0))))(e)

            phase(sync=sync, gpsimd=pool, tensor=tensor, vector=dve)

            wide = acc_raw[:, :, 0:2 * D]
            w4 = wts[:, 0:4 * D].rearrange("p (c n) -> p c n", c=4)

            def inputs_(e, c):
                nb = wide[:, :, 0:D]
                c(V.tensor_tensor(qz[:, :, :], nb, x_sb[:, :, :], ALU.mult))
                c(V.tensor_copy(wide[:, :, D:2 * D], x_sb[:, :, :]))
                c.wait()
                c(V.tensor_tensor(nb, nb, qz[:, :, :], ALU.add))
                c.wait()

            def bias(e, c):
                c(V.tensor_tensor(rows[:, 0:D], rows[:, 0:D], rows[:, D:2 * D], ALU.add))

            def evac(e, m, pp, st):
                return V.tensor_tensor(qz[:, bass.ds(m.index(), 1), :], pp[:, 0, 0:D], rows[:, 0:D], ALU.add)

            project("o3", 4, wide, [(w4[:, 0:2, :], halves(io["L3_gnn_W2"])), (w4[:, 2:4, :], halves(io["L3_gnn_W1"])),
                                    (rows[:, 0:D], row_bcast(io["L3_gnn_b1"])),
                                    (rows[:, D:2 * D], row_bcast(io["L3_gnn_b2"]))],
                    [(0, 0, D, [(c, w4[:, c, :]) for c in range(4)])], evac, prepare=inputs_, prep_ws=bias)

            def normalize(e, c, s_act):
                z = qz[:, :, :]
                n2 = small[:, 128:128 + NB]
                c(V.scalar_tensor_tensor(z, z, 0.2, z, ALU.mult, ALU.max))
                c.wait()
                c(V.tensor_tensor(junk, z, z, ALU.mult))
                c.wait()
                c(V.tensor_reduce(n2, junk, AX.X, ALU.add))
                c.wait()
                e.sem_inc(s_act[0], 1)
                e.wait_ge(s_act[1], 1)
                c(V.tensor_scalar(n2, n2, 1e-12, None, ALU.max))
                c.wait()
                c(V.reciprocal(n2, n2))
                c.wait()
                c(V.tensor_tensor(z, z, bcast(n2, 2, [P, NB, D]), ALU.mult))
                c.wait()
                c(V.tensor_tensor(x_sb[:, :, :], x_sb[:, :, :], z, ALU.add))
                c.wait()
                return 1

            v, a = layernorm("l3", before=normalize, roots=[small[:, 128:128 + NB]])
            phase(vector=v, scalar=a)

            def store(e):
                e.dma_start(out[0:(NT - 1) * P, :].rearrange("(j p) d -> p j d", p=P), x_sb[:, 0:NT - 1, :])\
                    .then_inc(S("s_out"), 16)
                e.dma_start(out[(NT - 1) * P:N_NODES, :], x_sb[0:LAST, NT - 1, :]).then_inc(S("s_out"), 16)
                e.wait_ge(S("s_out"), 32)

            phase(sync=store)

        layer2()
        layer3()

        block = ctx.enter_context(nc.Block())

        def run(e, todo):
            for fn, meet in todo:
                if fn:
                    fn(e)
                e.drain().then_inc(s_bar, 1)
                e.wait_ge(s_bar, meet)

        @block.sync
        def _(e):
            for counter, start in credits:
                e.sem_inc(counter, start)
            run(e, programs["sync"])

        @block.gpsimd
        def _(e):
            run(e, programs["gpsimd"])

        @block.scalar
        def _(e):
            run(e, programs["scalar"])

        @block.vector
        def _(e):
            run(e, programs["vector"])

        @block.tensor
        def _(e):
            run(e, programs["tensor"])


def layout(inputs):
    def pad(a, fill):
        a = np.asarray(a)
        out = np.full((E_PAD,) + a.shape[1:], fill, a.dtype)
        out[:N_EDGES] = a
        return out.reshape((P, EC) + a.shape[1:])

    src, dst = inputs["src"], inputs["dst"]
    more = EC // (NM // U)
    ins = {
        "x": inputs["x"],
        "dst_key": pad(dst, PAD_KEY), "src_idx": pad(src, 0),
        "src_key": pad(src, PAD_KEY), "dst_idx": pad(dst, 0),
        "edge_weight": pad(inputs["edge_weight"], 0),
        "edge_attr_4": np.pad(pad(inputs["edge_attr_4"], 0), ((0, 0), (0, more), (0, 0))),
        "edge_attr_8": np.pad(pad(inputs["edge_attr_8"], 0), ((0, 0), (0, more), (0, 0))),
        "node_vec": np.pad(np.asarray(inputs["node_vec"]), (0, NB * P - N_NODES)).reshape(NB, P).T,
    }
    for name, a in inputs.items():
        if name[:2] in ("L0", "L1", "L2", "L3"):
            ins[name] = np.asarray(a)
    for name in ("L3_gnn_W1", "L3_gnn_W2"):
        ins[name] = np.ascontiguousarray(ins[name].T)
    return {k: np.ascontiguousarray(a) for k, a in ins.items()}


def kernel(**inputs):
    import concourse.bacc as bacc
    from concourse.bass_utils import run_bass_kernel_spmd

    nc = bacc.Bacc("TRN2", target_bir_lowering=False, num_devices=1)
    arrays = {f"in_{name}": a for name, a in layout(inputs).items()}
    io = {name[3:]: nc.dram_tensor(name, a.shape, mybir.dt.from_np(a.dtype), kind="ExternalInput").ap()
          for name, a in arrays.items()}
    out = nc.dram_tensor("out", (N_NODES, D), F32, kind="ExternalOutput").ap()
    gnn_kernel(nc, io, out)
    return run_bass_kernel_spmd(nc, [arrays], core_ids=[0]).results[0]["out"]
```
